# Optimizing a Trainium2 kernel written in Bass

```python
import numpy as np
import jax
import jax.numpy as jnp

def _softmax(x, axis=-1):
    return jax.nn.softmax(x, axis=axis)

def _gelu(x):
    return jax.nn.gelu(x, approximate=True)

def _silu(x):
    return jax.nn.silu(x)

def _sigmoid(x):
    return jax.nn.sigmoid(x)

def _layernorm(x, axis=-1, eps=1e-05):
    m = jnp.mean(x, axis=axis, keepdims=True)
    v = jnp.var(x, axis=axis, keepdims=True)
    return (x - m) / jnp.sqrt(v + eps)

def _scatter_add(tgt, idx, src, axis=0):
    return tgt.at[idx].add(src)

def _segment_sum(src, seg, n):
    return jax.ops.segment_sum(src, seg, n)
kernel_name = 'mk_decoder_postln_d4_seqx_r8_32d529'

def setup_inputs(seed: int=0):
    np.random.seed(seed)
    _w = jnp.asarray

    def _rec_inputs():
        import jax
        import jax.numpy as jnp
        _rk = jax.random.key(seed)
        x = -0.0002928 + 1 * jax.random.normal(jax.random.fold_in(_rk, 1), (4, 256, 128), jnp.float32)
        _lenS = 256 - jax.random.randint(jax.random.fold_in(_rk, 7), (4,), 0, max(1, 256 // 4) + 1, jnp.int32)
        _lenS2 = 256 - jax.random.randint(jax.random.fold_in(_rk, 8), (4,), 0, max(1, 256 // 4) + 1, jnp.int32)
        _ctx_1024P = jax.random.normal(jax.random.fold_in(_rk, 11), (4, 16, 128), jnp.float32)
        _ctx_1024c = jax.random.dirichlet(jax.random.fold_in(_rk, 511), 0.3 * jnp.ones((16,), jnp.float32), (4, 256))
        _ctx_1024t = jnp.einsum('bsk,bkd->bsd', _ctx_1024c, _ctx_1024P)
        _ctx_1024t = _ctx_1024t * jax.lax.rsqrt(jnp.mean(jnp.square(_ctx_1024t)) + 1e-12) * 0.953939
        ctx_1024 = -1.39393e-06 + 0.999914 * (_ctx_1024t + 0.3 * jax.random.normal(jax.random.fold_in(_rk, 611), (4, 256, 128), jnp.float32))
        _validS = jnp.arange(256)[None, :] < _lenS[:, None]
        _validS2 = jnp.arange(256)[None, :] < _lenS2[:, None]
        _causal = jnp.tril(jnp.ones((256, 256), dtype=bool))
        mask_Bx1xSxS2_ik1 = jnp.where(jnp.broadcast_to(_validS2[:, None, None, :], (4, 1, 256, 256)), 1, 0).astype(jnp.int32)
        return (x, ctx_1024, mask_Bx1xSxS2_ik1)
    x, ctx_1024, mask_Bx1xSxS2_ik1 = _rec_inputs()

    def _L0_attn_setup():
        import jax, jax.numpy as jnp
        import numpy as np
        B_SZ, T, D_MODEL, D_STATE, DT_RANK = (4, 256, 128, 16, 64)
        key = jax.random.key(seed)
        ks = jax.random.split(key, 12)
        s = 0.02
        return {'u': jax.random.normal(ks[0], (B_SZ, T, D_MODEL), dtype=jnp.float32), 'A_log': s * jax.random.normal(ks[1], (D_MODEL, D_STATE), dtype=jnp.float32), 'W_xdt': s * jax.random.normal(ks[2], (DT_RANK, D_MODEL), dtype=jnp.float32), 'b_xdt': s * jax.random.normal(ks[3], (DT_RANK,), dtype=jnp.float32), 'W_dt': s * jax.random.normal(ks[4], (D_MODEL, DT_RANK), dtype=jnp.float32), 'b_dt': jax.random.uniform(ks[5], (D_MODEL,), dtype=jnp.float32, minval=-4.0, maxval=-1.0), 'W_B': s * jax.random.normal(ks[6], (D_STATE, D_MODEL), dtype=jnp.float32), 'b_B': s * jax.random.normal(ks[7], (D_STATE,), dtype=jnp.float32), 'W_C': s * jax.random.normal(ks[8], (D_STATE, D_MODEL), dtype=jnp.float32), 'b_C': s * jax.random.normal(ks[9], (D_STATE,), dtype=jnp.float32), 'D': jnp.ones((D_MODEL,), dtype=jnp.float32)}
    _L0_attn_all = _L0_attn_setup()
    _L0_attn_in = {k: v for k, v in _L0_attn_all.items() if k in ('A_log', 'W_xdt', 'b_xdt', 'W_dt', 'b_dt', 'W_B', 'b_B', 'W_C', 'b_C', 'D')}
    del _L0_attn_all

    def _L0_xattn_setup():
        import jax, jax.numpy as jnp
        import numpy as np
        D_MODEL = 128
        NUM_HEADS = 16
        HEAD_DIM = D_MODEL // NUM_HEADS

        def _split_heads(x):
            B, S, _ = x.shape
            return x.reshape(B, S, NUM_HEADS, HEAD_DIM).transpose(0, 2, 1, 3)
        key = jax.random.key(seed)
        ks = jax.random.split(key, 11)
        B, S = (2, 256)
        s = 1.0 / np.sqrt(D_MODEL)
        return {'q': jax.random.normal(ks[0], (B, S, D_MODEL), jnp.float32), 'k': jax.random.normal(ks[1], (B, S, D_MODEL), jnp.float32), 'v': jax.random.normal(ks[2], (B, S, D_MODEL), jnp.float32), 'Wq': jax.random.normal(ks[3], (D_MODEL, D_MODEL), jnp.float32) * s, 'bq': jnp.zeros((D_MODEL,), jnp.float32), 'Wk': jax.random.normal(ks[4], (D_MODEL, D_MODEL), jnp.float32) * s, 'bk': jnp.zeros((D_MODEL,), jnp.float32), 'Wv': jax.random.normal(ks[5], (D_MODEL, D_MODEL), jnp.float32) * s, 'bv': jnp.zeros((D_MODEL,), jnp.float32), 'Wo': jax.random.normal(ks[6], (D_MODEL, D_MODEL), jnp.float32) * s, 'bo': jnp.zeros((D_MODEL,), jnp.float32)}
    _L0_xattn_all = _L0_xattn_setup()
    _L0_xattn_in = {k: v for k, v in _L0_xattn_all.items() if k in ('Wq', 'bq', 'Wk', 'bk', 'Wv', 'bv', 'Wo', 'bo')}
    del _L0_xattn_all

    def _L0_ffn_setup():
        import jax, jax.numpy as jnp
        import numpy as np
        D_MODEL = 128
        N_HEADS = 16
        N_KV = 4
        NUM_REP = N_HEADS // N_KV
        HEAD_DIM = D_MODEL // N_HEADS
        N_EXPERTS = 8
        TOP_K = 2
        CAP_FACTOR = 1.25
        EPS_NORM = 1e-06

        def _rmsnorm(x, w):
            var = jnp.mean(x * x, axis=-1, keepdims=True)
            return w * (x * jax.lax.rsqrt(var + EPS_NORM))

        def _gqa(x, qw, qb, kw, kb, vw, vb, ow, ob):
            B, S, D = x.shape
            q = (x @ qw + qb).reshape(B, S, N_HEADS, HEAD_DIM).transpose(0, 2, 1, 3)
            k = (x @ kw + kb).reshape(B, S, N_KV, HEAD_DIM).transpose(0, 2, 1, 3)
            v = (x @ vw + vb).reshape(B, S, N_KV, HEAD_DIM).transpose(0, 2, 1, 3)
            k = jnp.repeat(k, NUM_REP, axis=1)
            v = jnp.repeat(v, NUM_REP, axis=1)
            scores = jnp.einsum('bhqd,bhkd->bhqk', q, k) / np.sqrt(HEAD_DIM).astype(np.float32)
            attn = jax.nn.softmax(scores, axis=-1)
            out = jnp.einsum('bhqk,bhkd->bhqd', attn, v)
            out = out.transpose(0, 2, 1, 3).reshape(B, S, D)
            return out @ ow + ob

        def _moe(x, gate_w, w1, w2):
            B, S, D = x.shape
            T = B * S
            x_flat = x.reshape(T, D)
            capacity = int(CAP_FACTOR * T * TOP_K / N_EXPERTS)
            logits = x_flat @ gate_w
            probs = jax.nn.sigmoid(logits)
            _, sel = jax.lax.top_k(probs, TOP_K)
            w_topk = jnp.take_along_axis(probs, sel, axis=1)
            w_topk = w_topk / (jnp.sum(w_topk, axis=-1, keepdims=True) + 1e-06)
            flat_sel = sel.reshape(-1)
            em = jax.nn.one_hot(flat_sel, N_EXPERTS, dtype=jnp.int32)
            ranks = jnp.take_along_axis(jnp.cumsum(em, axis=0), flat_sel[:, None], axis=1)[:, 0] - 1
            valid = ranks < capacity
            slot = flat_sel * capacity + ranks
            scatter_idx = jnp.where(valid, slot, N_EXPERTS * capacity)
            x_rep = jnp.repeat(x_flat, TOP_K, axis=0)
            padded = jnp.zeros((N_EXPERTS * capacity + 1, D), x.dtype).at[scatter_idx].set(x_rep)
            padded_x = padded[:N_EXPERTS * capacity].reshape(N_EXPERTS, capacity, D)
            h = jax.nn.gelu(jnp.einsum('ecd,edf->ecf', padded_x, w1), approximate=False)
            out_padded = jnp.einsum('ecf,efd->ecd', h, w2).reshape(N_EXPERTS * capacity, D)
            gather_idx = jnp.where(valid, slot, 0)
            out_rep = jnp.where(valid[:, None], out_padded[gather_idx], 0.0)
            out_w = out_rep * w_topk.reshape(-1)[:, None]
            return out_w.reshape(T, TOP_K, D).sum(axis=1).reshape(B, S, D)
        key = jax.random.key(seed)
        ks = jax.random.split(key, 12)
        s = 0.02
        return {'x': jax.random.normal(ks[0], (4, 128, D_MODEL), jnp.float32), 'qw': jax.random.normal(ks[1], (D_MODEL, D_MODEL), jnp.float32) * s, 'qb': jnp.zeros((D_MODEL,), jnp.float32), 'kw': jax.random.normal(ks[2], (D_MODEL, N_KV * HEAD_DIM), jnp.float32) * s, 'kb': jnp.zeros((N_KV * HEAD_DIM,), jnp.float32), 'vw': jax.random.normal(ks[3], (D_MODEL, N_KV * HEAD_DIM), jnp.float32) * s, 'vb': jnp.zeros((N_KV * HEAD_DIM,), jnp.float32), 'ow': jax.random.normal(ks[4], (D_MODEL, D_MODEL), jnp.float32) * s, 'ob': jnp.zeros((D_MODEL,), jnp.float32), 'gate_w': jax.random.normal(ks[5], (D_MODEL, N_EXPERTS), jnp.float32) * s, 'w1': jax.random.normal(ks[6], (N_EXPERTS, D_MODEL, 256), jnp.float32) * s, 'w2': jax.random.normal(ks[7], (N_EXPERTS, 256, D_MODEL), jnp.float32) * s, 'norm1_w': jnp.ones((D_MODEL,), jnp.float32), 'norm2_w': jnp.ones((D_MODEL,), jnp.float32)}
    _L0_ffn_all = _L0_ffn_setup()
    _L0_ffn_in = {k: v for k, v in _L0_ffn_all.items() if k in ('qw', 'qb', 'kw', 'kb', 'vw', 'vb', 'ow', 'ob', 'gate_w', 'w1', 'w2', 'norm1_w', 'norm2_w')}
    del _L0_ffn_all

    def _L1_attn_setup():
        import math
        import jax, jax.numpy as jnp
        import numpy as np
        NUM_HEADS = 16
        EMBED = 128
        B, T = (2, 256)
        key = jax.random.key(seed)
        k1, k2 = jax.random.split(key)
        x = jax.random.normal(k1, (B, T, EMBED), dtype=jnp.float32)
        bound = 1.0 / math.sqrt(NUM_HEADS * EMBED)
        weight = jax.random.uniform(k2, (NUM_HEADS * EMBED, EMBED), dtype=jnp.float32, minval=-bound, maxval=bound)
        return {'x': x, 'weight': weight}
    _L1_attn_all = _L1_attn_setup()
    _L1_attn_in = {k: v for k, v in _L1_attn_all.items() if k in ('weight',)}
    del _L1_attn_all

    def _L1_xattn_setup():
        import jax, jax.numpy as jnp
        import numpy as np
        D_MODEL = 128
        N_HEADS = 16
        HEAD_DIM = D_MODEL // N_HEADS
        key = jax.random.key(seed)
        k1, k2, k3, k4, k5, k6 = jax.random.split(key, 6)
        B, T_q, T_kv = (4, 128, 512)
        s = 1.0 / np.sqrt(D_MODEL)
        return {'query': jax.random.normal(k1, (B, T_q, D_MODEL), dtype=jnp.float32), 'kv_source': jax.random.normal(k2, (B, T_kv, D_MODEL), dtype=jnp.float32), 'w_q': jax.random.normal(k3, (D_MODEL, D_MODEL), dtype=jnp.float32) * s, 'w_k': jax.random.normal(k4, (D_MODEL, D_MODEL), dtype=jnp.float32) * s, 'w_v': jax.random.normal(k5, (D_MODEL, D_MODEL), dtype=jnp.float32) * s, 'w_o': jax.random.normal(k6, (D_MODEL, D_MODEL), dtype=jnp.float32) * s}
    _L1_xattn_all = _L1_xattn_setup()
    _L1_xattn_in = {k: v for k, v in _L1_xattn_all.items() if k in ('w_q', 'w_k', 'w_v', 'w_o')}
    del _L1_xattn_all

    def _L1_ffn_setup():
        import jax, jax.numpy as jnp
        import numpy as np
        B, S, D, H, E, K = (4, 256, 128, 256, 8, 2)
        TEMP = 5.0
        EPS = 1e-09
        key = jax.random.key(seed)
        k_x, k_wg, k_w1, k_w2 = jax.random.split(key, 4)
        scale = 0.02
        return {'x': jax.random.normal(k_x, (B, S, D), dtype=jnp.float32), 'Wg': jax.random.normal(k_wg, (D, E), dtype=jnp.float32) * scale, 'bg': jnp.zeros((E,), dtype=jnp.float32), 'W1': jax.random.normal(k_w1, (E, D, H), dtype=jnp.float32) * scale, 'b1': jnp.zeros((E, H), dtype=jnp.float32), 'W2': jax.random.normal(k_w2, (E, H, D), dtype=jnp.float32) * scale, 'b2': jnp.zeros((E, D), dtype=jnp.float32)}
    _L1_ffn_all = _L1_ffn_setup()
    _L1_ffn_in = {k: v for k, v in _L1_ffn_all.items() if k in ('Wg', 'bg', 'W1', 'b1', 'W2', 'b2')}
    del _L1_ffn_all

    def _L2_attn_setup():
        import jax, jax.numpy as jnp
        import numpy as np
        EMBED_DIM = 128
        NUM_HEADS = 16
        HEAD_DIM = EMBED_DIM // NUM_HEADS
        SCALE = 1.0 / float(np.sqrt(HEAD_DIM))
        key = jax.random.key(seed)
        ks = jax.random.split(key, 5)
        B, S, E = (2, 256, EMBED_DIM)
        x = jax.random.normal(ks[0], (B, S, E), dtype=jnp.float32)
        w_qkv = jax.random.normal(ks[1], (E, 3 * E), dtype=jnp.float32) / np.sqrt(E)
        b_qkv = jax.random.normal(ks[2], (3 * E,), dtype=jnp.float32) * 0.02
        w_out = jax.random.normal(ks[3], (E, E), dtype=jnp.float32) / np.sqrt(E)
        b_out = jax.random.normal(ks[4], (E,), dtype=jnp.float32) * 0.02
        return {'x': x, 'w_qkv': w_qkv, 'b_qkv': b_qkv, 'w_out': w_out, 'b_out': b_out}
    _L2_attn_all = _L2_attn_setup()
    _L2_attn_in = {k: v for k, v in _L2_attn_all.items() if k in ('w_qkv', 'b_qkv', 'w_out', 'b_out')}
    del _L2_attn_all

    def _L2_xattn_setup():
        import jax, jax.numpy as jnp
        import numpy as np
        B, S, E, H = (2, 256, 128, 16)
        D = E // H
        key = jax.random.key(seed)
        ks = jax.random.split(key, 14)
        inp = {'query': jax.random.normal(ks[0], (B, S, E), jnp.float32), 'key': jax.random.normal(ks[1], (B, S, E), jnp.float32), 'value': jax.random.normal(ks[2], (B, S, E), jnp.float32), 'adj': jax.random.normal(ks[3], (S, S), jnp.float32), 'mask': jax.random.randint(ks[4], (B, 1, S, S), 0, 2, jnp.int32)}
        sc = 1.0 / np.sqrt(E)
        inp['Wq'] = jax.random.normal(ks[5], (E, E), jnp.float32) * sc
        inp['bq'] = jax.random.normal(ks[6], (E,), jnp.float32) * sc
        inp['Wk'] = jax.random.normal(ks[7], (E, E), jnp.float32) * sc
        inp['bk'] = jax.random.normal(ks[8], (E,), jnp.float32) * sc
        inp['Wv'] = jax.random.normal(ks[9], (E, E), jnp.float32) * sc
        inp['bv'] = jax.random.normal(ks[10], (E,), jnp.float32) * sc
        inp['Wo'] = jax.random.normal(ks[11], (E, E), jnp.float32) * sc
        inp['bo'] = jax.random.normal(ks[12], (E,), jnp.float32) * sc
        return inp
    _L2_xattn_all = _L2_xattn_setup()
    _L2_xattn_in = {k: v for k, v in _L2_xattn_all.items() if k in ('adj', 'Wq', 'bq', 'Wk', 'bk', 'Wv', 'bv', 'Wo', 'bo')}
    del _L2_xattn_all

    def _L2_ffn_setup():
        import jax, jax.numpy as jnp
        import numpy as np
        TOP_K = 2
        key = jax.random.key(seed)
        ks = jax.random.split(key, 5)
        B, S, D, I, E = (4, 64, 128, 512, 8)
        x = jax.random.normal(ks[0], (B, S, D), dtype=jnp.float32)
        gate_w = jax.random.normal(ks[1], (E, D), dtype=jnp.float32) * 0.02
        w1 = jax.random.normal(ks[2], (E, I, D), dtype=jnp.float32) * 0.02
        w2 = jax.random.normal(ks[3], (E, D, I), dtype=jnp.float32) * 0.02
        w3 = jax.random.normal(ks[4], (E, I, D), dtype=jnp.float32) * 0.02
        return {'x': x, 'gate_w': gate_w, 'w1': w1, 'w2': w2, 'w3': w3}
    _L2_ffn_all = _L2_ffn_setup()
    _L2_ffn_in = {k: v for k, v in _L2_ffn_all.items() if k in ('gate_w', 'w1', 'w2', 'w3')}
    del _L2_ffn_all

    def _L3_attn_setup():
        import jax, jax.numpy as jnp
        import numpy as np
        B, L, D_MODEL, H, HD, FD = (1, 128, 128, 16, 64, 64)
        EPS = 1e-12

        def _heads(t):
            b, l, _ = t.shape
            return t.reshape(b, l, H, HD).transpose(0, 2, 1, 3)

        def _feature_map(t, K):
            f = jnp.einsum('hdf,bhld->bhlf', K, t)
            feats = jnp.concatenate([jax.nn.softmax(f, axis=-1), jax.nn.softmax(-f, axis=-1)], axis=-1)
            return jnp.maximum(feats, EPS)
        key = jax.random.key(seed)
        ks = jax.random.split(key, 7)
        s = 1.0 / np.sqrt(D_MODEL)
        return {'x': jax.random.normal(ks[0], (B, L, D_MODEL), jnp.float32), 'Wq': jax.random.normal(ks[1], (D_MODEL, H * HD), jnp.float32) * s, 'Wk': jax.random.normal(ks[2], (D_MODEL, H * HD), jnp.float32) * s, 'Wv': jax.random.normal(ks[3], (D_MODEL, H * HD), jnp.float32) * s, 'Wo': jax.random.normal(ks[4], (H * HD, D_MODEL), jnp.float32) * s, 'Kq': jax.random.normal(ks[5], (H, HD, FD), jnp.float32) * (1.0 / np.sqrt(HD)), 'Kk': jax.random.normal(ks[6], (H, HD, FD), jnp.float32) * (1.0 / np.sqrt(HD))}
    _L3_attn_all = _L3_attn_setup()
    _L3_attn_in = {k: v for k, v in _L3_attn_all.items() if k in ('Wq', 'Wk', 'Wv', 'Wo', 'Kq', 'Kk')}
    del _L3_attn_all

    def _L3_xattn_setup():
        import jax, jax.numpy as jnp
        import numpy as np
        N_HEAD = 16
        key = jax.random.key(seed)
        ks = jax.random.split(key, 5)
        b, l, d = (4, 256, 128)
        dh = d // N_HEAD
        return {'q': jax.random.normal(ks[0], (b, l, d), dtype=jnp.float32), 'kv': jax.random.normal(ks[1], (b, l, d), dtype=jnp.float32), 'Wq': jax.random.normal(ks[2], (d, d), dtype=jnp.float32) * 0.02, 'Wkv': jax.random.normal(ks[3], (2 * dh, d), dtype=jnp.float32) * 0.02, 'Wc': jax.random.normal(ks[4], (d, d), dtype=jnp.float32) * 0.02}
    _L3_xattn_all = _L3_xattn_setup()
    _L3_xattn_in = {k: v for k, v in _L3_xattn_all.items() if k in ('Wq', 'Wkv', 'Wc')}
    del _L3_xattn_all

    def _L3_ffn_setup():
        import jax, jax.numpy as jnp
        import numpy as np
        HIDDEN = 128
        NUM_EXPERTS = 8
        TOP_K = 2
        B, S = (4, 128)
        key = jax.random.key(seed)
        ks = jax.random.split(key, 8)
        H, E = (HIDDEN, NUM_EXPERTS)
        sc = lambda fan_in: 1.0 / np.sqrt(fan_in)
        x = jax.random.normal(ks[0], (B, S, H), dtype=jnp.float32)
        Wr = jax.random.uniform(ks[1], (H, E), minval=-sc(H), maxval=sc(H), dtype=jnp.float32)
        br = jax.random.uniform(ks[2], (E,), minval=-sc(H), maxval=sc(H), dtype=jnp.float32)
        W1 = jax.random.uniform(ks[3], (E, H, 2 * H), minval=-sc(H), maxval=sc(H), dtype=jnp.float32)
        b1 = jax.random.uniform(ks[4], (E, 2 * H), minval=-sc(H), maxval=sc(H), dtype=jnp.float32)
        W2 = jax.random.uniform(ks[5], (E, 2 * H, H), minval=-sc(2 * H), maxval=sc(2 * H), dtype=jnp.float32)
        b2 = jax.random.uniform(ks[6], (E, H), minval=-sc(2 * H), maxval=sc(2 * H), dtype=jnp.float32)
        return {'x': x, 'Wr': Wr, 'br': br, 'W1': W1, 'b1': b1, 'W2': W2, 'b2': b2}
    _L3_ffn_all = _L3_ffn_setup()
    _L3_ffn_in = {k: v for k, v in _L3_ffn_all.items() if k in ('Wr', 'br', 'W1', 'b1', 'W2', 'b2')}
    del _L3_ffn_all
    return {'x': x, 'ctx_1024': ctx_1024, 'mask_Bx1xSxS2_ik1': mask_Bx1xSxS2_ik1, 'L0_attn_A_log': _L0_attn_in['A_log'], 'L0_attn_W_xdt': _L0_attn_in['W_xdt'], 'L0_attn_b_xdt': _L0_attn_in['b_xdt'], 'L0_attn_W_dt': _L0_attn_in['W_dt'], 'L0_attn_b_dt': _L0_attn_in['b_dt'], 'L0_attn_W_B': _L0_attn_in['W_B'], 'L0_attn_b_B': _L0_attn_in['b_B'], 'L0_attn_W_C': _L0_attn_in['W_C'], 'L0_attn_b_C': _L0_attn_in['b_C'], 'L0_attn_D': _L0_attn_in['D'], 'L0_xattn_Wq': _L0_xattn_in['Wq'], 'L0_xattn_bq': _L0_xattn_in['bq'], 'L0_xattn_Wk': _L0_xattn_in['Wk'], 'L0_xattn_bk': _L0_xattn_in['bk'], 'L0_xattn_Wv': _L0_xattn_in['Wv'], 'L0_xattn_bv': _L0_xattn_in['bv'], 'L0_xattn_Wo': _L0_xattn_in['Wo'], 'L0_xattn_bo': _L0_xattn_in['bo'], 'L0_ffn_qw': _L0_ffn_in['qw'], 'L0_ffn_qb': _L0_ffn_in['qb'], 'L0_ffn_kw': _L0_ffn_in['kw'], 'L0_ffn_kb': _L0_ffn_in['kb'], 'L0_ffn_vw': _L0_ffn_in['vw'], 'L0_ffn_vb': _L0_ffn_in['vb'], 'L0_ffn_ow': _L0_ffn_in['ow'], 'L0_ffn_ob': _L0_ffn_in['ob'], 'L0_ffn_gate_w': _L0_ffn_in['gate_w'], 'L0_ffn_w1': _L0_ffn_in['w1'], 'L0_ffn_w2': _L0_ffn_in['w2'], 'L0_ffn_norm1_w': _L0_ffn_in['norm1_w'], 'L0_ffn_norm2_w': _L0_ffn_in['norm2_w'], 'L1_attn_weight': _L1_attn_in['weight'], 'L1_xattn_w_q': _L1_xattn_in['w_q'], 'L1_xattn_w_k': _L1_xattn_in['w_k'], 'L1_xattn_w_v': _L1_xattn_in['w_v'], 'L1_xattn_w_o': _L1_xattn_in['w_o'], 'L1_ffn_Wg': _L1_ffn_in['Wg'], 'L1_ffn_bg': _L1_ffn_in['bg'], 'L1_ffn_W1': _L1_ffn_in['W1'], 'L1_ffn_b1': _L1_ffn_in['b1'], 'L1_ffn_W2': _L1_ffn_in['W2'], 'L1_ffn_b2': _L1_ffn_in['b2'], 'L2_attn_w_qkv': _L2_attn_in['w_qkv'], 'L2_attn_b_qkv': _L2_attn_in['b_qkv'], 'L2_attn_w_out': _L2_attn_in['w_out'], 'L2_attn_b_out': _L2_attn_in['b_out'], 'L2_xattn_adj': _L2_xattn_in['adj'], 'L2_xattn_Wq': _L2_xattn_in['Wq'], 'L2_xattn_bq': _L2_xattn_in['bq'], 'L2_xattn_Wk': _L2_xattn_in['Wk'], 'L2_xattn_bk': _L2_xattn_in['bk'], 'L2_xattn_Wv': _L2_xattn_in['Wv'], 'L2_xattn_bv': _L2_xattn_in['bv'], 'L2_xattn_Wo': _L2_xattn_in['Wo'], 'L2_xattn_bo': _L2_xattn_in['bo'], 'L2_ffn_gate_w': _L2_ffn_in['gate_w'], 'L2_ffn_w1': _L2_ffn_in['w1'], 'L2_ffn_w2': _L2_ffn_in['w2'], 'L2_ffn_w3': _L2_ffn_in['w3'], 'L3_attn_Wq': _L3_attn_in['Wq'], 'L3_attn_Wk': _L3_attn_in['Wk'], 'L3_attn_Wv': _L3_attn_in['Wv'], 'L3_attn_Wo': _L3_attn_in['Wo'], 'L3_attn_Kq': _L3_attn_in['Kq'], 'L3_attn_Kk': _L3_attn_in['Kk'], 'L3_xattn_Wq': _L3_xattn_in['Wq'], 'L3_xattn_Wkv': _L3_xattn_in['Wkv'], 'L3_xattn_Wc': _L3_xattn_in['Wc'], 'L3_ffn_Wr': _L3_ffn_in['Wr'], 'L3_ffn_br': _L3_ffn_in['br'], 'L3_ffn_W1': _L3_ffn_in['W1'], 'L3_ffn_b1': _L3_ffn_in['b1'], 'L3_ffn_W2': _L3_ffn_in['W2'], 'L3_ffn_b2': _L3_ffn_in['b2']}

def reference(x, ctx_1024, mask_Bx1xSxS2_ik1, L0_attn_A_log, L0_attn_W_xdt, L0_attn_b_xdt, L0_attn_W_dt, L0_attn_b_dt, L0_attn_W_B, L0_attn_b_B, L0_attn_W_C, L0_attn_b_C, L0_attn_D, L0_xattn_Wq, L0_xattn_bq, L0_xattn_Wk, L0_xattn_bk, L0_xattn_Wv, L0_xattn_bv, L0_xattn_Wo, L0_xattn_bo, L0_ffn_qw, L0_ffn_qb, L0_ffn_kw, L0_ffn_kb, L0_ffn_vw, L0_ffn_vb, L0_ffn_ow, L0_ffn_ob, L0_ffn_gate_w, L0_ffn_w1, L0_ffn_w2, L0_ffn_norm1_w, L0_ffn_norm2_w, L1_attn_weight, L1_xattn_w_q, L1_xattn_w_k, L1_xattn_w_v, L1_xattn_w_o, L1_ffn_Wg, L1_ffn_bg, L1_ffn_W1, L1_ffn_b1, L1_ffn_W2, L1_ffn_b2, L2_attn_w_qkv, L2_attn_b_qkv, L2_attn_w_out, L2_attn_b_out, L2_xattn_adj, L2_xattn_Wq, L2_xattn_bq, L2_xattn_Wk, L2_xattn_bk, L2_xattn_Wv, L2_xattn_bv, L2_xattn_Wo, L2_xattn_bo, L2_ffn_gate_w, L2_ffn_w1, L2_ffn_w2, L2_ffn_w3, L3_attn_Wq, L3_attn_Wk, L3_attn_Wv, L3_attn_Wo, L3_attn_Kq, L3_attn_Kk, L3_xattn_Wq, L3_xattn_Wkv, L3_xattn_Wc, L3_ffn_Wr, L3_ffn_br, L3_ffn_W1, L3_ffn_b1, L3_ffn_W2, L3_ffn_b2):
    import jax
    import jax.numpy as jnp

    def _L0_attn_ref(u, A_log, W_xdt, b_xdt, W_dt, b_dt, W_B, b_B, W_C, b_C, D):
        import jax, jax.numpy as jnp
        import numpy as np
        B_SZ, T, D_MODEL, D_STATE, DT_RANK = (4, 256, 128, 16, 64)
        A = -jnp.exp(A_log)
        x_dt = jnp.einsum('btd,rd->btr', u, W_xdt) + b_xdt
        dt = jax.nn.softplus(jnp.einsum('btr,dr->btd', x_dt, W_dt) + b_dt)
        Bt = jnp.einsum('btd,nd->btn', u, W_B) + b_B
        Ct = jnp.einsum('btd,nd->btn', u, W_C) + b_C

        def step(h, inputs):
            u_t, dt_t, B_t, C_t = inputs
            A_bar = jnp.exp(dt_t[:, :, None] * A[None, :, :])
            B_bar = dt_t[:, :, None] * B_t[:, None, :]
            h = A_bar * h + B_bar * u_t[:, :, None]
            y_t = jnp.sum(h * C_t[:, None, :], axis=-1) + D * u_t
            return (h, y_t)
        h0 = jnp.zeros((u.shape[0], A.shape[0], A.shape[1]), dtype=u.dtype)
        xs = (jnp.swapaxes(u, 0, 1), jnp.swapaxes(dt, 0, 1), jnp.swapaxes(Bt, 0, 1), jnp.swapaxes(Ct, 0, 1))
        _, ys = jax.lax.scan(step, h0, xs)
        return jnp.swapaxes(ys, 0, 1)

    def _L0_xattn_ref(q, k, v, Wq, bq, Wk, bk, Wv, bv, Wo, bo):
        import jax, jax.numpy as jnp
        import numpy as np
        D_MODEL = 128
        NUM_HEADS = 16
        HEAD_DIM = D_MODEL // NUM_HEADS

        def _split_heads(x):
            B, S, _ = x.shape
            return x.reshape(B, S, NUM_HEADS, HEAD_DIM).transpose(0, 2, 1, 3)
        B, S, _ = q.shape
        qh = _split_heads(q @ Wq.T + bq)
        kh = _split_heads(k @ Wk.T + bk)
        vh = _split_heads(v @ Wv.T + bv)
        scale = 1.0 / jnp.sqrt(jnp.asarray(HEAD_DIM, qh.dtype))
        scores = jnp.einsum('bhqd,bhkd->bhqk', qh, kh) * scale
        attn = jax.nn.softmax(scores, axis=-1)
        out = jnp.einsum('bhqk,bhkd->bhqd', attn, vh)
        out = out.transpose(0, 2, 1, 3).reshape(B, S, D_MODEL)
        return out @ Wo.T + bo

    def _L0_ffn_ref(x, qw, qb, kw, kb, vw, vb, ow, ob, gate_w, w1, w2, norm1_w, norm2_w):
        import jax, jax.numpy as jnp
        import numpy as np
        D_MODEL = 128
        N_HEADS = 16
        N_KV = 4
        NUM_REP = N_HEADS // N_KV
        HEAD_DIM = D_MODEL // N_HEADS
        N_EXPERTS = 8
        TOP_K = 2
        CAP_FACTOR = 1.25
        EPS_NORM = 1e-06

        def _rmsnorm(x, w):
            var = jnp.mean(x * x, axis=-1, keepdims=True)
            return w * (x * jax.lax.rsqrt(var + EPS_NORM))

        def _gqa(x, qw, qb, kw, kb, vw, vb, ow, ob):
            B, S, D = x.shape
            q = (x @ qw + qb).reshape(B, S, N_HEADS, HEAD_DIM).transpose(0, 2, 1, 3)
            k = (x @ kw + kb).reshape(B, S, N_KV, HEAD_DIM).transpose(0, 2, 1, 3)
            v = (x @ vw + vb).reshape(B, S, N_KV, HEAD_DIM).transpose(0, 2, 1, 3)
            k = jnp.repeat(k, NUM_REP, axis=1)
            v = jnp.repeat(v, NUM_REP, axis=1)
            scores = jnp.einsum('bhqd,bhkd->bhqk', q, k) / np.sqrt(HEAD_DIM).astype(np.float32)
            attn = jax.nn.softmax(scores, axis=-1)
            out = jnp.einsum('bhqk,bhkd->bhqd', attn, v)
            out = out.transpose(0, 2, 1, 3).reshape(B, S, D)
            return out @ ow + ob

        def _moe(x, gate_w, w1, w2):
            B, S, D = x.shape
            T = B * S
            x_flat = x.reshape(T, D)
            capacity = int(CAP_FACTOR * T * TOP_K / N_EXPERTS)
            logits = x_flat @ gate_w
            probs = jax.nn.sigmoid(logits)
            _, sel = jax.lax.top_k(probs, TOP_K)
            w_topk = jnp.take_along_axis(probs, sel, axis=1)
            w_topk = w_topk / (jnp.sum(w_topk, axis=-1, keepdims=True) + 1e-06)
            flat_sel = sel.reshape(-1)
            em = jax.nn.one_hot(flat_sel, N_EXPERTS, dtype=jnp.int32)
            ranks = jnp.take_along_axis(jnp.cumsum(em, axis=0), flat_sel[:, None], axis=1)[:, 0] - 1
            valid = ranks < capacity
            slot = flat_sel * capacity + ranks
            scatter_idx = jnp.where(valid, slot, N_EXPERTS * capacity)
            x_rep = jnp.repeat(x_flat, TOP_K, axis=0)
            padded = jnp.zeros((N_EXPERTS * capacity + 1, D), x.dtype).at[scatter_idx].set(x_rep)
            padded_x = padded[:N_EXPERTS * capacity].reshape(N_EXPERTS, capacity, D)
            h = jax.nn.gelu(jnp.einsum('ecd,edf->ecf', padded_x, w1), approximate=False)
            out_padded = jnp.einsum('ecf,efd->ecd', h, w2).reshape(N_EXPERTS * capacity, D)
            gather_idx = jnp.where(valid, slot, 0)
            out_rep = jnp.where(valid[:, None], out_padded[gather_idx], 0.0)
            out_w = out_rep * w_topk.reshape(-1)[:, None]
            return out_w.reshape(T, TOP_K, D).sum(axis=1).reshape(B, S, D)
        src = x + _gqa(x, qw, qb, kw, kb, vw, vb, ow, ob)
        src = _rmsnorm(src, norm1_w)
        src = src + _moe(src, gate_w, w1, w2)
        return _rmsnorm(src, norm2_w)

    def _L1_attn_ref(x, weight):
        import math
        import jax, jax.numpy as jnp
        import numpy as np
        NUM_HEADS = 16
        EMBED = 128
        B, T = (2, 256)
        b, t, c = x.shape
        nh = NUM_HEADS
        hs = c // nh
        y = x.reshape(b, t, nh, hs).transpose(0, 2, 1, 3)
        scores = jnp.einsum('bhtk,bhsk->bhts', y, y) / math.sqrt(hs)
        attn = jax.nn.softmax(scores, axis=-1)
        o = jnp.einsum('bhts,bsc->bhtc', attn, x)
        o = o.transpose(0, 2, 1, 3).reshape(b, t, nh * c)
        return o @ weight

    def _L1_xattn_ref(query, kv_source, w_q, w_k, w_v, w_o):
        import jax, jax.numpy as jnp
        import numpy as np
        D_MODEL = 128
        N_HEADS = 16
        HEAD_DIM = D_MODEL // N_HEADS
        B, T_q, _ = query.shape
        T_kv = kv_source.shape[1]
        q = (query @ w_q.T).reshape(B, T_q, N_HEADS, HEAD_DIM)
        k = (kv_source @ w_k.T).reshape(B, T_kv, N_HEADS, HEAD_DIM)
        v = (kv_source @ w_v.T).reshape(B, T_kv, N_HEADS, HEAD_DIM)
        scale = HEAD_DIM ** (-0.5)
        attn = jax.nn.softmax(jnp.einsum('bqhd,bkhd->bhqk', q, k) * scale, axis=-1)
        out = jnp.einsum('bhqk,bkhd->bqhd', attn, v).reshape(B, T_q, D_MODEL)
        return out @ w_o.T

    def _L1_ffn_ref(x, Wg, bg, W1, b1, W2, b2):
        import jax, jax.numpy as jnp
        import numpy as np
        B, S, D, H, E, K = (4, 256, 128, 256, 8, 2)
        TEMP = 5.0
        EPS = 1e-09
        logits = jnp.einsum('bsd,de->bse', x, Wg) + bg
        probs = jax.nn.softmax(logits / TEMP, axis=-1)
        vals, idx = jax.lax.top_k(probs, K)
        onehot = jax.nn.one_hot(idx, E, dtype=x.dtype)
        mask = jnp.einsum('bske,bsk->bse', onehot, vals)
        gates = mask / (jnp.sum(mask, axis=-1, keepdims=True) + EPS)
        h = jax.nn.gelu(jnp.einsum('bsd,edh->besh', x, W1) + b1[None, :, None, :], approximate=False)
        out = jnp.einsum('besh,ehd->besd', h, W2) + b2[None, :, None, :]
        y = jnp.einsum('bse,besd->bsd', gates, out)
        return y

    def _L2_attn_ref(x, w_qkv, b_qkv, w_out, b_out):
        import jax, jax.numpy as jnp
        import numpy as np
        EMBED_DIM = 128
        NUM_HEADS = 16
        HEAD_DIM = EMBED_DIM // NUM_HEADS
        SCALE = 1.0 / float(np.sqrt(HEAD_DIM))
        B, S, E = x.shape
        H, Dh = (NUM_HEADS, HEAD_DIM)
        qkv = x @ w_qkv + b_qkv
        qkv = qkv.reshape(B, S, 3, H, Dh)
        qkv = jnp.transpose(qkv, (2, 0, 3, 1, 4))
        q, k, v = (qkv[0], qkv[1], qkv[2])
        scores = jnp.einsum('bhqd,bhkd->bhqk', q, k) * SCALE
        causal = jnp.triu(jnp.full((S, S), -jnp.inf, dtype=scores.dtype), k=1)
        scores = scores + causal
        attn = jax.nn.softmax(scores, axis=-1)
        out = jnp.einsum('bhqk,bhkd->bhqd', attn, v)
        out = jnp.transpose(out, (0, 2, 1, 3)).reshape(B, S, E)
        return out @ w_out + b_out

    def _L2_xattn_ref(query, key, value, adj, mask, Wq, bq, Wk, bk, Wv, bv, Wo, bo):
        import jax, jax.numpy as jnp
        import numpy as np
        B, S, E, H = (2, 256, 128, 16)
        D = E // H
        b, s, _ = query.shape

        def heads(x, W, bias):
            y = jnp.einsum('bse,ef->bsf', x, W.T) + bias
            return y.reshape(b, s, H, D).transpose(0, 2, 1, 3)
        Q = heads(query, Wq, bq)
        K = heads(key, Wk, bk)
        V = heads(value, Wv, bv)
        scores = jnp.einsum('bhqd,bhkd->bhqk', Q, K) / jnp.sqrt(jnp.float32(D))
        scores = scores + adj[None, None, :, :]
        scores = jnp.where(mask == 0, jnp.float32(-jnp.inf), scores)
        weights = jax.nn.softmax(scores, axis=-1)
        out = jnp.einsum('bhqk,bhkd->bhqd', weights, V)
        out = out.transpose(0, 2, 1, 3).reshape(b, s, E)
        return jnp.einsum('bse,ef->bsf', out, Wo.T) + bo

    def _L2_ffn_ref(x, gate_w, w1, w2, w3):
        import jax, jax.numpy as jnp
        import numpy as np
        TOP_K = 2
        bsz, seq, dim = x.shape
        xt = x.reshape(-1, dim)
        scores = jnp.einsum('td,ed->te', xt, gate_w)
        probs = jax.nn.softmax(scores, axis=-1)
        expert_weights, expert_indices = jax.lax.top_k(probs, TOP_K)
        expert_weights = expert_weights / expert_weights.sum(-1, keepdims=True)
        x1 = jax.nn.silu(jnp.einsum('ti,eoi->teo', xt, w1))
        x3 = jnp.einsum('ti,eoi->teo', xt, w3)
        expert_outs = jnp.einsum('teo,eio->tei', x1 * x3, w2)
        sel = jnp.take_along_axis(expert_outs, expert_indices[:, :, None], axis=1)
        out = jnp.einsum('tai,ta->ti', sel, expert_weights)
        return out.reshape(bsz, seq, dim)

    def _L3_attn_ref(x, Wq, Wk, Wv, Wo, Kq, Kk):
        import jax, jax.numpy as jnp
        import numpy as np
        B, L, D_MODEL, H, HD, FD = (1, 128, 128, 16, 64, 64)
        EPS = 1e-12

        def _heads(t):
            b, l, _ = t.shape
            return t.reshape(b, l, H, HD).transpose(0, 2, 1, 3)

        def _feature_map(t, K):
            f = jnp.einsum('hdf,bhld->bhlf', K, t)
            feats = jnp.concatenate([jax.nn.softmax(f, axis=-1), jax.nn.softmax(-f, axis=-1)], axis=-1)
            return jnp.maximum(feats, EPS)
        q = _heads(x @ Wq)
        k = _heads(x @ Wk)
        v = _heads(x @ Wv)
        qf = _feature_map(q, Kq)
        kf = _feature_map(k, Kk)
        kv = jnp.cumsum(kf[:, :, :, None, :] * v[..., None], axis=2)
        o = jnp.einsum('bhlf,bhldf->bhld', qf, kv)
        z = jnp.einsum('bhlf,bhlf->bhl', qf, jnp.cumsum(kf, axis=2)) + EPS
        o = o / z[..., None]
        y = o.transpose(0, 2, 1, 3).reshape(x.shape[0], x.shape[1], H * HD)
        return y @ Wo

    def _L3_xattn_ref(q, kv, Wq, Wkv, Wc):
        import jax, jax.numpy as jnp
        import numpy as np
        N_HEAD = 16
        b, l, d = q.shape
        h = N_HEAD
        dh = d // h
        qp = jnp.einsum('bld,ed->ble', q, Wq)
        scores = jnp.einsum('bld,bmd->blm', qp, kv)
        idx = jnp.argmax(scores, axis=-1)
        mem = jnp.take_along_axis(kv, idx[..., None], axis=1)
        mkv = jnp.einsum('bld,ed->ble', mem, Wkv)
        mk, mv = jnp.split(mkv, 2, axis=-1)
        qh = qp.reshape(b, l, h, dh).transpose(0, 2, 1, 3)
        scale = 1.0 / np.sqrt(dh).astype(np.float32)
        logits = jnp.einsum('bhld,bmd->bhlm', qh, mk) * scale
        attn = jax.nn.softmax(logits, axis=-1)
        out = jnp.einsum('bhlm,bmd->bhld', attn, mv)
        out = out.transpose(0, 2, 1, 3).reshape(b, l, d)
        return jnp.einsum('bld,ed->ble', out, Wc)

    def _L3_ffn_ref(x, Wr, br, W1, b1, W2, b2):
        import jax, jax.numpy as jnp
        import numpy as np
        HIDDEN = 128
        NUM_EXPERTS = 8
        TOP_K = 2
        B, S = (4, 128)
        B_, S_, H = x.shape
        xf = x.reshape(-1, H)
        logits = xf @ Wr + br
        topk_w, topk_idx = jax.lax.top_k(logits, TOP_K)
        topk_w = jax.nn.softmax(topk_w, axis=-1)
        gate = jnp.sum(jax.nn.one_hot(topk_idx, NUM_EXPERTS, dtype=xf.dtype) * topk_w[..., None], axis=1)
        h = jax.nn.relu(jnp.einsum('th,ehf->etf', xf, W1) + b1[:, None, :])
        y = jnp.einsum('etf,efh->eth', h, W2) + b2[:, None, :]
        out = jnp.einsum('te,eth->th', gate, y)
        return out.reshape(B_, S_, H)
    x = _layernorm(x + _L0_attn_ref(x, L0_attn_A_log, L0_attn_W_xdt, L0_attn_b_xdt, L0_attn_W_dt, L0_attn_b_dt, L0_attn_W_B, L0_attn_b_B, L0_attn_W_C, L0_attn_b_C, L0_attn_D), axis=-1)
    x = _layernorm(x + _L0_xattn_ref(x, ctx_1024, ctx_1024, L0_xattn_Wq, L0_xattn_bq, L0_xattn_Wk, L0_xattn_bk, L0_xattn_Wv, L0_xattn_bv, L0_xattn_Wo, L0_xattn_bo), axis=-1)
    x = _layernorm(x + _L0_ffn_ref(x, L0_ffn_qw, L0_ffn_qb, L0_ffn_kw, L0_ffn_kb, L0_ffn_vw, L0_ffn_vb, L0_ffn_ow, L0_ffn_ob, L0_ffn_gate_w, L0_ffn_w1, L0_ffn_w2, L0_ffn_norm1_w, L0_ffn_norm2_w), axis=-1)
    x = _layernorm(x + _L1_attn_ref(x, L1_attn_weight), axis=-1)
    x = _layernorm(x + _L1_xattn_ref(x, ctx_1024, L1_xattn_w_q, L1_xattn_w_k, L1_xattn_w_v, L1_xattn_w_o), axis=-1)
    x = _layernorm(x + _L1_ffn_ref(x, L1_ffn_Wg, L1_ffn_bg, L1_ffn_W1, L1_ffn_b1, L1_ffn_W2, L1_ffn_b2), axis=-1)
    x = _layernorm(x + _L2_attn_ref(x, L2_attn_w_qkv, L2_attn_b_qkv, L2_attn_w_out, L2_attn_b_out), axis=-1)
    x = _layernorm(x + _L2_xattn_ref(x, ctx_1024, ctx_1024, L2_xattn_adj, mask_Bx1xSxS2_ik1, L2_xattn_Wq, L2_xattn_bq, L2_xattn_Wk, L2_xattn_bk, L2_xattn_Wv, L2_xattn_bv, L2_xattn_Wo, L2_xattn_bo), axis=-1)
    x = _layernorm(x + _L2_ffn_ref(x, L2_ffn_gate_w, L2_ffn_w1, L2_ffn_w2, L2_ffn_w3), axis=-1)
    x = _layernorm(x + _L3_attn_ref(x, L3_attn_Wq, L3_attn_Wk, L3_attn_Wv, L3_attn_Wo, L3_attn_Kq, L3_attn_Kk), axis=-1)
    x = _layernorm(x + _L3_xattn_ref(x, ctx_1024, L3_xattn_Wq, L3_xattn_Wkv, L3_xattn_Wc), axis=-1)
    x = _layernorm(x + _L3_ffn_ref(x, L3_ffn_Wr, L3_ffn_br, L3_ffn_W1, L3_ffn_b1, L3_ffn_W2, L3_ffn_b2), axis=-1)
    return x

_drawn_inputs = setup_inputs


def setup_inputs(seed=0):
    import zlib

    import numpy as np

    out = dict(_drawn_inputs(seed))
    spreads = {'L0_attn_D': (1.0, 0.2),
     'L0_xattn_bq': (0.0, 0.1),
     'L0_xattn_bk': (0.0, 0.8),
     'L0_xattn_bv': (0.0, 0.1),
     'L0_xattn_bo': (0.0, 0.1),
     'L0_ffn_qb': (0.0, 0.8),
     'L0_ffn_kb': (0.0, 0.8),
     'L0_ffn_vb': (0.0, 0.386),
     'L0_ffn_ob': (0.0, 0.1),
     'L0_ffn_norm1_w': (1.0, 0.2),
     'L0_ffn_norm2_w': (1.0, 0.2),
     'L1_ffn_bg': (0.0, 0.1),
     'L1_ffn_b1': (0.0, 0.432),
     'L1_ffn_b2': (0.0, 0.1)}
    factors = {'L0_attn_A_log': 8.0,
     'L0_attn_W_xdt': 8.0,
     'L0_attn_b_xdt': 8.0,
     'L0_attn_W_dt': 8.0,
     'L0_attn_b_dt': 6.547,
     'L0_attn_W_B': 4.444,
     'L0_attn_b_B': 8.0,
     'L0_attn_W_C': 4.455,
     'L0_attn_b_C': 8.0,
     'L0_ffn_qw': 8.0,
     'L0_ffn_kw': 8.0,
     'L0_ffn_gate_w': 5.427,
     'L0_ffn_w1': 4.867,
     'L0_ffn_w2': 4.454,
     'L1_ffn_W1': 2.869,
     'L2_xattn_bk': 8.0,
     'L2_ffn_gate_w': 5.494,
     'L2_ffn_w1': 6.585,
     'L2_ffn_w2': 5.569,
     'L2_ffn_w3': 5.34,
     'L3_attn_Wq': 3.969,
     'L3_attn_Wk': 4.219,
     'L3_attn_Kq': 4.317,
     'L3_attn_Kk': 4.068,
     'L3_ffn_b1': 3.902}
    for name, (base, spread) in spreads.items():
        noise = np.random.default_rng([zlib.crc32(name.encode()), seed]).standard_normal(out[name].shape)
        drawn = base * np.exp(spread * noise) if base else spread * noise
        out[name] = jnp.asarray(drawn.astype(out[name].dtype))
    for name, factor in factors.items():
        out[name] = (out[name] * factor).astype(out[name].dtype)
    return out
```

```python
from contextlib import ExitStack

import concourse.bass as bass
from concourse import mybir

B, S, D = 4, 256, 128
NH, DH = 16, 8
NT = B * S
TPB = S // 128
NTT = NT // 128
NE = 8
SCALE = float(DH) ** -0.5
NEG = -1e30
CAPACITY = int(1.25 * NT * 2 / NE)
LN_EPS = 1e-5
RMS_EPS = 1e-6
NSTATE, DT_RANK = 16, 64
HD, FD = 64, 64
Q_PARTS = (0, 0, 1, 0, 2, 1)
K_PARTS = (0, 1, 0, 2, 0, 1)
NBUF_P = 4

CROSS = (0, 3, 5)
SELF_WIDE = 2
CAUSAL = 4
MASKED = 5
GATHERED = 6
SUBLAYERS = [("mamba", 0), ("attn", 0), ("attn", 1), ("moe", 0), ("attn", 2), ("attn", 3), ("moe", 1),
             ("attn", 4), ("attn", 5), ("moe", 2), ("linear", 0), ("attn", 6), ("moe", 3)]
SUB_OF = {x: s for s, x in enumerate(SUBLAYERS)}
LAST = len(SUBLAYERS) - 1
MOE_F = (256, 256, 512, 256)


def finish_steps(s, b):
    steps = [("STAT", s, b)]
    if SUBLAYERS[s] == ("moe", 0):
        steps.append(("STAT2", s, b))
    steps.append(("NORM", s, b))
    if s != LAST:
        steps.append(("XT", s, b))
    return steps


def attention_prep(a, b):
    steps = []
    if a == GATHERED:
        steps += [("GQ", b)] + [("GS", b, t) for t in range(TPB)] + [("GT", b), ("GM", b)]
    if a == MASKED:
        steps.append(("BIAS", b))
    steps += [("QK", a, b), ("SPLIT", a, b)]
    if a == SELF_WIDE:
        steps += [("Z", b, i) for i in range(8)]
    else:
        steps += [("V", a, b)]
    return steps


def attention_tail(a, b):
    steps = []
    if a != SELF_WIDE:
        steps += [("OT", a, b, t) for t in range(TPB)] + [("OX", a, b), ("Y", a, b)]
    return steps + finish_steps(SUB_OF[("attn", a)], b)


def weigh(a, b, h):
    if a == SELF_WIDE:
        return [("ZV", b, h)]
    return [("PV", a, b, h)] + ([("OG", a, b, h // 4)] if h % 4 == 3 else [])


def spread(main, side, first=0):
    out, n = [], len(main) - first
    for i, steps in enumerate(main):
        out += steps
        if i >= first:
            lo, hi = (i - first) * len(side) // n, (i - first + 1) * len(side) // n
            out += side[lo:hi]
    return out


def attention_run(layers):
    units = [(a, p) for a in layers for p in range(B // 2)]
    out = attention_prep(units[0][0], 0) + attention_prep(units[0][0], 1)
    tail = []
    for i, (a, p) in enumerate(units):
        b0, b1 = 2 * p, 2 * p + 1
        out += spread([[("SM", a, b0, u)] for u in range(16)], tail, 3)
        out += [("MS", a, b0), ("MT", a, b0)]
        for h in range(NH):
            out += [("P2", a, b0, h), ("SM", a, b1, h)]
            if h >= 2:
                out += weigh(a, b0, h - 2)
        out += weigh(a, b0, NH - 2) + weigh(a, b0, NH - 1)
        out += [("MS", a, b1), ("MT", a, b1)]
        main = [[("P2", a, b1, h)] + (weigh(a, b1, h - 2) if h >= 2 else []) for h in range(NH)]
        main += [weigh(a, b1, NH - 2), weigh(a, b1, NH - 1)]
        side = attention_tail(a, b0)
        nxt = units[i + 1] if i + 1 < len(units) else None
        if nxt:
            side = side + attention_prep(nxt[0], 2 * nxt[1])
        out += spread(main, side, 1)
        if nxt and nxt[0] != a and nxt[1] == 0 or nxt and nxt[0] == a:
            out += attention_prep(nxt[0], 2 * nxt[1] + 1)
        tail = attention_tail(a, b1)
    return out + tail


def moe_steps(m):
    s = SUB_OF[("moe", m)]
    out, nf = [], MOE_F[m] // 128
    if m == 0:
        out += [("GATE", m, b) for b in range(B)] + [("RANK", m)]
    for c in range(2):
        if m:
            out += [("GATE", m, 2 * c), ("GATE", m, 2 * c + 1)]
        if m in (1, 3):
            out += [("GB", m, c), ("BI", m, c)]
        seq = [(e, f) for e in range(NE) for f in range(nf)]
        for i, (e, f) in enumerate(seq):
            out.append(("MH", m, c, e, f))
            if m == 2:
                out.append(("MG", m, c, e, f))
            if f == nf - 1 and e:
                out.append(("MO", m, c, e - 1))
        out.append(("MO", m, c, NE - 1))
        out += finish_steps(s, 2 * c) + finish_steps(s, 2 * c + 1)
    return out


def mamba_steps():
    out = [("DT", 0), ("DT", 1), ("DZ", 0), ("DZ", 1)]
    for n in range(NSTATE):
        for c in range(2):
            out += [("MB", n, c), ("MC", n, c)]
    for b in range(B):
        out += [("MY", b)] + finish_steps(0, b)
    return out


def linear_steps():
    s = SUB_OF[("linear", 0)]
    out = [("LC", w, i) for w in range(2) for i in range(2)]
    for b in range(B):
        parts = [(w, b, t, half) for t in range(TPB) for half in range(2) for w in range(2)]
        for i, part in enumerate(parts):
            out.append(("LF", *part))
            if i < 2 * TPB:
                out.append(("LV", b, i // 2, i % 2))
            if i:
                out += [("LS", *parts[i - 1]), ("LT", *parts[i - 1], 0), ("LT", *parts[i - 1], 1)]
        out += [("LS", *parts[-1]), ("LT", *parts[-1], 0), ("LT", *parts[-1], 1)]
        for h in range(NH):
            out.append(("LA", b, h))
            if h % 4 == 3:
                out += [("LO", b, h // 4, t) for t in range(TPB)]
        for t in range(TPB):
            out += [("LX", b, t, i) for i in range(2)]
        out.append(("LY", b))
        out += finish_steps(s, b)
    return out


def schedule():
    out = mamba_steps() + attention_run([0, 1]) + moe_steps(0) + attention_run([2, 3]) + moe_steps(1)
    return out + attention_run([4, 5]) + moe_steps(2) + linear_steps() + attention_run([6]) + moe_steps(3)


BANKS = {"max": 2, "exp": 3, "misc": 2}
USES = {
    "max": ("SM", "ZV", "MO", "BI", "LF", "LO"),
    "exp": ("P2", "MH", "MG", "LA", "MB", "MC"),
    "misc": ("QK", "V", "Z", "MT", "OT", "OX", "Y", "XT", "GATE", "RANK", "GB", "DT", "DZ", "MY",
             "GQ", "GS", "GT", "GM", "LC", "LV", "LT", "LX", "LY"),
}
POOL_OF = {k: p for p, ks in USES.items() for k in ks}


def decoder(nc, I, scratch, out):
    fp32, bf16, u32, i32 = mybir.dt.float32, mybir.dt.bfloat16, mybir.dt.uint32, mybir.dt.int32
    ALU, ACT, AX = mybir.AluOpType, mybir.ActivationFunctionType, mybir.AxisListType
    steps = schedule()
    count, seen, turn, turns, bank_steps = {}, {}, {}, {p: 0 for p in BANKS}, {p: [] for p in BANKS}
    for st in steps:
        seen[st[0]] = seen.get(st[0], 0) + 1
        count[st] = seen[st[0]]
        if st[0] in POOL_OF:
            p = POOL_OF[st[0]]
            turn[st] = turns[p]
            turns[p] += 1
            bank_steps[p].append(st)
    with ExitStack() as ctx:
        def sb(name, shape, dt=fp32):
            return ctx.enter_context(nc.sbuf_tensor(name, shape, dt))

        def sem(name):
            return ctx.enter_context(nc.semaphore(name))

        bank = {p: [ctx.enter_context(nc.psum_tensor(f"bank_{p}{i}", [128, 512], fp32)) for i in range(n)]
                for p, n in BANKS.items()}
        weigh_bank = ctx.enter_context(nc.psum_tensor("bank_weigh", [128, 512], fp32))

        def psum(st):
            p = POOL_OF[st[0]]
            return bank[p][turn[st] % BANKS[p]]

        x_tok = sb("x_tok", [128, NTT, D])
        xT = sb("xT", [128, NT])
        ctxT = sb("ctxT", [128, NT])
        res = sb("res", [128, 2, TPB, D])
        stats = sb("stats", [128, TPB, 6])
        mv = sb("mv", [128, 2, TPB, 2])
        rstd = sb("rstd", [128, 2, TPB])
        minus_half = sb("minus_half", [128, TPB])
        wA = sb("wA", [128, 7, 4, D])
        bqk = sb("bqk", [128, 7, 2])
        bvo = sb("bvo", [128, 7, 2, D])
        qk32 = sb("qk32", [128, 2, 2, S])
        rem = sb("rem", [128, 2, S])
        parts = sb("parts", [128, 2, 2, 3, S], bf16)
        QR = sb("QR", [128, 2, NH, S], bf16)
        KR = sb("KR", [128, 2, NH, S], bf16)
        V = sb("V", [128, 2, TPB, NH, 32])
        mx = sb("mx", [128, 2, TPB, NH])
        ms = sb("ms", [128, 2, TPB, 128], bf16)
        msT = sb("msT", [128, 2, S], bf16)
        P = sb("P", [128, NBUF_P, TPB * S])
        og = sb("og", [128, 2, 4, S])
        rden = sb("rden", [128, TPB, NH])
        o = sb("o", [128, TPB, D])
        oT = sb("oT", [128, S])
        acc = sb("acc", [128, 4, D])
        ident = sb("ident", [128, 128])
        identb = sb("identb", [128, 128], bf16)
        pick = sb("pick", [128, NH], bf16)
        causal_q = sb("causal_q", [128, TPB, S], bf16)
        causal_k = sb("causal_k", [128, TPB, S], bf16)
        keep_past = sb("keep_past", [128, TPB * S], bf16)
        earlier = sb("earlier", [128, 128])
        ones = sb("ones", [128, 128])
        iota = sb("iota", [128, S])
        gate_w = sb("gate_w", [128, 4, NE])
        gate_b = sb("gate_b", [128, 4, NE])
        b1 = sb("b1", [128, 2, NE, 2])
        b2 = sb("b2", [NE, 2, D])
        norm_w = sb("norm_w", [128, 2, D])
        w13 = sb("w13", [128, 2, NE, 512])
        w1, w3 = w13[:, 0], w13[:, 1]
        w2 = sb("w2", [128, NE, 4, D])
        wide_w = w13[:, 1].rearrange("p e f -> p (e f)")[:, 0:NH * D]
        featT = w13[:, :, :, :].rearrange("p w e (x s) -> p w (e x) s", s=S)
        logits = sb("logits", [128, TPB, NE])
        top = sb("top", [128, TPB, 8])
        top_at = sb("top_at", [128, TPB, 8], u32)
        top_atf = sb("top_atf", [128, TPB, 8])
        gw = sb("gw", [128, TPB, 8])
        gs = sb("gs", [128, TPB, 8])
        gden = sb("gden", [128, TPB, 1])
        gz = sb("gz", [128, TPB, 1])
        gtmp = sb("gtmp", [128, NE])
        gates = sb("gates", [128, NTT, NE])
        chosen = sb("chosen", [128, NTT, NE])
        prefix = sb("prefix", [128, NTT, NE])
        gT = sb("gT", [NE, 512])
        AREA = 9216
        area = sb("area", [128, AREA])
        at = [0]

        def carve(*shape, room=None):
            n = 1
            for k in shape:
                n *= k
            base = area[:, :] if room is None else room
            v = base[:, at[0]:at[0] + n]
            at[0] += n
            assert at[0] <= base.shape[1], at[0]
            if len(shape) > 1:
                names = " ".join(f"a{i}" for i in range(len(shape)))
                v = v.rearrange(f"p ({names}) -> p {names}", **{f"a{i}": k for i, k in enumerate(shape)})
            return v

        w13_room = w13[:, :, :, :].rearrange("p w e f -> p (w e f)")
        w2_room = w2[:, :, :, :].rearrange("p e f d -> p (e f d)")
        xdt, zb, dt, dtu, yacc = (carve(NT, room=w13_room) for _ in range(5))
        absz, softp = carve(512, room=w13_room), carve(512, room=w13_room)
        abar, bu = carve(2, 512, room=w13_room), carve(2, 512, room=w13_room)
        at[0] = 0
        hs, gc = carve(2, 512, room=w2_room), carve(2, 512, room=w2_room)
        wx_dt, w_dt = carve(DT_RANK, room=w2_room), carve(D, room=w2_room)
        wBC, negA, bBC, vecs = (carve(2, NSTATE, room=w2_room), carve(NSTATE, room=w2_room),
                                carve(2, NSTATE, room=w2_room), carve(4, room=w2_room))
        iota_i = area[:, 0:S].bitcast(i32)
        at[0] = 0
        ZW = D + 2
        Z = carve(2, TPB, NH, ZW)
        at[0] = 0
        hT = carve(2, 4, 512)
        gated = carve(2, 512)
        x_before = area[:, at[0]:at[0] + NTT * D].rearrange("p (t d) -> p t d", d=D)
        lw = carve(4, 1024)
        at[0] = 0
        lraw_w = carve(2, 8, D)
        lraw_k = carve(2, 8, FD)
        at[0] = 0
        le, lv = carve(2, 8, 2, FD), carve(TPB, NH, HD + 1)
        at[0] = 0
        lf, lo = carve(8, 2, FD, room=w2_room), carve(TPB, NH * HD, room=w2_room)
        loT = og
        at[0] = 0
        ctx_tok = w13[:, 1].rearrange("p e f -> p (e f)")[:, 0:NTT * D].rearrange("p (t d) -> p t d", d=D)
        gq, one_hot, one_hotT, memT = carve(S), carve(2, S), carve(2, S), carve(2, S)
        at[0] = 0
        adj, biasf, biasr = carve(2, 2 * S), carve(2, 2 * S), carve(2, 2 * S)
        mask = area[:, at[0]:at[0] + 2 * 4 * S].bitcast(i32).rearrange("p (b o n) -> p b o n", b=2, o=2)
        at[0] += 2 * 4 * S
        bias_parts = carve(2 * 2 * 3 * S).bitcast(bf16).rearrange("p (b k o n) -> p b k o n", b=2, k=3, o=2)

        one_col = sb("one_col", [128, 1])
        lmax_v = sb("lmax", [128, 2, 8])
        gtmp2 = sb("lden", [128, NH])
        lden_v = gtmp2[:, :]
        filled = {k: sem(f"{k}_filled") for k in POOL_OF}
        read = {k: sem(f"{k}_read") for k in POOL_OF}
        filled["PV"] = sem("PV_filled")
        read["OG"] = sem("OG_read")
        consts, consts_pool = sem("consts"), sem("consts_pool")
        ctx_in, wide_in = sem("ctx_in"), sem("wide_in")
        loaded, mamba_in, moe_in, mask_in, lin_in = sem("loaded"), sem("mamba_in"), sem("moe_in"), sem("mask_in"), sem("lin_in")
        split_done, parts_stored, rows_in = sem("split_done"), sem("parts_stored"), [sem("rows_in0"), sem("rows_in1")]
        mask_more = [sem("mask2_in"), sem("mask3_in")]
        shift_done, bias_sum, bias_done, z_ones = sem("shift_done"), sem("bias_sum"), sem("bias_done"), sem("z_ones")
        stat_done, rstd_done, norm_done = sem("stat_done"), sem("rstd_done"), sem("norm_done")
        dve_chain, act_chain, pool_chain = sem("dve_chain"), sem("act_chain"), sem("pool_chain")
        dz_act, dz_dve, abar_done, scan_done, yacc_done, state_out = (
            sem("dz_act"), sem("dz_dve"), sem("abar_done"), sem("scan_done"), sem("yacc_done"), sem("state_out"))
        top_done, gate_exp, gates_done, ranked = sem("top_done"), sem("gate_exp"), sem("gates_done"), sem("ranked")
        lexp_done, lsum_done, lfeat_done, out_done = (
            sem("lexp_done"), sem("lsum_done"), sem("lfeat_done"), sem("out_done"))

        units = [st for st in steps if st[0] == "QK"]
        unit = {(st[1], st[2]): i for i, st in enumerate(units)}
        exps = [st for st in steps if st[0] == "P2"]

        def weighs(n):
            _, a, b, h = exps[n]
            return ("ZV", b, h) if a == SELF_WIDE else ("PV", a, b, h)

        STATS = [st for st in steps if st[0] in ("STAT", "STAT2")]
        stat_no = {st: i + 1 for i, st in enumerate(STATS)}

        def x_from(s, b):
            return ("XT", s - 1, b) if s else None

        def finished(eng, st):
            eng.wait_ge(read[st[0]], count[st])

        def full(eng, st):
            eng.wait_ge(filled[st[0]], count[st])

        block = ctx.enter_context(nc.Block())
        N_MAMBA, N_LIN = 9, 6
        N_LOADED0 = 9

        @block.sync
        def _(sp):
            def load(dst, name, to):
                sp.dma_start(dst, I[name]).then_inc(to, 16)

            load(xT[:, :], "xT", mamba_in)
            load(wx_dt[:, :], "w_xdt", mamba_in)
            load(w_dt[0:DT_RANK, :], "w_dt", mamba_in)
            load(wBC[:, :, :], "w_BC", mamba_in)
            load(negA[:, :], "A_log", mamba_in)
            load(bBC[:, :, :], "b_BC", mamba_in)
            load(vecs[:, 0:2], "dt_D", mamba_in)
            load(vecs[0:DT_RANK, 2:3], "b_xdt", mamba_in)
            load(x_tok[:, :, :], "x", mamba_in)
            load(ctxT[:, :], "ctxT", loaded)
            load(wA[:, :, :, :], "w_attn", loaded)
            load(bqk[:, :, :], "b_qk", loaded)
            load(bvo[:, :, :, :], "b_vo", loaded)
            load(gate_w[:, :, :], "gate_w", loaded)
            load(gate_b[:, :, :], "gate_b", loaded)
            load(b1[:, :, :, :], "b1", loaded)
            load(b2[:, :, :], "b2", loaded)
            load(norm_w[:, :, :], "norm_w", loaded)
            for st in steps:
                if st[0] == "SPLIT":
                    n = unit[st[1:]]
                    sp.wait_ge(split_done, n + 1)
                    if n >= 2:
                        sp.wait_ge(rows_in[n % 2], 192 * (n // 2))
                    sp.dma_start(scratch[n % 2].rearrange("q k p t -> p (q k) t"),
                                 parts[:, n % 2].rearrange("p q k t -> p (q k) t")).then_inc(parts_stored, 16)
                    sp.wait_ge(parts_stored, 16 * (n + 1))
                    if n >= 2:
                        full(sp, ("P2", units[n - 2][1], units[n - 2][2], NH - 1))
                    else:
                        sp.wait_ge(consts, 1)
                    for t in range(6):
                        for q, (rows, which) in enumerate(((QR, Q_PARTS), (KR, K_PARTS))):
                            sp.dma_start(rows[DH * t:DH * (t + 1), n % 2],
                                         scratch[n % 2, q, which[t]].rearrange("(h d) t -> d h t", d=DH)).then_inc(rows_in[n % 2], 16)
                elif st == ("MY", B - 1):
                    full(sp, st)
                    load(wide_w, "wide_w", wide_in)
                    load(w1[:, :, 0:256], "w1_0", moe_in)
                    load(w2[:, :, 0:2, :], "w2_0", moe_in)
                elif st[0] == "BIAS":
                    b = st[1]
                    if b == 0:
                        load(adj, "adj", mask_in)
                        load(mask[:, 0], "mask0", mask_in)
                        load(mask[:, 1], "mask1", mask_in)
                    elif b < 3:
                        sp.wait_ge(bias_sum, b)
                        load(mask[:, (b + 1) % 2], f"mask{b + 1}", mask_more[b - 1])
                elif st == ("MO", 0, 1, NE - 1):
                    full(sp, st)
                    load(w1[:, :, 0:256], "w1_1", moe_in)
                    load(w2[:, :, 0:2, :], "w2_1", moe_in)
                elif st == ("MO", 1, 1, NE - 1):
                    full(sp, st)
                    finished(sp, st)
                    load(w1[:, :, :], "w1_2", moe_in)
                    load(w3[:, :, :], "w3_2", moe_in)
                    load(w2[:, :, :, :], "w2_2", moe_in)
                elif st == ("MO", 2, 1, NE - 1):
                    full(sp, st)
                    load(lw[:, 2, :], "lin_v", lin_in)
                    load(lw[:, 3, :], "lin_o", lin_in)
                    for i in range(2):
                        load(lraw_w[64 * i:64 * i + 64, :, :, :], f"lin_w{i}", lin_in)
                        load(lraw_k[64 * i:64 * i + 64, :, :, :], f"lin_k{i}", lin_in)
                elif st == ("LA", B - 1, NH - 1):
                    full(sp, st)
                    finished(sp, st)
                    load(w1[:, :, 0:256], "w1_3", moe_in)
                    load(ctx_tok, "ctx", ctx_in)
                elif st == ("LY", B - 1):
                    full(sp, st)
                    load(w2[:, :, 0:2, :], "w2_3", moe_in)
                elif st[0] == "NORM" and st[1] == LAST:
                    b = st[2]
                    sp.wait_ge(norm_done, count[st])
                    sp.dma_start(out[b].rearrange("(t p) d -> p t d", p=128),
                                 x_tok[:, TPB * b:TPB * (b + 1), :]).then_inc(out_done, 16)
            sp.wait_ge(out_done, 16 * B)

        def mask_terms(a, b, orientation, t):
            if a == CAUSAL:
                return [causal_q[:, t, :]] if orientation == 0 else [causal_k[:, :, :].rearrange("p t s -> p (t s)")]
            if a == MASKED:
                if orientation == 0:
                    return [bias_parts[:, b % 2, i, 0, t * S:(t + 1) * S] for i in range(3)]
                return [bias_parts[:, b % 2, i, 1, :] for i in range(3)]
            return []

        def loTv(t, j):
            return loT[:, t, j // 2, (j % 2) * 128:(j % 2 + 1) * 128]

        MOE_LOADS = (2, 4, 7, 9)

        @block.tensor
        def _(pe):
            def src(a, b):
                if a == GATHERED:
                    return memT[:, unit[(a, b)] % 2, :]
                return (ctxT if a in CROSS else xT)[:, b * S:(b + 1) * S]

            def wait_x(s, b):
                if s:
                    finished(pe, ("XT", s - 1, b))

            pe.wait_ge(consts_pool, 1)
            pe.wait_ge(mamba_in, 16 * N_MAMBA)
            for st in steps:
                k = st[0]
                if k in POOL_OF:
                    before = turn[st] - BANKS[POOL_OF[k]]
                    if before >= 0:
                        finished(pe, bank_steps[POOL_OF[k]][before])
                    bk = psum(st)
                last = None
                if k == "DT":
                    last = nc.tensor.matmul(bk[0:DT_RANK, :], wx_dt[:, :], xT[:, 512 * st[1]:512 * (st[1] + 1)], start=True, stop=True)
                elif k == "DZ":
                    finished(pe, ("DT", st[1]))
                    last = nc.tensor.matmul(bk[:, :], w_dt[0:DT_RANK, :], xdt[0:DT_RANK, 512 * st[1]:512 * (st[1] + 1)], start=True, stop=True)
                elif k in ("MB", "MC"):
                    w = wBC[:, int(k == "MC"), st[1]:st[1] + 1].to_broadcast([128, 128])
                    last = nc.tensor.matmul(bk[:, :], w, xT[:, 512 * st[2]:512 * (st[2] + 1)], start=True, stop=True)
                elif k == "MY":
                    b = st[1]
                    pe.wait_ge(state_out, b + 1)
                    for t in range(TPB):
                        last = nc.tensor.transpose(bk[:, t * 128:(t + 1) * 128], yacc[:, b * S + t * 128:b * S + (t + 1) * 128], ident[:, :])
                elif k == "XT":
                    _, s, b = st
                    pe.wait_ge(norm_done, count[("NORM", s, b)])
                    for t in range(TPB):
                        last = nc.tensor.transpose(bk[:, t * 128:(t + 1) * 128], x_tok[:, TPB * b + t, :], ident[:, :])
                elif k == "GQ":
                    b = st[1]
                    wait_x(SUB_OF[("attn", GATHERED)], b)
                    last = nc.tensor.matmul(bk[:, 0:S], wA[:, GATHERED, 0, :], xT[:, b * S:(b + 1) * S], start=True, stop=True)
                elif k == "GS":
                    _, b, t = st
                    finished(pe, ("GQ", b))
                    last = nc.tensor.matmul(bk[:, 0:S], gq[:, t * 128:(t + 1) * 128], ctxT[:, b * S:(b + 1) * S], start=True, stop=True)
                elif k == "GT":
                    b = st[1]
                    finished(pe, ("GS", b, TPB - 1))
                    for m in range(TPB):
                        for t in range(TPB):
                            last = nc.tensor.transpose(bk[:, m * S + t * 128:m * S + (t + 1) * 128], one_hot[:, t, m * 128:(m + 1) * 128], ident[:, :])
                elif k == "GM":
                    b = st[1]
                    finished(pe, ("GT", b))
                    pe.wait_ge(ctx_in, 16)
                    for m in range(TPB):
                        last = nc.tensor.matmul(bk[:, 0:S], ctx_tok[:, TPB * b + m, :], one_hotT[:, m, :], start=(m == 0), stop=(m == TPB - 1))
                elif k == "QK":
                    _, a, b = st
                    if unit[(a, b)] == 0:
                        pe.wait_ge(loaded, 16 * N_LOADED0)
                    wait_x(SUB_OF[("attn", a)], b)
                    if a == GATHERED:
                        finished(pe, ("GM", b))
                    for j, x in enumerate((xT[:, b * S:(b + 1) * S], src(a, b))):
                        w = ident[:, :] if a == SELF_WIDE else wA[:, a, j, :]
                        last = nc.tensor.matmul(bk[:, j * S:(j + 1) * S], w, x, start=True, stop=True)
                elif k == "V":
                    _, a, b = st
                    x = src(a, b)
                    for t in range(TPB):
                        last = nc.tensor.matmul(bk[:, t * 128:(t + 1) * 128], x[:, t * 128:(t + 1) * 128], wA[:, a, 2, :], start=True, stop=True)
                elif k == "Z":
                    _, b, i = st
                    pe.wait_ge(wide_in, 16)
                    x = xT[:, b * S + (i // 4) * 128:b * S + (i // 4 + 1) * 128]
                    last = nc.tensor.matmul(bk[:, :], x, wide_w[:, 512 * (i % 4):512 * (i % 4 + 1)], start=True, stop=True)
                elif k == "SM":
                    _, a, b, u = st
                    n, h0, t = unit[(a, b)], 2 * (u // 2), u % 2
                    if u == 0:
                        pe.wait_ge(rows_in[n % 2], 192 * (n // 2 + 1))
                    if u == 0 and a == MASKED:
                        pe.wait_ge(bias_done, b + 1)
                    adds = mask_terms(a, b, 0, t)
                    both = bk[:, :].rearrange("p (h s) -> p h s", h=2)
                    for i, m in enumerate(adds):
                        nc.tensor.matmul(both, identb[:, :], m.unsqueeze(1).to_broadcast([128, 2, S]), start=(i == 0), stop=False, skip_group_check=True)
                    for j in range(2):
                        last = nc.tensor.matmul(bk[:, j * S:(j + 1) * S], QR[:, n % 2, h0 + j, t * 128:(t + 1) * 128], KR[:, n % 2, h0 + j, :],
                                                start=not adds, stop=True, skip_group_check=True)
                elif k == "MT":
                    _, a, b = st
                    n = unit[(a, b)]
                    pe.wait_ge(shift_done, n + 1)
                    for t in range(TPB):
                        last = nc.tensor.matmul(bk[:, t * 128:(t + 1) * 128], ms[:, n % 2, t, :], identb[:, :], start=True, stop=True)
                elif k == "P2":
                    _, a, b, h = st
                    n = unit[(a, b)]
                    if h == 0:
                        finished(pe, ("MT", a, b))
                    whole = bk[:, :].rearrange("p (t s) -> p t s", t=2)
                    nc.tensor.matmul(whole, pick[:, h:h + 1].to_broadcast([128, 128]), msT[:, n % 2, :].unsqueeze(1).to_broadcast([128, 2, S]), start=True, stop=False, skip_group_check=True)
                    for m in mask_terms(a, b, 1, None):
                        nc.tensor.matmul(bk[:, :], identb[:, :], m, start=False, stop=False, skip_group_check=True)
                    for t in range(TPB):
                        last = nc.tensor.matmul(bk[:, t * S:(t + 1) * S], KR[:, n % 2, h, t * 128:(t + 1) * 128], QR[:, n % 2, h, :],
                                                start=False, stop=True, skip_group_check=True)
                elif k == "PV":
                    _, a, b, h = st
                    n, e = unit[(a, b)], count[("P2", a, b, h)]
                    g, j = h // 4, h % 4
                    og_no = count[("OG", a, b, g)]
                    if h == 0:
                        finished(pe, ("V", a, b))
                    if j == 0 and og_no > 1:
                        pe.wait_ge(read["OG"], og_no - 1)
                    pe.wait_ge(read["P2"], e)
                    half = (og_no - 1) % 2
                    for t in range(TPB):
                        last = nc.tensor.matmul(weigh_bank[32 * j:32 * j + 32, half * S:(half + 1) * S], V[:, n % 2, t, h, :],
                                                P[:, (e - 1) % NBUF_P, t * S:(t + 1) * S], start=(t == 0), stop=(t == TPB - 1))
                elif k == "ZV":
                    _, b, h = st
                    n, e = unit[(SELF_WIDE, b)], count[("P2", SELF_WIDE, b, h)]
                    if h == 0:
                        finished(pe, ("Z", b, 7))
                    pe.wait_ge(read["P2"], e)
                    for q in range(TPB):
                        for t in range(TPB):
                            last = nc.tensor.matmul(bk[:, q * S:q * S + D + 1], P[:, (e - 1) % NBUF_P, t * S + q * 128:t * S + (q + 1) * 128],
                                                    Z[:, b % 2, t, h, 0:D + 1], start=(t == 0), stop=(t == TPB - 1))
                elif k == "OT":
                    _, a, b, t = st
                    pe.wait_ge(read["OG"], count[("OG", a, b, 3)])
                    for g in range(4):
                        last = nc.tensor.transpose(bk[:, g * 128:(g + 1) * 128], og[:, unit[(a, b)] % 2, g, t * 128:(t + 1) * 128], ident[:, :])
                elif k == "OX":
                    _, a, b = st
                    finished(pe, ("OT", a, b, TPB - 1))
                    for t in range(TPB):
                        last = nc.tensor.transpose(bk[:, t * 128:(t + 1) * 128], o[:, t, :], ident[:, :])
                elif k == "Y":
                    _, a, b = st
                    finished(pe, ("OX", a, b))
                    for t in range(TPB):
                        last = nc.tensor.matmul(bk[:, t * 128:(t + 1) * 128], oT[:, t * 128:(t + 1) * 128], wA[:, a, 3, :], start=True, stop=True)
                elif k == "GATE":
                    _, m, b = st
                    wait_x(SUB_OF[("moe", m)], b)
                    for t in range(TPB):
                        last = nc.tensor.matmul(bk[:, t * NE:(t + 1) * NE], xT[:, b * S + t * 128:b * S + (t + 1) * 128], gate_w[:, m, :], start=True, stop=True)
                elif k == "RANK":
                    pe.wait_ge(gates_done, count[("GATE", 0, B - 1)])
                    flat = chosen[:, :, :].rearrange("p t e -> p (t e)")
                    nc.tensor.matmul(bk[:, 0:NTT * NE], earlier[:, :], flat, start=True, stop=True)
                    last = nc.tensor.matmul(bk[:, NTT * NE:2 * NTT * NE], ones[:, :], flat, start=True, stop=True)
                elif k == "GB":
                    _, m, c = st
                    pe.wait_ge(gates_done, count[("GATE", m, 2 * c + 1)])
                    for t in range(4):
                        last = nc.tensor.matmul(bk[0:NE, t * 128:(t + 1) * 128], gates[:, 4 * c + t, :], ident[:, :], start=True, stop=True)
                elif k == "BI":
                    _, m, c = st
                    finished(pe, ("GB", m, c))
                    for t in range(4):
                        last = nc.tensor.matmul(bk[:, t * 128:(t + 1) * 128], gT[:, t * 128:(t + 1) * 128], b2[:, m // 2, :], start=True, stop=True)
                elif k in ("MH", "MG"):
                    _, m, c, e, f = st
                    if c == 0 and e == 0 and f == 0:
                        pe.wait_ge(moe_in, 16 * MOE_LOADS[m])
                    w = w1 if k == "MH" else w3
                    last = nc.tensor.matmul(bk[:, :], w[:, e, f * 128:(f + 1) * 128], xT[:, 512 * c:512 * (c + 1)], start=True, stop=True)
                elif k == "MO":
                    _, m, c, e = st
                    nf = MOE_F[m] // 128
                    finished(pe, ("MG" if m == 2 else "MH", m, c, e, nf - 1))
                    for t in range(4):
                        for f in range(nf):
                            last = nc.tensor.matmul(bk[:, t * 128:(t + 1) * 128], hT[:, e % 2, f, t * 128:(t + 1) * 128], w2[:, e, f, :],
                                                    start=(f == 0), stop=(f == nf - 1))
                elif k == "LC":
                    _, w, i = st
                    pe.wait_ge(lin_in, 16 * N_LIN)
                    for h in range(8):
                        last = nc.tensor.matmul(bk[:, h * FD:(h + 1) * FD], lraw_w[64 * i:64 * i + 64, w, h, :], lraw_k[64 * i:64 * i + 64, w, h, :], start=True, stop=True)
                elif k == "LV":
                    _, b, t, half = st
                    last = nc.tensor.matmul(bk[:, :], xT[:, b * S + t * 128:b * S + (t + 1) * 128], lw[:, 2, half * 512:(half + 1) * 512], start=True, stop=True)
                elif k == "LF":
                    _, w, b, t, half = st
                    wait_x(SUB_OF[("linear", 0)], b)
                    finished(pe, ("LC", w, half))
                    last = nc.tensor.matmul(bk[:, :], xT[:, b * S + t * 128:b * S + (t + 1) * 128], lw[:, w, half * 512:(half + 1) * 512], start=True, stop=True)
                elif k == "LT":
                    _, w, b, t, half, i = st
                    pe.wait_ge(lfeat_done, count[("LS", w, b, t, half)])
                    buf = (count[("LF", w, b, t, half)] - 1) % 2
                    for h in range(4):
                        last = nc.tensor.transpose(bk[:, h * 128:(h + 1) * 128], le[:, buf, 4 * i + h].rearrange("p a f -> p (a f)"), ident[:, :])
                elif k == "LA":
                    _, b, h = st
                    finished(pe, ("LT", 1, b, TPB - 1, 1, 1))
                    for t in range(TPB):
                        last = nc.tensor.matmul(bk[:, t * S:(t + 1) * S], featT[:, 1, h, t * 128:(t + 1) * 128], featT[:, 0, h, :], start=True, stop=True)
                elif k == "LO":
                    _, b, g, t = st
                    finished(pe, ("LA", b, 4 * g + 3))
                    finished(pe, ("LV", b, TPB - 1, 1))
                    for j in range(4):
                        h = 4 * g + j
                        for i in range(t + 1):
                            last = nc.tensor.matmul(bk[:, j * 66:j * 66 + HD + 1], P[:, (count[("LA", b, h)] - 1) % NBUF_P, i * S + t * 128:i * S + (t + 1) * 128],
                                                    lv[:, i, h, :], start=(i == 0), stop=(i == t))
                elif k == "LX":
                    _, b, t, i = st
                    finished(pe, ("LO", b, 3, TPB - 1))
                    for j in range(4):
                        last = nc.tensor.transpose(bk[:, j * 128:(j + 1) * 128], lo[:, t, (4 * i + j) * 128:(4 * i + j + 1) * 128], ident[:, :])
                elif k == "LY":
                    b = st[1]
                    finished(pe, ("LX", b, TPB - 1, 1))
                    for t in range(TPB):
                        for j in range(8):
                            last = nc.tensor.matmul(bk[:, t * 128:(t + 1) * 128], loTv(t, j), lw[:, 3, j * 128:(j + 1) * 128], start=(j == 0), stop=(j == 7))
                if last is not None:
                    last.then_inc(filled[k], 1)

        @block.scalar
        def _(act):
            chain = [0]

            def link(ins):
                chain[0] += 1
                ins.then_inc(act_chain, 1)
                act.wait_ge(act_chain, chain[0])

            act.wait_ge(mamba_in, 16 * N_MAMBA)
            link(nc.scalar.activation(negA[:, :], negA[:, :], ACT.Exp))
            link(nc.scalar.mul(negA[:, :], negA[:, :], -1.0))
            for st in steps:
                k = st[0]
                bk = psum(st) if k in POOL_OF else None
                if k == "DT":
                    full(act, st)
                    nc.scalar.activation(xdt[0:DT_RANK, 512 * st[1]:512 * (st[1] + 1)], bk[0:DT_RANK, :], ACT.Identity,
                                         bias=vecs[0:DT_RANK, 2:3]).then_inc(read[k], 1)
                elif k == "DZ":
                    c = slice(512 * st[1], 512 * (st[1] + 1))
                    full(act, st)
                    nc.scalar.activation(zb[:, c], bk[:, :], ACT.Identity, bias=vecs[:, 0:1]).then_inc(read[k], 1)
                    act.wait_ge(read[k], count[st])
                    if st[1]:
                        act.wait_ge(dz_dve, st[1])
                    link(nc.scalar.activation(absz[:, :], zb[:, c], ACT.Abs))
                    link(nc.scalar.activation(absz[:, :], absz[:, :], ACT.Exp, scale=-1.0))
                    nc.scalar.activation(softp[:, :], absz[:, :], ACT.Ln, bias=one_col[:, 0:1]).then_inc(dz_act, 1)
                elif k == "MB":
                    _, n, c = st
                    i = count[st] - 1
                    if i < 2:
                        act.wait_ge(dz_dve, 2)
                    else:
                        act.wait_ge(scan_done, i - 1)
                    nc.scalar.activation(abar[:, i % 2, :], dt[:, 512 * c:512 * (c + 1)], ACT.Exp, scale=negA[:, n:n + 1]).then_inc(abar_done, 1)
                elif k == "XT":
                    _, s, b = st
                    full(act, st)
                    nc.scalar.copy(xT[:, b * S:(b + 1) * S], bk[:, 0:S]).then_inc(read[k], 1)
                elif k == "GQ":
                    full(act, st)
                    if st[1] == 0:
                        full(act, ("LY", B - 1))
                    nc.scalar.copy(gq, bk[:, 0:S]).then_inc(read[k], 1)
                elif k == "GT":
                    full(act, st)
                    nc.scalar.copy(one_hotT.rearrange("p m s -> p (m s)"), bk[:, :]).then_inc(read[k], 1)
                elif k == "GM":
                    b = st[1]
                    full(act, st)
                    nc.scalar.copy(memT[:, b % 2, :], bk[:, 0:S]).then_inc(read[k], 1)
                elif k == "QK":
                    _, a, b = st
                    n = unit[(a, b)]
                    full(act, st)
                    if n == 0:
                        act.wait_ge(loaded, 16 * N_LOADED0)
                    if n >= 2:
                        act.wait_ge(split_done, n - 1)
                    nc.scalar.activation(qk32[:, n % 2, 0, :], bk[:, 0:S], ACT.Identity, bias=bqk[:, a, 0:1])
                    nc.scalar.activation(qk32[:, n % 2, 1, :], bk[:, S:2 * S], ACT.Identity, bias=bqk[:, a, 1:2]).then_inc(read[k], 1)
                elif k == "Z":
                    _, b, i = st
                    full(act, st)
                    if b >= 2:
                        full(act, ("ZV", b - 2, NH - 1))
                    else:
                        act.wait_ge(z_ones, 1)
                    nc.scalar.copy(Z[:, b % 2, i // 4, 4 * (i % 4):4 * (i % 4) + 4, 0:D], bk[:, :].rearrange("p (h d) -> p h d", d=D)).then_inc(read[k], 1)
                elif k == "MT":
                    _, a, b = st
                    n = unit[(a, b)]
                    full(act, st)
                    if n >= 2:
                        full(act, ("P2", units[n - 2][1], units[n - 2][2], NH - 1))
                    nc.scalar.copy(msT[:, n % 2, :], bk[:, 0:S]).then_inc(read[k], 1)
                elif k == "P2":
                    e = count[st]
                    if e > NBUF_P:
                        full(act, weighs(e - 1 - NBUF_P))
                    if st[2:] == (0, 0) and SUBLAYERS[SUB_OF[("attn", st[1])] - 1][0] == "linear":
                        full(act, ("LO", B - 1, 3, TPB - 1))
                    full(act, st)
                    nc.scalar.activation(P[:, (e - 1) % NBUF_P, :], bk[:, :], ACT.Exp, scale=SCALE).then_inc(read[k], 1)
                elif k == "OG":
                    _, a, b, g = st
                    n, half = unit[(a, b)], (count[st] - 1) % 2
                    full(act, ("PV", a, b, 4 * g + 3))
                    if n >= 2 and units[n - 2][1] != SELF_WIDE:
                        full(act, ("OT", units[n - 2][1], units[n - 2][2], TPB - 1))
                    nc.scalar.copy(og[:, n % 2, g, :], weigh_bank[:, half * S:(half + 1) * S]).then_inc(read["OG"], 1)
                elif k == "OX":
                    _, a, b = st
                    full(act, st)
                    if count[st] > 1:
                        act.wait_ge(filled["Y"], count[st] - 1)
                    nc.scalar.copy(oT[:, :], bk[:, 0:S]).then_inc(read[k], 1)
                elif k == "GATE":
                    _, m, b = st
                    act.wait_ge(top_done, count[st])
                    flat = gw[:, :, :].rearrange("p t e -> p (t e)")
                    nc.scalar.activation(gs[:, :, :].rearrange("p t e -> p (t e)"), flat, ACT.Exp,
                                         scale=(-1.0, 0.2, 1.0, 1.0)[m]).then_inc(gate_exp, 1)
                elif k == "GB":
                    full(act, st)
                    nc.scalar.copy(gT[:, :], bk[0:NE, :]).then_inc(read[k], 1)
                elif k == "MH":
                    _, m, c, e, f = st
                    full(act, st)
                    if m == 2:
                        i = count[("MG", m, c, e, f)]
                        if i > 2:
                            act.wait_ge(read["MG"], i - 2)
                        nc.scalar.activation(gated[:, (i - 1) % 2, :], bk[:, :], ACT.Silu).then_inc(read[k], 1)
                    else:
                        if f == 0 and count[("MO", m, c, e)] > 2:
                            act.wait_ge(filled["MO"], count[("MO", m, c, e)] - 2)
                        if m == 0:
                            nc.scalar.activation(hT[:, e % 2, f, :], bk[:, :], ACT.Gelu).then_inc(read[k], 1)
                        else:
                            nc.scalar.activation(hT[:, e % 2, f, :], bk[:, :], ACT.Gelu if m == 1 else ACT.Relu,
                                                 bias=b1[:, m // 2, e, f:f + 1]).then_inc(read[k], 1)
                elif k == "LC":
                    _, w, i = st
                    full(act, st)
                    nc.scalar.copy(lw[:, w, i * 512:(i + 1) * 512], bk[:, :]).then_inc(read[k], 1)
                elif k == "LV":
                    _, b, t, half = st
                    full(act, st)
                    if b == 0 and t == 0 and half == 0:
                        full(act, ("LC", 1, 1))
                    if b:
                        full(act, ("LO", b - 1, 3, TPB - 1))
                    nc.scalar.copy(lv[:, t, 8 * half:8 * half + 8, 0:HD], bk[:, :].rearrange("p (h d) -> p h d", d=HD)).then_inc(read[k], 1)
                elif k == "LF":
                    i = count[st]
                    act.wait_ge(read[k], i)
                    if i > 2:
                        act.wait_ge(filled["LT"], 2 * (i - 2))
                    nc.scalar.activation(le[:, (i - 1) % 2].rearrange("p h a f -> p (h a f)"), lf.rearrange("p h a f -> p (h a f)"), ACT.Exp).then_inc(lexp_done, 1)
                elif k == "LX":
                    _, b, t, i = st
                    full(act, st)
                    if b:
                        full(act, ("LY", b - 1))
                    nc.scalar.copy(loT[:, t, 2 * i:2 * i + 2, :].rearrange("p a b -> p (a b)"), bk[:, :]).then_inc(read[k], 1)

        @block.gpsimd
        def _(pool):
            chain = [0]

            def link(ins):
                chain[0] += 1
                ins.then_inc(pool_chain, 1)
                pool.wait_ge(pool_chain, chain[0])

            for m in (ident, identb):
                link(nc.gpsimd.memset(m[:, :], 0.0))
                link(nc.gpsimd.affine_select(out=m[:, :], in_=m[:, :], compare_op=ALU.not_equal, fill=1.0, base=0, pattern=[[-1, 128]], channel_multiplier=1))
            nc.gpsimd.memset(ones[:, :], 1.0).then_inc(pool_chain, 1)
            nc.gpsimd.memset(one_col[:, :], 1.0).then_inc(pool_chain, 1)
            chain[0] += 2
            link(nc.gpsimd.memset(minus_half[:, :], -0.5))
            link(nc.gpsimd.memset(earlier[:, :], 1.0))
            link(nc.gpsimd.affine_select(out=earlier[:, :], in_=earlier[:, :], compare_op=ALU.is_ge, fill=0.0, base=-1, pattern=[[1, 128]], channel_multiplier=-1))
            link(nc.gpsimd.memset(pick[:, :], 0.0))
            for part in range(2):
                link(nc.gpsimd.affine_select(out=pick[:, :], in_=pick[:, :], compare_op=ALU.not_equal, fill=1.0, base=-NH * part,
                                             pattern=[[-1, NH]], channel_multiplier=1))
            link(nc.gpsimd.memset(causal_q[:, :, :], 0.0))
            link(nc.gpsimd.affine_select(out=causal_q[:, :, :], in_=causal_q[:, :, :], compare_op=ALU.is_ge, fill=NEG, base=0,
                                         pattern=[[128, TPB], [-1, S]], channel_multiplier=1))
            link(nc.gpsimd.memset(causal_k[:, :, :], 0.0))
            link(nc.gpsimd.affine_select(out=causal_k[:, :, :], in_=causal_k[:, :, :], compare_op=ALU.is_ge, fill=NEG, base=0,
                                         pattern=[[-128, TPB], [1, S]], channel_multiplier=-1))
            keep = keep_past[:, :].rearrange("p (t s) -> p t s", t=TPB)
            link(nc.gpsimd.memset(keep_past[:, :], 1.0))
            link(nc.gpsimd.affine_select(out=keep, in_=keep, compare_op=ALU.is_ge, fill=0.0, base=0,
                                         pattern=[[-128, TPB], [1, S]], channel_multiplier=-1))
            link(nc.gpsimd.iota(iota_i[:, :], pattern=[[1, S]], base=0, channel_multiplier=0))
            nc.gpsimd.tensor_copy(iota[:, :], iota_i[:, :]).then_inc(consts_pool, 1)
            for st in steps:
                k = st[0]
                if k == "MC":
                    _, n, c = st
                    i = count[st]
                    part = yacc[:, 512 * c:512 * (c + 1)]
                    finished(pool, st)
                    if n == 0:
                        nc.gpsimd.tensor_copy(part, gc[:, (i - 1) % 2, :]).then_inc(yacc_done, 1)
                    else:
                        pool.wait_ge(yacc_done, i - 1)
                        nc.gpsimd.tensor_tensor(part, part, gc[:, (i - 1) % 2, :], ALU.add).then_inc(yacc_done, 1)
                elif k in ("STAT", "STAT2"):
                    _, s, b = st
                    no = stat_no[st]
                    rms = k == "STAT" and SUBLAYERS[s] in (("attn", 1), ("moe", 0))
                    pool.wait_ge(stat_done, no)
                    link(nc.gpsimd.tensor_scalar(rstd[:, b % 2, :], mv[:, b % 2, :, 1], RMS_EPS if rms else LN_EPS, None, ALU.add))
                    nc.gpsimd.tensor_tensor(rstd[:, b % 2, :], rstd[:, b % 2, :], minus_half[:, :], ALU.pow).then_inc(rstd_done, 1)
                elif k == "SPLIT":
                    _, a, b = st
                    n = unit[(a, b)]
                    finished(pool, ("QK", a, b))
                    if n >= 2:
                        pool.wait_ge(parts_stored, 16 * (n - 1))
                    x, hi, mid, low = qk32[:, n % 2], parts[:, n % 2, :, 0, :], parts[:, n % 2, :, 1, :], parts[:, n % 2, :, 2, :]
                    link(nc.gpsimd.tensor_copy(hi, x))
                    link(nc.gpsimd.tensor_tensor(rem[:, :, :], x, hi, ALU.subtract))
                    link(nc.gpsimd.tensor_copy(mid, rem[:, :, :]))
                    nc.gpsimd.tensor_tensor(low, rem[:, :, :], mid, ALU.subtract).then_inc(split_done, 1)
                elif k == "BIAS":
                    b = st[1]
                    pool.wait_ge(bias_sum, b + 1)
                    if b >= 2:
                        full(pool, ("P2", MASKED, b - 2, NH - 1))
                    hi, mid, low = (bias_parts[:, b % 2, i] for i in range(3))
                    link(nc.gpsimd.tensor_copy(hi, biasf))
                    link(nc.gpsimd.tensor_tensor(biasr, biasf, hi, ALU.subtract))
                    link(nc.gpsimd.tensor_copy(mid, biasr))
                    nc.gpsimd.tensor_tensor(low, biasr, mid, ALU.subtract).then_inc(bias_done, 1)
                elif st == ("QK", SELF_WIDE, 0):
                    full(pool, ("MO", 0, 1, NE - 1))
                    nc.gpsimd.memset(Z[:, :, :, :, D:D + 1].rearrange("p b t h o -> p (b t h o)"), 1.0).then_inc(z_ones, 1)
                elif k == "LS":
                    i = count[st]
                    pool.wait_ge(lsum_done, i)
                    x = le[:, (i - 1) % 2].rearrange("p h a f -> p (h a) f")
                    nc.gpsimd.tensor_tensor(x, x, lden_v.unsqueeze(2).to_broadcast([128, 16, FD]), ALU.mult).then_inc(lfeat_done, 1)
                elif st == ("LC", 1, 1):
                    full(pool, st)
                    nc.gpsimd.memset(lv[:, :, :, HD:HD + 1].rearrange("p t h o -> p (t h o)"), 1.0).then_inc(z_ones, 1)

        @block.vector
        def _(dve):
            chain = [0]

            def link(ins):
                chain[0] += 1
                ins.then_inc(dve_chain, 1)
                dve.wait_ge(dve_chain, chain[0])

            V_ = nc.vector
            link(V_.memset(QR[:, :, :, :], 0.0))
            link(V_.memset(V[:, :, :, :, :], 0.0))
            link(V_.memset(V[:, :, :, :, DH:DH + 1], 1.0))
            link(V_.memset(ms[:, :, :, :], 0.0))
            V_.memset(KR[:, :, :, :], 0.0).then_inc(consts, 1)
            dve.wait_ge(consts, 1)
            dve.wait_ge(mamba_in, 16 * N_MAMBA)

            def statistics(src, b, rms):
                for t in range(TPB):
                    V_.bn_stats(stats[:, t, :], src[:, t, :]).then_inc(dve_chain, 1)
                chain[0] += TPB
                dve.wait_ge(dve_chain, chain[0])
                for t in range(TPB):
                    last = V_.bn_aggr(mv[:, b % 2, t, :], stats[:, t, :])
                    if rms or t < TPB - 1:
                        last.then_inc(dve_chain, 1)
                        chain[0] += 1
                if rms:
                    dve.wait_ge(dve_chain, chain[0])
                    for t in range(TPB):
                        last = V_.scalar_tensor_tensor(out=mv[:, b % 2, t, 1:2], in0=mv[:, b % 2, t, 0:1], scalar=mv[:, b % 2, t, 0:1],
                                                       in1=mv[:, b % 2, t, 1:2], op0=ALU.mult, op1=ALU.add)
                        if t < TPB - 1:
                            last.then_inc(dve_chain, 1)
                            chain[0] += 1
                last.then_inc(stat_done, 1)

            for st in steps:
                k = st[0]
                bk = psum(st) if k in POOL_OF else None
                if k == "DZ":
                    c = slice(512 * st[1], 512 * (st[1] + 1))
                    dve.wait_ge(dz_act, st[1] + 1)
                    link(V_.scalar_tensor_tensor(out=dt[:, c], in0=zb[:, c], scalar=0.0, in1=softp, op0=ALU.max, op1=ALU.add))
                    V_.tensor_tensor(dtu[:, c], dt[:, c], xT[:, c], ALU.mult).then_inc(dz_dve, 1)
                    dve.wait_ge(dz_dve, st[1] + 1)
                elif k == "MB":
                    _, n, c = st
                    i = count[st]
                    full(dve, st)
                    V_.scalar_tensor_tensor(out=bu[:, (i - 1) % 2, :], in0=bk[:, :], scalar=bBC[:, 0, n:n + 1], in1=dtu[:, 512 * c:512 * (c + 1)],
                                            op0=ALU.add, op1=ALU.mult).then_inc(read[k], 1)
                    dve.wait_ge(read[k], i)
                    dve.wait_ge(abar_done, i)
                    for b in range(2):
                        part = slice(b * S, (b + 1) * S)
                        last = V_.tensor_tensor_scan(hs[:, (i - 1) % 2, part], abar[:, (i - 1) % 2, part], bu[:, (i - 1) % 2, part], 0.0, ALU.mult, ALU.add)
                        if b == 0:
                            last.then_inc(dve_chain, 1)
                            chain[0] += 1
                    last.then_inc(scan_done, 1)
                elif k == "MC":
                    _, n, c = st
                    i = count[st]
                    full(dve, st)
                    dve.wait_ge(scan_done, i)
                    dve.wait_ge(dve_chain, chain[0])
                    if i > 2:
                        dve.wait_ge(yacc_done, i - 2)
                    V_.scalar_tensor_tensor(out=gc[:, (i - 1) % 2, :], in0=bk[:, :], scalar=bBC[:, 1, n:n + 1], in1=hs[:, (i - 1) % 2, :],
                                            op0=ALU.add, op1=ALU.mult).then_inc(read[k], 1)
                elif k == "MY":
                    b = st[1]
                    c = slice(b * S, (b + 1) * S)
                    if b == 0:
                        dve.wait_ge(yacc_done, 2 * NSTATE)
                    link(V_.scalar_tensor_tensor(out=yacc[:, c], in0=xT[:, c], scalar=vecs[:, 1:2], in1=yacc[:, c], op0=ALU.mult, op1=ALU.add))
                    V_.tensor_tensor(yacc[:, c], yacc[:, c], xT[:, c], ALU.add).then_inc(state_out, 1)
                elif k == "STAT":
                    _, s, b = st
                    kind, a = SUBLAYERS[s]
                    r, x = res[:, b % 2], x_tok[:, TPB * b:TPB * (b + 1), :]
                    if kind == "mamba":
                        src = ("MY", b)
                    elif kind == "linear":
                        src = ("LY", b)
                    elif kind == "attn" and a != SELF_WIDE:
                        src = ("Y", a, b)
                    else:
                        src = None
                    if src:
                        full(dve, src)
                        y = psum(src)[:, 0:S].rearrange("p (t d) -> p t d", t=TPB)
                        if kind == "mamba":
                            V_.tensor_copy(r, y).then_inc(read[src[0]], 1)
                        else:
                            V_.tensor_tensor(r, y, x, ALU.add).then_inc(read[src[0]], 1)
                        finished(dve, src)
                        if kind == "attn" and a not in (3, GATHERED):
                            link(V_.tensor_tensor(r, r, bvo[:, a, 1:2, :].to_broadcast([128, TPB, D]), ALU.add))
                    else:
                        y = acc[:, (b % 2) * TPB:(b % 2 + 1) * TPB, :]
                        link(V_.tensor_tensor(r, y, x, ALU.add))
                    statistics(r, b, (kind, a) in (("attn", 1), ("moe", 0)))
                elif k == "STAT2":
                    _, s, b = st
                    dve.wait_ge(rstd_done, stat_no[("STAT", s, b)])
                    for t in range(TPB):
                        link(V_.scalar_tensor_tensor(out=res[:, b % 2, t, :], in0=res[:, b % 2, t, :], scalar=rstd[:, b % 2, t:t + 1], in1=norm_w[:, 1, :],
                                                     op0=ALU.mult, op1=ALU.mult))
                    link(V_.tensor_tensor(res[:, b % 2], res[:, b % 2], x_before[:, TPB * b:TPB * (b + 1), :], ALU.add))
                    statistics(res[:, b % 2], b, False)
                elif k == "NORM":
                    _, s, b = st
                    dve.wait_ge(rstd_done, stat_no[("STAT2" if SUBLAYERS[s] == ("moe", 0) else "STAT", s, b)])
                    if SUBLAYERS[s] == ("attn", 1):
                        link(V_.tensor_copy(x_before[:, TPB * b:TPB * (b + 1), :], x_tok[:, TPB * b:TPB * (b + 1), :]))
                    for t in range(TPB):
                        x, r = x_tok[:, TPB * b + t, :], res[:, b % 2, t, :]
                        if SUBLAYERS[s] == ("attn", 1):
                            last = V_.scalar_tensor_tensor(out=x, in0=r, scalar=rstd[:, b % 2, t:t + 1], in1=norm_w[:, 0, :], op0=ALU.mult, op1=ALU.mult)
                        else:
                            last = V_.tensor_scalar(x, r, mv[:, b % 2, t, 0:1], rstd[:, b % 2, t:t + 1], ALU.subtract, ALU.mult)
                        if t < TPB - 1:
                            last.then_inc(dve_chain, 1)
                            chain[0] += 1
                    last.then_inc(norm_done, 1)
                    dve.wait_ge(norm_done, count[st])
                    dve.wait_ge(dve_chain, chain[0])
                elif k == "V":
                    _, a, b = st
                    n = unit[(a, b)]
                    full(dve, st)
                    if n >= 2 and units[n - 2][1] != SELF_WIDE:
                        full(dve, ("PV", units[n - 2][1], units[n - 2][2], NH - 1))
                    for t in range(TPB):
                        last = V_.tensor_tensor(V[:, n % 2, t, :, 0:DH], bk[:, t * 128:(t + 1) * 128].rearrange("p (h d) -> p h d", d=DH),
                                                bvo[:, a, 0, :].rearrange("p (h d) -> p h d", d=DH), ALU.add)
                    last.then_inc(read[k], 1)
                elif k == "SM":
                    _, a, b, u = st
                    full(dve, st)
                    V_.reduce_max(mx[:, unit[(a, b)] % 2, u % 2, 2 * (u // 2):2 * (u // 2) + 2],
                                  bk[:, :].rearrange("p (h s) -> p h s", h=2), AX.X).then_inc(read[k], 1)
                elif k == "MS":
                    _, a, b = st
                    n = unit[(a, b)]
                    finished(dve, ("SM", a, b, 15))
                    if n >= 2:
                        full(dve, ("MT", units[n - 2][1], units[n - 2][2]))
                    hi, low = ms[:, n % 2, :, 0:NH], ms[:, n % 2, :, NH:2 * NH]
                    link(V_.tensor_scalar(hi, mx[:, n % 2], -1.0, None, ALU.mult))
                    V_.scalar_tensor_tensor(out=low, in0=mx[:, n % 2], scalar=-1.0, in1=hi, op0=ALU.mult, op1=ALU.subtract).then_inc(shift_done, 1)
                elif k == "ZV":
                    _, b, h = st
                    full(dve, st)
                    y = bk[:, :].rearrange("p (t s) -> p t s", t=TPB)
                    link(V_.reciprocal(rden[:, :, 0:1], y[:, :, D:D + 1]))
                    for t in range(TPB):
                        to = acc[:, (b % 2) * TPB + t, :]
                        if h == 0:
                            last = V_.tensor_scalar(to, y[:, t, 0:D], rden[:, t, 0:1], None, ALU.mult)
                        else:
                            last = V_.scalar_tensor_tensor(out=to, in0=y[:, t, 0:D], scalar=rden[:, t, 0:1], in1=to, op0=ALU.mult, op1=ALU.add)
                        if t < TPB - 1:
                            last.then_inc(dve_chain, 1)
                            chain[0] += 1
                    last.then_inc(read[k], 1)
                    dve.wait_ge(dve_chain, chain[0])
                    dve.wait_ge(read[k], count[st])
                elif k == "OT":
                    _, a, b, t = st
                    full(dve, st)
                    y = bk[:, :].rearrange("p (h c) -> p h c", c=32)
                    link(V_.reciprocal(rden[:, t, :].unsqueeze(2), y[:, :, DH:DH + 1]))
                    i = count[("OX", a, b)]
                    if i > 1:
                        dve.wait_ge(filled["OX"], i - 1)
                    V_.tensor_tensor(o[:, t, :].rearrange("p (h d) -> p h d", d=DH), y[:, :, 0:DH],
                                     rden[:, t, :].unsqueeze(2).to_broadcast([128, NH, DH]), ALU.mult).then_inc(read[k], 1)
                elif k == "GS":
                    _, b, t = st
                    full(dve, st)
                    if t == 0 and b:
                        full(dve, ("GT", b - 1))
                    link(V_.max(top[:, 0, :], bk[:, 0:S]))
                    link(V_.max_index(top_at[:, 0, :], top[:, 0, :], bk[:, 0:S]))
                    link(V_.tensor_copy(top_atf[:, 0, :], top_at[:, 0, :]))
                    V_.tensor_scalar(one_hot[:, t, :], iota[:, :], top_atf[:, 0, 0:1], None, ALU.is_equal).then_inc(read[k], 1)
                elif k == "BIAS":
                    b = st[1]
                    if b == 0:
                        dve.wait_ge(mask_in, 48)
                    if b >= 2:
                        dve.wait_ge(mask_more[b - 2], 16)
                    if b:
                        dve.wait_ge(bias_done, b)
                    link(V_.tensor_scalar(biasf, mask[:, b % 2], 0.0, NEG, ALU.is_equal, ALU.mult))
                    V_.scalar_tensor_tensor(out=biasf, in0=adj, scalar=1.0 / SCALE, in1=biasf, op0=ALU.mult, op1=ALU.add).then_inc(bias_sum, 1)
                elif k == "GATE":
                    _, m, b = st
                    full(dve, st)
                    lg = bk[:, 0:TPB * NE].rearrange("p (t e) -> p t e", e=NE)
                    V_.tensor_tensor(logits[:, :, :], lg, gate_b[:, m:m + 1, :].to_broadcast([128, TPB, NE]), ALU.add).then_inc(read[k], 1)
                    finished(dve, st)
                    for t in range(TPB):
                        link(V_.max(top[:, t, :], logits[:, t, :]))
                    for t in range(TPB):
                        link(V_.max_index(top_at[:, t, :], top[:, t, :], logits[:, t, :]))
                    link(V_.tensor_copy(top_atf[:, :, :], top_at[:, :, :]))
                    if m == 0:
                        V_.tensor_copy(gw[:, :, :], top[:, :, :]).then_inc(top_done, 1)
                    else:
                        V_.tensor_tensor(gw[:, :, :], top[:, :, :], top[:, :, 0:1].to_broadcast([128, TPB, 8]), ALU.subtract).then_inc(top_done, 1)
                    dve.wait_ge(gate_exp, count[st])
                    if m == 0:
                        link(V_.tensor_scalar(gs[:, :, :], gs[:, :, :], 1.0, None, ALU.add))
                        link(V_.reciprocal(gs[:, :, :], gs[:, :, :]))
                    link(V_.tensor_tensor(gden[:, :, :], gs[:, :, 0:1], gs[:, :, 1:2], ALU.add))
                    if m == 0:
                        link(V_.tensor_scalar(gden[:, :, :], gden[:, :, :], 1e-6, None, ALU.add))
                    if m == 1:
                        link(V_.reduce_sum(gz[:, :, :], gs[:, :, :], AX.X))
                        link(V_.scalar_tensor_tensor(out=gden[:, :, :], in0=gz[:, :, :], scalar=1e-9, in1=gden[:, :, :], op0=ALU.mult, op1=ALU.add))
                    link(V_.reciprocal(gden[:, :, :], gden[:, :, :]))
                    link(V_.tensor_tensor(gs[:, :, :], gs[:, :, :], gden[:, :, :].to_broadcast([128, TPB, 8]), ALU.mult))
                    for t in range(TPB):
                        g = gates[:, TPB * b + t, :]
                        link(V_.tensor_scalar(g, iota[:, 0:NE], top_atf[:, t, 0:1], gs[:, t, 0:1], ALU.is_equal, ALU.mult))
                        link(V_.tensor_scalar(gtmp[:, :], iota[:, 0:NE], top_atf[:, t, 1:2], gs[:, t, 1:2], ALU.is_equal, ALU.mult))
                        link(V_.tensor_tensor(g, g, gtmp[:, :], ALU.add))
                        if m == 0:
                            ch = chosen[:, TPB * b + t, :]
                            link(V_.tensor_scalar(ch, iota[:, 0:NE], top_atf[:, t, 0:1], None, ALU.is_equal))
                            link(V_.scalar_tensor_tensor(out=ch, in0=iota[:, 0:NE], scalar=top_atf[:, t, 1:2], in1=ch, op0=ALU.is_equal, op1=ALU.add))
                    V_.tensor_copy(gtmp[:, :], gtmp[:, :]).then_inc(gates_done, 1)
                    dve.wait_ge(gates_done, count[st])
                elif k == "RANK":
                    full(dve, st)
                    sums = bk[:, NTT * NE:2 * NTT * NE].rearrange("p (t e) -> p t e", e=NE)
                    link(V_.memset(prefix[:, 0, :], 0.0))
                    for t in range(1, NTT):
                        link(V_.tensor_tensor(prefix[:, t, :], sums[:, t - 1, :], prefix[:, t - 1, :], ALU.add))
                    V_.tensor_tensor(prefix[:, :, :], bk[:, 0:NTT * NE].rearrange("p (t e) -> p t e", e=NE), prefix[:, :, :], ALU.add).then_inc(read[k], 1)
                    finished(dve, st)
                    link(V_.scalar_tensor_tensor(out=gates[:, :, :], in0=prefix[:, :, :], scalar=float(CAPACITY), in1=gates[:, :, :], op0=ALU.is_lt, op1=ALU.mult))
                elif k == "BI":
                    full(dve, st)
                    V_.tensor_copy(acc[:, :, :], bk[:, :].rearrange("p (t d) -> p t d", d=D)).then_inc(read[k], 1)
                    finished(dve, st)
                elif k == "MG":
                    _, m, c, e, f = st
                    full(dve, st)
                    finished(dve, ("MH", m, c, e, f))
                    if f == 0 and count[("MO", m, c, e)] > 2:
                        dve.wait_ge(filled["MO"], count[("MO", m, c, e)] - 2)
                    V_.tensor_tensor(hT[:, e % 2, f, :], bk[:, :], gated[:, (count[st] - 1) % 2, :], ALU.mult).then_inc(read[k], 1)
                elif k == "MO":
                    _, m, c, e = st
                    full(dve, st)
                    for t in range(4):
                        g = gates[:, 4 * c + t, e:e + 1]
                        y = bk[:, t * 128:(t + 1) * 128]
                        if e == 0 and m in (0, 2):
                            last = V_.tensor_scalar(acc[:, t, :], y, g, None, ALU.mult)
                        else:
                            last = V_.scalar_tensor_tensor(out=acc[:, t, :], in0=y, scalar=g, in1=acc[:, t, :], op0=ALU.mult, op1=ALU.add)
                        if t < 3:
                            last.then_inc(dve_chain, 1)
                            chain[0] += 1
                    last.then_inc(read[k], 1)
                    finished(dve, st)
                    dve.wait_ge(dve_chain, chain[0])
                elif k == "LF":
                    i = count[st]
                    full(dve, st)
                    f = bk[:, :].rearrange("p (h f) -> p h f", f=FD)
                    link(V_.reduce_max(lmax_v[:, 0, :], f, AX.X))
                    link(V_.tensor_reduce(lmax_v[:, 1, :], f, AX.X, ALU.min))
                    if i > 1:
                        dve.wait_ge(lexp_done, i - 1)
                    link(V_.tensor_tensor(lf[:, :, 0, :], f, lmax_v[:, 0, :].unsqueeze(2).to_broadcast([128, 8, FD]), ALU.subtract))
                    V_.scalar_tensor_tensor(out=lf[:, :, 1, :], in0=f, scalar=-1.0, in1=lmax_v[:, 1, :].unsqueeze(2).to_broadcast([128, 8, FD]),
                                            op0=ALU.mult, op1=ALU.add).then_inc(read[k], 1)
                elif k == "LS":
                    i = count[st]
                    dve.wait_ge(lexp_done, i)
                    if i > 1:
                        dve.wait_ge(lfeat_done, i - 1)
                    link(V_.reduce_sum(lden_v, le[:, (i - 1) % 2].rearrange("p h a f -> p (h a) f"), AX.X))
                    V_.reciprocal(lden_v, lden_v).then_inc(lsum_done, 1)
                elif k == "LT":
                    _, w, b, t, half, i = st
                    full(dve, st)
                    if b:
                        full(dve, ("LA", b - 1, NH - 1))
                    h = 8 * half + 4 * i
                    V_.tensor_scalar(featT[:, w, h:h + 4, t * 128:(t + 1) * 128], bk[:, :].rearrange("p (h s) -> p h s", h=4), 1e-12, None, ALU.max).then_inc(read[k], 1)
                elif k == "LA":
                    _, b, h = st
                    i = count[st]
                    full(dve, st)
                    if i > 4:
                        dve.wait_ge(filled["LO"], 2 * ((i - 5) // 4 + 1))
                    V_.tensor_tensor(P[:, (i - 1) % NBUF_P, :], bk[:, :], keep_past[:, :], ALU.mult).then_inc(read[k], 1)
                elif k == "LO":
                    _, b, g, t = st
                    full(dve, st)
                    if g == 0 and b:
                        full(dve, ("LX", b - 1, TPB - 1, 1))
                    y = bk[:, 0:4 * 66].rearrange("p (h c) -> p h c", c=66)
                    link(V_.tensor_scalar(rden[:, 0, 0:4].unsqueeze(2), y[:, :, HD:HD + 1], 1e-12, None, ALU.add))
                    link(V_.reciprocal(rden[:, 0, 0:4], rden[:, 0, 0:4]))
                    V_.tensor_tensor(lo[:, t, 4 * g * HD:4 * (g + 1) * HD].rearrange("p (h d) -> p h d", d=HD), y[:, :, 0:HD],
                                     rden[:, 0, 0:4].unsqueeze(2).to_broadcast([128, 4, HD]), ALU.mult).then_inc(read[k], 1)
                    finished(dve, st)


def kernel(**inputs):
    import numpy as np
    import concourse.bacc as bacc
    from concourse.bass_utils import run_bass_kernel_spmd as run

    w = {k: np.asarray(v) for k, v in inputs.items()}
    f32 = np.float32
    zero = np.zeros((D,), f32)
    zero2 = np.zeros((D, D), f32)

    def tokens(a):
        return a.reshape(NTT, 128, D).transpose(1, 0, 2)

    def all_heads(a, n):
        return np.repeat(a.reshape(a.shape[:-1] + (n, DH)), NH // n, axis=-2).reshape(a.shape[:-1] + (D,))

    g = "L0_ffn_"
    wkv = w["L3_xattn_Wkv"]
    qkv = w["L2_attn_w_qkv"]
    attn = [
        [w["L0_xattn_W" + c].T for c in "qkvo"],
        [w[g + "qw"], all_heads(w[g + "kw"], 4), all_heads(w[g + "vw"], 4), w[g + "ow"]],
        [zero2] * 4,
        [w["L1_xattn_w_" + c].T for c in "qkvo"],
        [qkv[:, 0:D], qkv[:, D:2 * D], qkv[:, 2 * D:3 * D], w["L2_attn_w_out"]],
        [w["L2_xattn_W" + c].T for c in "qkvo"],
        [w["L3_xattn_Wq"].T, all_heads(wkv[0:DH].T, 1), all_heads(wkv[DH:2 * DH].T, 1), w["L3_xattn_Wc"].T],
    ]
    bq = w["L2_attn_b_qkv"]
    bias = [
        [w["L0_xattn_b" + c] for c in "qkvo"],
        [w[g + "qb"], all_heads(w[g + "kb"], 4), all_heads(w[g + "vb"], 4), w[g + "ob"]],
        [zero] * 4,
        [zero] * 4,
        [bq[0:D], bq[D:2 * D], bq[2 * D:3 * D], w["L2_attn_b_out"]],
        [w["L2_xattn_b" + c] for c in "qkvo"],
        [zero] * 4,
    ]
    bias = np.stack([np.stack(x) for x in bias])
    mask = w["mask_Bx1xSxS2_ik1"][:, 0]
    adj = w["L2_xattn_adj"]

    def both_ways(a):
        pair = np.stack([a, np.swapaxes(a, -1, -2)], axis=-3)
        pair = pair.reshape(pair.shape[:-2] + (TPB, 128, S))
        return np.moveaxis(pair, -2, 0).reshape((128,) + pair.shape[:-3] + (TPB * S,))

    lin = "L3_attn_"
    lin_w = np.stack([w[lin + c].T.reshape(NH, HD, D).transpose(1, 0, 2) for c in ("Wq", "Wk")], axis=1)
    lin_k = np.stack([w[lin + c].transpose(1, 0, 2) for c in ("Kq", "Kk")], axis=1)
    wide = w["L1_attn_weight"].reshape(NH, D, D).transpose(1, 0, 2).reshape(D, NH * D)

    def up(a):
        return a.transpose(1, 0, 2)

    def down(a):
        return a.reshape(NE, -1, 128, D).transpose(2, 0, 1, 3)

    def rows(a):
        return np.broadcast_to(a[None], (128,) + a.shape)

    zero8 = np.zeros((NE,), f32)
    arrays = {
        "xT": w["x"].reshape(NT, D).T, "x": tokens(w["x"]),
        "ctxT": w["ctx_1024"].reshape(NT, D).T, "ctx": tokens(w["ctx_1024"]),
        "w_xdt": w["L0_attn_W_xdt"].T, "w_dt": w["L0_attn_W_dt"].T,
        "w_BC": np.stack([w["L0_attn_W_B"].T, w["L0_attn_W_C"].T], axis=1),
        "A_log": w["L0_attn_A_log"], "b_BC": rows(np.stack([w["L0_attn_b_B"], w["L0_attn_b_C"]])),
        "dt_D": np.stack([w["L0_attn_b_dt"], w["L0_attn_D"]], axis=1), "b_xdt": w["L0_attn_b_xdt"][:, None],
        "w_attn": np.stack([np.stack(x) for x in attn]).transpose(2, 0, 1, 3),
        "b_qk": bias[:, 0:2].transpose(2, 0, 1), "b_vo": rows(bias[:, 2:4]),
        "gate_w": np.stack([w[g + "gate_w"], w["L1_ffn_Wg"], w["L2_ffn_gate_w"].T, w["L3_ffn_Wr"]], axis=1),
        "gate_b": rows(np.stack([zero8, w["L1_ffn_bg"], zero8, w["L3_ffn_br"]])),
        "b1": np.stack([w["L1_ffn_b1"], w["L3_ffn_b1"]]).reshape(2, NE, 2, 128).transpose(3, 0, 1, 2),
        "b2": np.stack([w["L1_ffn_b2"], w["L3_ffn_b2"]], axis=1),
        "norm_w": rows(np.stack([w[g + "norm1_w"], w[g + "norm2_w"]])),
        "wide_w": wide,
        "w1_0": up(w[g + "w1"]), "w2_0": down(w[g + "w2"]),
        "w1_1": up(w["L1_ffn_W1"]), "w2_1": down(w["L1_ffn_W2"]),
        "w1_2": w["L2_ffn_w1"].transpose(2, 0, 1), "w3_2": w["L2_ffn_w3"].transpose(2, 0, 1),
        "w2_2": down(w["L2_ffn_w2"].transpose(0, 2, 1)),
        "w1_3": up(w["L3_ffn_W1"]), "w2_3": down(w["L3_ffn_W2"]),
        **{f"mask{b}": both_ways(mask[b]) for b in range(B)}, "adj": both_ways(adj),
        "lin_v": w[lin + "Wv"], "lin_o": w[lin + "Wo"].reshape(8, 128, D).transpose(1, 0, 2).reshape(128, 8 * D),
        "lin_w0": lin_w[:, :, 0:8], "lin_w1": lin_w[:, :, 8:16], "lin_k0": lin_k[:, :, 0:8], "lin_k1": lin_k[:, :, 8:16],
    }
    arrays = {k: np.ascontiguousarray(v) for k, v in arrays.items()}
    nc = bacc.Bacc("TRN2", target_bir_lowering=False, num_devices=1)
    ins = {k: nc.dram_tensor(f"in_{k}", a.shape, mybir.dt.from_np(a.dtype), kind="ExternalInput").ap() for k, a in arrays.items()}
    scratch = nc.dram_tensor("split_parts", (2, 2, 3, 128, S), mybir.dt.bfloat16, kind="Internal").ap()
    out = nc.dram_tensor("out", (B, S, D), mybir.dt.float32, kind="ExternalOutput").ap()
    decoder(nc, ins, scratch, out)
    r = run(nc, [{f"in_{k}": a for k, a in arrays.items()}], core_ids=[0])
    return r.results[0]["out"]
```

```python
from contextlib import ExitStack

import concourse.bass as bass
from concourse import mybir

B, S, D = 4, 256, 128
NH, DH = 16, 8
NT = B * S
TPB = S // 128
NTT = NT // 128
NE = 8
SCALE = float(DH) ** -0.5
NEG = -1e30
CAPACITY = int(1.25 * NT * 2 / NE)
LN_EPS = 1e-5
RMS_EPS = 1e-6
NSTATE, DT_RANK = 16, 64
HD, FD = 64, 64
PART_RUNS = ((0, 3, 0, 0), (3, 2, 0, 1), (5, 1, 0, 2))
NBUF_P = 4

CROSS = (0, 3, 5)
SELF_WIDE = 2
CAUSAL = 4
MASKED = 5
GATHERED = 6
SUBLAYERS = [("mamba", 0), ("attn", 0), ("attn", 1), ("moe", 0), ("attn", 2), ("attn", 3), ("moe", 1),
             ("attn", 4), ("attn", 5), ("moe", 2), ("linear", 0), ("attn", 6), ("moe", 3)]
SUB_OF = {x: s for s, x in enumerate(SUBLAYERS)}
LAST = len(SUBLAYERS) - 1
MOE_F = (256, 256, 512, 256)


def finish_steps(s, b):
    steps = [("STAT", s, b)]
    if SUBLAYERS[s] == ("moe", 0):
        steps.append(("STAT2", s, b))
    steps.append(("NORM", s, b))
    if s != LAST:
        steps.append(("XT", s, b))
    return steps


def spread(main, side):
    out, n = [], len(main)
    for i, steps in enumerate(main):
        out += steps
        out += side[i * len(side) // n:(i + 1) * len(side) // n]
    return out


def gates_after(s, b):
    return [("GATE", SUBLAYERS[s + 1][1], b)] if s < LAST and SUBLAYERS[s + 1][0] == "moe" else []


def finish(s, b):
    return finish_steps(s, b) + gates_after(s, b)


def project(a, b):
    steps = []
    if a == GATHERED:
        steps += [("GQ", b)] + [("GS", b, t) for t in range(TPB)] + [("GT", b), ("GM", b)]
    return steps + [("QK", a, b), ("SPLIT", a, b)]


def values(a, b):
    return [("Z", b, i) for i in range(8)] if a == SELF_WIDE else [("V", a, b)]


def maxima(a, b):
    steps = [("BIAS", b)] if a == MASKED else []
    return steps + [("SM", a, b, u) for u in range(16)] + [("MS", a, b), ("MT", a, b)]


def attention_tail(a, b):
    steps = []
    if a != SELF_WIDE:
        steps += [("OT", a, b, t) for t in range(TPB)] + [("OX", a, b), ("Y", a, b)]
    return steps + finish(SUB_OF[("attn", a)], b)


def weigh(a, b, h):
    if a == SELF_WIDE:
        return [("ZV", b, h)]
    return [("PV", a, b, h)] + ([("OG", a, b, h // 4)] if h % 4 == 3 else [])


def attention_start(layers):
    a = layers[0]
    rows = [[("ROWS", a, b, half) for half in range(2)] for b in range(2)]
    return project(a, 0) + rows[0] + project(a, 1) + rows[1] + (values(a, 0) if a != SELF_WIDE else []) + maxima(a, 0)


def attention_run(layers, before):
    order = [(a, b) for a in layers for b in range(B)]
    out, tail = values(SELF_WIDE, 0) if layers[0] == SELF_WIDE else [], []
    for n, (a, b) in enumerate(order):
        heads = [[("P2", a, b, h)] + (weigh(a, b, h - 2) if h >= 2 else []) for h in range(NH)]
        heads += [weigh(a, b, NH - 2) + weigh(a, b, NH - 1)]
        first = ([("ROWS", *order[n + 1], 1)] if n else []) + values(*order[n + 1]) if n + 1 < len(order) else []
        late = maxima(*order[n + 1]) if n + 1 < len(order) else []
        for i in (2, 3) if n == 0 else (n + 3,):
            if i < len(order):
                tail = tail + (before.get(i, []) if i < B else []) + project(*order[i])
        if n + 2 < len(order):
            heads[12].append(("ROWS", *order[n + 2], 0))
        cut = 3
        out += spread(heads[:cut], first)
        out += spread(heads[cut:], merge(tail, late))
        tail = attention_tail(a, b)
    return out, tail


def merge(a, b):
    out, i, j = [], 0, 0
    while i < len(a) or j < len(b):
        if j >= len(b) or (i < len(a) and i * len(b) <= j * len(a)):
            out.append(a[i])
            i += 1
        else:
            out.append(b[j])
            j += 1
    return out


def moe_chunk(m, c):
    nf = MOE_F[m] // 128
    main = []
    for e in range(NE):
        for f in range(nf):
            main.append([("MH", m, c, e, f)] + ([("MG", m, c, e, f)] if m == 2 else []))
            if f == nf - 1 and e:
                main.append([("MO", m, c, e - 1)])
    return main + [[("MO", m, c, NE - 1)]]


def experts(m, pending, start):
    s = SUB_OF[("moe", m)]
    bias = [[("GB", m, c), ("BI", m, c)] if m in (1, 3) else [] for c in range(2)]
    if m == 0:
        out = pending + [("RANK", m)] + spread(moe_chunk(m, 0), [])
    else:
        out = bias[0] + spread(moe_chunk(m, 0), pending)
    out += [("STAT", s, 0), ("STAT", s, 1)] + bias[1]
    return out + spread(moe_chunk(m, 1), finish(s, 0)[1:] + finish(s, 1)[1:] + start), {b: finish(s, b) for b in (2, 3)}


def mamba_steps(start):
    out = [("DT", 0), ("DT", 1), ("DZ", 0), ("DZ", 1)]
    side = []
    for c in range(2):
        out += spread([[("MB", n, c), ("MC", n, c)] for n in range(NSTATE)], side)
        side = [("MY", 0)] + finish(0, 0) + [("MY", 1)] + finish(0, 1) + start
    return out, {b: [("MY", b)] + finish(0, b) for b in (2, 3)}


def linear_steps(before):
    s = SUB_OF[("linear", 0)]
    out = [("LC", w, i) for i in range(2) for w in range(2)]
    units = [(b, half) for b in range(B) for half in range(2)]
    parts = [(w, b, t, half) for b, half in units for t in range(TPB) for w in range(2)]
    waiting = []
    for i in range(len(parts) + 6):
        if i % 4 == 2 and i >= 6:
            pb, ph = units[(i - 6) // 4]
            for g in range(4 * ph, 4 * ph + 4):
                waiting += [("LA", pb, 2 * g), ("LA", pb, 2 * g + 1)] + ([("LO", pb, g - 1)] if g % 4 else [])
            waiting.append(("LO", pb, 4 * ph + 3))
            if ph:
                waiting += [("LX", pb, t, j) for t in range(TPB) for j in range(2)] + [("LY", pb)] + finish(s, pb)
        if i in (4, 12):
            waiting += before.get(2 + (i > 4), [])
        slots = [[], [], []]
        if i < len(parts):
            w, b, t, half = parts[i]
            slots[0].append(("LF", *parts[i]))
            if i % 4 == 3:
                slots[0] += [("LV", b, j, half) for j in range(TPB)]
        if 0 < i <= len(parts):
            slots[2].append(("LS", *parts[i - 1]))
        if 1 < i <= len(parts) + 1:
            slots[1] += [("LK", *parts[i - 2]), ("LT", *parts[i - 2], 0), ("LT", *parts[i - 2], 1)]
        left = 3 * (4 - (i - 2) % 4)
        for slot in slots:
            out += slot
            take = -(-len(waiting) // left)
            out += waiting[:take]
            del waiting[:take]
            left -= 1
    return out + waiting


def schedule():
    out, before = mamba_steps(attention_start([0, 1]))
    run, tail = attention_run([0, 1], before)
    out += run
    for m, layers in ((0, [2, 3]), (1, [4, 5])):
        part, before = experts(m, tail, attention_start(layers))
        out += part
        run, tail = attention_run(layers, before)
        out += run
    part, before = experts(2, tail, [])
    out += part + linear_steps(before) + attention_start([6])
    run, tail = attention_run([6], {})
    part, before = experts(3, run and tail, [])
    return out + run + part + before[2] + before[3]


BANKS = {"max": 2, "exp": 2, "misc": 2}
USES = {
    "max": ("SM", "ZV", "MO", "BI", "LF", "LO"),
    "exp": ("P2", "MH", "MG", "LA", "MB", "MC"),
    "misc": ("QK", "V", "Z", "MT", "OT", "OX", "Y", "XT", "GATE", "RANK", "GB", "DT", "DZ", "MY",
             "GQ", "GS", "GT", "GM", "LC", "LV", "LT", "LX", "LY"),
}
POOL_OF = {k: p for p, ks in USES.items() for k in ks}


def decoder(nc, I, scratch, out):
    fp32, bf16, u32, i32 = mybir.dt.float32, mybir.dt.bfloat16, mybir.dt.uint32, mybir.dt.int32
    ALU, ACT, AX = mybir.AluOpType, mybir.ActivationFunctionType, mybir.AxisListType
    steps = schedule()
    count, seen, turn, turns, bank_steps = {}, {}, {}, {p: 0 for p in BANKS}, {p: [] for p in BANKS}
    for st in steps:
        seen[st[0]] = seen.get(st[0], 0) + 1
        count[st] = seen[st[0]]
        if st[0] in POOL_OF:
            p = POOL_OF[st[0]]
            turn[st] = turns[p]
            turns[p] += 1
            bank_steps[p].append(st)
    with ExitStack() as ctx:
        def sb(name, shape, dt=fp32):
            return ctx.enter_context(nc.sbuf_tensor(name, shape, dt))

        def sem(name):
            return ctx.enter_context(nc.semaphore(name))

        bank = {p: [ctx.enter_context(nc.psum_tensor(f"bank_{p}{i}", [128, 512], fp32)) for i in range(n)]
                for p, n in BANKS.items()}
        weigh_banks = [ctx.enter_context(nc.psum_tensor(f"bank_weigh{i}", [128, 512], fp32)) for i in range(2)]

        def psum(st):
            p = POOL_OF[st[0]]
            return bank[p][turn[st] % BANKS[p]]

        x_tok = sb("x_tok", [128, NTT, D])
        xT = sb("xT", [128, NT])
        ctxT = sb("ctxT", [128, NT])
        res = sb("res", [128, 2, TPB, D])
        stats = sb("stats", [128, TPB, 6])
        mv = sb("mv", [128, 2, TPB, 2])
        rstd = sb("rstd", [128, 2, TPB])
        minus_half = sb("minus_half", [128, TPB])
        wA = sb("wA", [128, 7, 4, D])
        bqk = sb("bqk", [128, 7, 2])
        bvo = sb("bvo", [128, 7, 2, D])
        qk32 = sb("qk32", [128, 2, 2, S])
        rem = sb("rem", [128, 2, S])
        parts = sb("parts", [128, 2, 2, 3, S], bf16)
        QR = sb("QR", [128, 2, NH, S], bf16)
        KR = sb("KR", [128, 2, NH, S], bf16)
        V = sb("V", [128, 2, TPB, NH, 32])
        mx = sb("mx", [128, 2, TPB, NH])
        ms = sb("ms", [128, 2, TPB, 128], bf16)
        msT = sb("msT", [128, 2, S], bf16)
        P = sb("P", [128, NBUF_P, TPB * S])
        og = sb("og", [128, 2, 4, S])
        rden = sb("rden", [128, TPB, NH])
        o = sb("o", [128, TPB, D])
        oT = sb("oT", [128, S])
        acc = sb("acc", [128, 4, D])
        ident = sb("ident", [128, 128])
        identb = sb("identb", [128, 128], bf16)
        pick = sb("pick", [128, NH], bf16)
        causal_q = sb("causal_q", [128, 128], bf16)
        causal_k = sb("causal_k", [128, 128], bf16)
        keep_past = sb("keep_past", [128, S + 128], bf16)
        earlier = sb("earlier", [128, 128])
        ones = sb("ones", [128, 128])
        iota = sb("iota", [128, S])
        gate_w = sb("gate_w", [128, 4, NE])
        gate_b = sb("gate_b", [128, 4, NE])
        b1 = sb("b1", [128, 2, NE, 2])
        b2 = sb("b2", [NE, 2, D])
        norm_w = sb("norm_w", [128, 2, D])
        w13 = sb("w13", [128, 2, NE, 512])
        w1, w3 = w13[:, 0], w13[:, 1]
        w2 = sb("w2", [128, NE, 4, D])
        wide_w = w13[:, 1].rearrange("p e f -> p (e f)")[:, 0:NH * D]
        featT = w13[:, :, :, :].rearrange("p w e (x s) -> p w (e x) s", s=S)
        logits = sb("logits", [128, TPB, NE])
        top = sb("top", [128, TPB, 8])
        top_at = sb("top_at", [128, TPB, 8], u32)
        top_atf = sb("top_atf", [128, TPB, 8])
        gw = sb("gw", [128, TPB, 8])
        gs = sb("gs", [128, TPB, 8])
        gden = sb("gden", [128, TPB, 1])
        gz = sb("gz", [128, TPB, 1])
        gtmp = sb("gtmp", [128, NE])
        gates = sb("gates", [128, NTT, NE])
        chosen = sb("chosen", [128, NTT, NE])
        prefix = sb("prefix", [128, NTT, NE])
        gT = sb("gT", [NE, 512])
        AREA = 9344
        area = sb("area", [128, AREA])
        at = [0]

        def carve(*shape, room=None):
            n = 1
            for k in shape:
                n *= k
            base = area[:, :] if room is None else room
            v = base[:, at[0]:at[0] + n]
            at[0] += n
            assert at[0] <= base.shape[1], at[0]
            if len(shape) > 1:
                names = " ".join(f"a{i}" for i in range(len(shape)))
                v = v.rearrange(f"p ({names}) -> p {names}", **{f"a{i}": k for i, k in enumerate(shape)})
            return v

        w13_room = w13[:, :, :, :].rearrange("p w e f -> p (w e f)")
        w2_room = w2[:, :, :, :].rearrange("p e f d -> p (e f d)")
        xdt, zb, dt, dtu, yacc = (carve(NT, room=w13_room) for _ in range(5))
        absz, softp = carve(512, room=w13_room), carve(512, room=w13_room)
        abar, bu = carve(2, 512, room=w13_room), carve(2, 512, room=w13_room)
        at[0] = 0
        hs, gc = carve(2, 512, room=w2_room), carve(2, 512, room=w2_room)
        wx_dt, w_dt = carve(DT_RANK, room=w2_room), carve(D, room=w2_room)
        wBC, negA, bBC, vecs = (carve(2, NSTATE, room=w2_room), carve(NSTATE, room=w2_room),
                                carve(2, NSTATE, room=w2_room), carve(4, room=w2_room))
        iota_i = area[:, 0:S].bitcast(i32)
        at[0] = 0
        ZW = D + 2
        Z = carve(2, TPB, NH, ZW)
        at[0] = 0
        hT = carve(2, 4, 512)
        gated = carve(2, 512)
        x_before = area[:, AREA - NTT * D:AREA].rearrange("p (t d) -> p t d", d=D)
        at[0] += 64
        lw = carve(4, 1024)
        at[0] = 0
        lraw_w = carve(2, 8, D)
        lraw_k = carve(2, 8, FD)
        at[0] = 0
        le, lv = carve(3, 8, 2, FD), carve(TPB, NH, HD + 1)
        at[0] = 0
        lf, lo = carve(2, 8, 2, FD, room=w2_room), carve(TPB, NH * HD, room=w2_room)
        loT = og
        at[0] = 0
        ctx_tok = w13[:, 1].rearrange("p e f -> p (e f)")[:, 0:NTT * D].rearrange("p (t d) -> p t d", d=D)
        gq, one_hot, one_hotT, memT = carve(S), carve(2, S), carve(2, S), carve(2, S)
        at[0] = 0
        adj, biasf, unused = carve(2, 2 * S), carve(2, 2, 2 * S), carve(2, S)
        mask = area[:, at[0]:at[0] + 2 * 4 * S].bitcast(i32).rearrange("p (b o n) -> p b o n", b=2, o=2)
        at[0] += 2 * 4 * S

        one_col = sb("one_col", [128, 1])
        clipped = sem("clipped")
        lmax_v = sb("lmax", [128, 2, 8])
        lden = sb("lden", [128, 2, NH])
        filled = {k: sem(f"{k}_filled") for k in POOL_OF}
        read = {k: sem(f"{k}_read") for k in POOL_OF}
        filled["PV"] = sem("PV_filled")
        read["OG"] = sem("OG_read")
        consts, consts_pool = sem("consts"), sem("consts_pool")
        ctx_in, wide_in = sem("ctx_in"), sem("wide_in")
        loaded, mamba_in, moe_in, mask_in, lin_in = sem("loaded"), sem("mamba_in"), sem("moe_in"), sem("mask_in"), sem("lin_in")
        split_done, parts_stored, rows_in = sem("split_done"), sem("parts_stored"), [[sem(f"rows_in{i}{j}") for j in range(2)] for i in range(2)]
        mask_more = [sem("mask2_in"), sem("mask3_in")]
        shift_done, bias_sum, biased, z_ones = sem("shift_done"), sem("bias_sum"), sem("biased"), sem("z_ones")
        stat_done, rstd_done, norm_done = sem("stat_done"), sem("rstd_done"), sem("norm_done")
        dve_chain, act_chain, pool_chain = sem("dve_chain"), sem("act_chain"), sem("pool_chain")
        dz_act, dz_dve, abar_done, scan_done, yacc_done, state_out = (
            sem("dz_act"), sem("dz_dve"), sem("abar_done"), sem("scan_done"), sem("yacc_done"), sem("state_out"))
        top_done, gate_exp, gates_done, ranked = sem("top_done"), sem("gate_exp"), sem("gates_done"), sem("ranked")
        lexp_done, lsum_done, lfeat_done, out_done = (
            sem("lexp_done"), sem("lsum_done"), sem("lfeat_done"), sem("out_done"))

        units = [st for st in steps if st[0] == "QK"]
        unit = {(st[1], st[2]): i for i, st in enumerate(units)}
        exps = [st for st in steps if st[0] == "P2"]

        def weighs(n):
            _, a, b, h = exps[n]
            return ("ZV", b, h) if a == SELF_WIDE else ("PV", a, b, h)

        STATS = [st for st in steps if st[0] in ("STAT", "STAT2")]
        stat_no = {st: i + 1 for i, st in enumerate(STATS)}

        def x_from(s, b):
            return ("XT", s - 1, b) if s else None

        def finished(eng, st):
            eng.wait_ge(read[st[0]], count[st])

        def full(eng, st):
            eng.wait_ge(filled[st[0]], count[st])

        block = ctx.enter_context(nc.Block())
        N_MAMBA, N_LIN = 9, 6
        N_LOADED0 = 9

        @block.sync
        def _(sp):
            def load(dst, name, to):
                sp.dma_start(dst, I[name]).then_inc(to, 16)

            load(xT[:, :], "xT", mamba_in)
            load(wx_dt[:, :], "w_xdt", mamba_in)
            load(w_dt[0:DT_RANK, :], "w_dt", mamba_in)
            load(wBC[:, :, :], "w_BC", mamba_in)
            load(negA[:, :], "A_log", mamba_in)
            load(bBC[:, :, :], "b_BC", mamba_in)
            load(vecs[:, 0:2], "dt_D", mamba_in)
            load(vecs[0:DT_RANK, 2:3], "b_xdt", mamba_in)
            load(x_tok[:, :, :], "x", mamba_in)
            load(ctxT[:, :], "ctxT", loaded)
            load(wA[:, :, :, :], "w_attn", loaded)
            load(bqk[:, :, :], "b_qk", loaded)
            load(bvo[:, :, :, :], "b_vo", loaded)
            load(gate_w[:, :, :], "gate_w", loaded)
            load(gate_b[:, :, :], "gate_b", loaded)
            load(b1[:, :, :, :], "b1", loaded)
            load(b2[:, :, :], "b2", loaded)
            load(norm_w[:, :, :], "norm_w", loaded)
            for st in steps:
                if st[0] == "SPLIT":
                    n = unit[st[1:]]
                    sp.wait_ge(split_done, n + 1)
                    if n >= 2:
                        for half in range(2):
                            sp.wait_ge(rows_in[n % 2][half], 96 * (n // 2))
                    sp.dma_start(scratch[n % 2].rearrange("q k p t -> p (q k) t"),
                                 parts[:, n % 2].rearrange("p q k t -> p (q k) t")).then_inc(parts_stored, 16)
                elif st[0] == "ROWS":
                    half = st[3]
                    n = unit[st[1:3]]
                    sp.wait_ge(parts_stored, 16 * (n + 1))
                    if n >= 2:
                        full(sp, ("P2", units[n - 2][1], units[n - 2][2], 8 * half + 7))
                    else:
                        sp.wait_ge(consts, 1)
                    heads = slice(8 * half, 8 * half + 8)
                    for row, np_, *firsts in PART_RUNS:
                        for q, rows in enumerate((QR, KR)):
                            part = scratch[n % 2, q, firsts[q]:firsts[q] + np_].rearrange("k (d h) t -> (k d) h t", d=DH)
                            sp.dma_start(rows[DH * row:DH * (row + np_), n % 2, heads, :], part[:, heads, :]).then_inc(rows_in[n % 2][half], 16)
                elif st == ("MY", B - 1):
                    full(sp, st)
                    load(wide_w, "wide_w", wide_in)
                    load(w1[:, :, 0:256], "w1_0", moe_in)
                    load(w2[:, :, 0:2, :], "w2_0", moe_in)
                elif st[0] == "BIAS":
                    b = st[1]
                    if b == 0:
                        load(adj, "adj", mask_in)
                        load(mask[:, 0], "mask0", mask_in)
                        load(mask[:, 1], "mask1", mask_in)
                    elif b < 3:
                        sp.wait_ge(bias_sum, b)
                        load(mask[:, (b + 1) % 2], f"mask{b + 1}", mask_more[b - 1])
                elif st == ("MO", 0, 1, NE - 1):
                    full(sp, st)
                    load(w1[:, :, 0:256], "w1_1", moe_in)
                    load(w2[:, :, 0:2, :], "w2_1", moe_in)
                elif st == ("MO", 1, 1, NE - 1):
                    full(sp, st)
                    finished(sp, st)
                    load(w1[:, :, :], "w1_2", moe_in)
                    load(w3[:, :, :], "w3_2", moe_in)
                    load(w2[:, :, :, :], "w2_2", moe_in)
                elif st == ("MO", 2, 1, NE - 1):
                    full(sp, st)
                    load(lw[:, 2, :], "lin_v", lin_in)
                    load(lw[:, 3, :], "lin_o", lin_in)
                    for i in range(2):
                        load(lraw_w[64 * i:64 * i + 64, :, :, :], f"lin_w{i}", lin_in)
                        load(lraw_k[64 * i:64 * i + 64, :, :, :], f"lin_k{i}", lin_in)
                elif st == ("LA", B - 1, NH - 1):
                    full(sp, st)
                    finished(sp, st)
                    load(w1[:, :, 0:256], "w1_3", moe_in)
                    load(ctx_tok, "ctx", ctx_in)
                elif st == ("LY", B - 1):
                    full(sp, st)
                    load(w2[:, :, 0:2, :], "w2_3", moe_in)
                elif st[0] == "NORM" and st[1] == LAST:
                    b = st[2]
                    sp.wait_ge(norm_done, count[st])
                    sp.dma_start(out[b].rearrange("(t p) d -> p t d", p=128),
                                 x_tok[:, TPB * b:TPB * (b + 1), :]).then_inc(out_done, 16)
            sp.wait_ge(out_done, 16 * B)

        def wide_sum(b):
            return og[:, unit[(SELF_WIDE, b)] % 2, 0, :].rearrange("p (t d) -> p t d", d=D)

        def loTv(t, j):
            return loT[:, t, j // 2, (j % 2) * 128:(j % 2 + 1) * 128]

        MOE_LOADS = (2, 4, 7, 9)

        @block.tensor
        def _(pe):
            def src(a, b):
                if a == GATHERED:
                    return memT[:, unit[(a, b)] % 2, :]
                return (ctxT if a in CROSS else xT)[:, b * S:(b + 1) * S]

            def wait_x(s, b):
                if s:
                    finished(pe, ("XT", s - 1, b))

            pe.wait_ge(consts_pool, 1)
            pe.wait_ge(mamba_in, 16 * N_MAMBA)
            for st in steps:
                k = st[0]
                if k in POOL_OF:
                    before = turn[st] - BANKS[POOL_OF[k]]
                    if before >= 0:
                        finished(pe, bank_steps[POOL_OF[k]][before])
                    bk = psum(st)
                last = None
                if k == "DT":
                    last = nc.tensor.matmul(bk[0:DT_RANK, :], wx_dt[:, :], xT[:, 512 * st[1]:512 * (st[1] + 1)], start=True, stop=True)
                elif k == "DZ":
                    finished(pe, ("DT", st[1]))
                    last = nc.tensor.matmul(bk[:, :], w_dt[0:DT_RANK, :], xdt[0:DT_RANK, 512 * st[1]:512 * (st[1] + 1)], start=True, stop=True)
                elif k in ("MB", "MC"):
                    w = wBC[:, int(k == "MC"), st[1]:st[1] + 1].to_broadcast([128, 128])
                    last = nc.tensor.matmul(bk[:, :], w, xT[:, 512 * st[2]:512 * (st[2] + 1)], start=True, stop=True)
                elif k == "MY":
                    b = st[1]
                    pe.wait_ge(state_out, b + 1)
                    for t in range(TPB):
                        last = nc.tensor.transpose(bk[:, t * 128:(t + 1) * 128], yacc[:, b * S + t * 128:b * S + (t + 1) * 128], ident[:, :])
                elif k == "XT":
                    _, s, b = st
                    pe.wait_ge(norm_done, count[("NORM", s, b)])
                    for t in range(TPB):
                        last = nc.tensor.transpose(bk[:, t * 128:(t + 1) * 128], x_tok[:, TPB * b + t, :], ident[:, :])
                elif k == "GQ":
                    b = st[1]
                    wait_x(SUB_OF[("attn", GATHERED)], b)
                    last = nc.tensor.matmul(bk[:, 0:S], wA[:, SELF_WIDE, 2, :], xT[:, b * S:(b + 1) * S], start=True, stop=True)
                elif k == "GS":
                    _, b, t = st
                    finished(pe, ("GQ", b))
                    last = nc.tensor.matmul(bk[:, 0:S], gq[:, t * 128:(t + 1) * 128], ctxT[:, b * S:(b + 1) * S], start=True, stop=True)
                elif k == "GT":
                    b = st[1]
                    finished(pe, ("GS", b, TPB - 1))
                    for m in range(TPB):
                        for t in range(TPB):
                            last = nc.tensor.transpose(bk[:, m * S + t * 128:m * S + (t + 1) * 128], one_hot[:, t, m * 128:(m + 1) * 128], ident[:, :])
                elif k == "GM":
                    b = st[1]
                    finished(pe, ("GT", b))
                    pe.wait_ge(ctx_in, 16)
                    for m in range(TPB):
                        last = nc.tensor.matmul(bk[:, 0:S], ctx_tok[:, TPB * b + m, :], one_hotT[:, m, :], start=(m == 0), stop=(m == TPB - 1))
                elif k == "QK":
                    _, a, b = st
                    if unit[(a, b)] == 0:
                        pe.wait_ge(loaded, 16 * N_LOADED0)
                    wait_x(SUB_OF[("attn", a)], b)
                    if a == GATHERED:
                        finished(pe, ("GM", b))
                    for j, x in enumerate((xT[:, b * S:(b + 1) * S], src(a, b))):
                        w = wA[:, a, j, :]
                        last = nc.tensor.matmul(bk[:, j * S:(j + 1) * S], w, x, start=True, stop=True)
                elif k == "V":
                    _, a, b = st
                    x = src(a, b)
                    for t in range(TPB):
                        last = nc.tensor.matmul(bk[:, t * 128:(t + 1) * 128], x[:, t * 128:(t + 1) * 128], wA[:, a, 2, :], start=True, stop=True)
                elif k == "Z":
                    _, b, i = st
                    pe.wait_ge(wide_in, 16)
                    x = xT[:, b * S + (i // 4) * 128:b * S + (i // 4 + 1) * 128]
                    last = nc.tensor.matmul(bk[:, :], x, wide_w[:, 512 * (i % 4):512 * (i % 4 + 1)], start=True, stop=True)
                elif k == "SM":
                    _, a, b, u = st
                    n, h0, t = unit[(a, b)], 2 * (u // 2), u % 2
                    if u % 8 == 0:
                        pe.wait_ge(rows_in[n % 2][u // 8], 96 * (n // 2 + 1))
                    nk = (t + 1) * 128 if a == CAUSAL else S
                    if a == CAUSAL:
                        diagonal = bk[:, :].rearrange("p (h s) -> p h s", h=2)[:, :, t * 128:(t + 1) * 128]
                        nc.tensor.matmul(diagonal, identb[:, :], causal_q[:, :].unsqueeze(1).to_broadcast([128, 2, 128]), start=True, stop=False, skip_group_check=True)
                    for j in range(2):
                        last = nc.tensor.matmul(bk[:, j * S:j * S + nk], QR[:, n % 2, h0 + j, t * 128:(t + 1) * 128], KR[:, n % 2, h0 + j, 0:nk],
                                                start=a != CAUSAL, stop=True, skip_group_check=True)
                elif k == "MT":
                    _, a, b = st
                    n = unit[(a, b)]
                    pe.wait_ge(shift_done, n + 1)
                    for t in range(TPB):
                        last = nc.tensor.matmul(bk[:, t * 128:(t + 1) * 128], ms[:, n % 2, t, :], identb[:, :], start=True, stop=True)
                elif k == "P2":
                    _, a, b, h = st
                    n = unit[(a, b)]
                    if h == 0:
                        finished(pe, ("MT", a, b))
                    ones_of_h = pick[:, h:h + 1].to_broadcast([128, 128])
                    if a == CAUSAL:
                        nc.tensor.matmul(bk[:, 0:S], ones_of_h, msT[:, n % 2, :], start=True, stop=False, skip_group_check=True)
                        nc.tensor.matmul(bk[:, S:S + 128], ones_of_h, msT[:, n % 2, 128:S], start=False, stop=False, skip_group_check=True)
                        diagonals = bk[:, :].rearrange("p (t s) -> p t s", t=2)[:, :, 0:128]
                        nc.tensor.matmul(diagonals, identb[:, :], causal_k[:, :].unsqueeze(1).to_broadcast([128, 2, 128]), start=False, stop=False, skip_group_check=True)
                    else:
                        whole = bk[:, :].rearrange("p (t s) -> p t s", t=2)
                        nc.tensor.matmul(whole, ones_of_h, msT[:, n % 2, :].unsqueeze(1).to_broadcast([128, 2, S]), start=True, stop=False, skip_group_check=True)
                    for t in range(TPB):
                        q0 = t * 128 if a == CAUSAL else 0
                        last = nc.tensor.matmul(bk[:, t * S:t * S + S - q0], KR[:, n % 2, h, t * 128:(t + 1) * 128], QR[:, n % 2, h, q0:S],
                                                start=False, stop=True, skip_group_check=True)
                elif k == "PV":
                    _, a, b, h = st
                    n, e = unit[(a, b)], count[("P2", a, b, h)]
                    g, j = h // 4, h % 4
                    og_no = count[("OG", a, b, g)]
                    if h == 0:
                        finished(pe, ("V", a, b))
                    if j == 0 and og_no > 2:
                        pe.wait_ge(read["OG"], og_no - 2)
                    pe.wait_ge(read["P2"], e)
                    half = (og_no - 1) % 2
                    for t in range(TPB):
                        q0 = t * 128 if a == CAUSAL else 0
                        last = nc.tensor.matmul(weigh_banks[half][32 * j:32 * j + 32, q0:S], V[:, n % 2, t, h, :],
                                                P[:, (e - 1) % NBUF_P, t * S:t * S + S - q0], start=(t == 0), stop=(t == TPB - 1), skip_group_check=True)
                elif k == "ZV":
                    _, b, h = st
                    n, e = unit[(SELF_WIDE, b)], count[("P2", SELF_WIDE, b, h)]
                    if h == 0:
                        finished(pe, ("Z", b, 7))
                    pe.wait_ge(read["P2"], e)
                    for q in range(TPB):
                        for t in range(TPB):
                            last = nc.tensor.matmul(bk[:, q * S:q * S + D + 1], P[:, (e - 1) % NBUF_P, t * S + q * 128:t * S + (q + 1) * 128],
                                                    Z[:, b % 2, t, h, 0:D + 1], start=(t == 0), stop=(t == TPB - 1))
                elif k == "OT":
                    _, a, b, t = st
                    pe.wait_ge(read["OG"], count[("OG", a, b, 3)])
                    for g in range(4):
                        last = nc.tensor.transpose(bk[:, g * 128:(g + 1) * 128], og[:, unit[(a, b)] % 2, g, t * 128:(t + 1) * 128], ident[:, :])
                elif k == "OX":
                    _, a, b = st
                    finished(pe, ("OT", a, b, TPB - 1))
                    for t in range(TPB):
                        last = nc.tensor.transpose(bk[:, t * 128:(t + 1) * 128], o[:, t, :], ident[:, :])
                elif k == "Y":
                    _, a, b = st
                    finished(pe, ("OX", a, b))
                    for t in range(TPB):
                        last = nc.tensor.matmul(bk[:, t * 128:(t + 1) * 128], oT[:, t * 128:(t + 1) * 128], wA[:, a, 3, :], start=True, stop=True)
                elif k == "GATE":
                    _, m, b = st
                    wait_x(SUB_OF[("moe", m)], b)
                    for t in range(TPB):
                        last = nc.tensor.matmul(bk[:, t * NE:(t + 1) * NE], xT[:, b * S + t * 128:b * S + (t + 1) * 128], gate_w[:, m, :], start=True, stop=True)
                elif k == "RANK":
                    pe.wait_ge(gates_done, count[("GATE", 0, B - 1)])
                    flat = chosen[:, :, :].rearrange("p t e -> p (t e)")
                    nc.tensor.matmul(bk[:, 0:NTT * NE], earlier[:, :], flat, start=True, stop=True)
                    last = nc.tensor.matmul(bk[:, NTT * NE:2 * NTT * NE], ones[:, :], flat, start=True, stop=True)
                elif k == "GB":
                    _, m, c = st
                    pe.wait_ge(gates_done, count[("GATE", m, 2 * c + 1)])
                    for t in range(4):
                        last = nc.tensor.matmul(bk[0:NE, t * 128:(t + 1) * 128], gates[:, 4 * c + t, :], ident[:, :], start=True, stop=True)
                elif k == "BI":
                    _, m, c = st
                    finished(pe, ("GB", m, c))
                    for t in range(4):
                        last = nc.tensor.matmul(bk[:, t * 128:(t + 1) * 128], gT[:, t * 128:(t + 1) * 128], b2[:, m // 2, :], start=True, stop=True)
                elif k in ("MH", "MG"):
                    _, m, c, e, f = st
                    if c == 0 and e == 0 and f == 0:
                        pe.wait_ge(moe_in, 16 * MOE_LOADS[m])
                    w = w1 if k == "MH" else w3
                    last = nc.tensor.matmul(bk[:, :], w[:, e, f * 128:(f + 1) * 128], xT[:, 512 * c:512 * (c + 1)], start=True, stop=True)
                elif k == "MO":
                    _, m, c, e = st
                    nf = MOE_F[m] // 128
                    finished(pe, ("MG" if m == 2 else "MH", m, c, e, nf - 1))
                    for t in range(4):
                        for f in range(nf):
                            last = nc.tensor.matmul(bk[:, t * 128:(t + 1) * 128], hT[:, e % 2, f, t * 128:(t + 1) * 128], w2[:, e, f, :],
                                                    start=(f == 0), stop=(f == nf - 1))
                elif k == "LC":
                    _, w, i = st
                    pe.wait_ge(lin_in, 16 * N_LIN)
                    for h in range(8):
                        last = nc.tensor.matmul(bk[:, h * FD:(h + 1) * FD], lraw_w[64 * i:64 * i + 64, w, h, :], lraw_k[64 * i:64 * i + 64, w, h, :], start=True, stop=True)
                elif k == "LV":
                    _, b, t, half = st
                    last = nc.tensor.matmul(bk[:, :], xT[:, b * S + t * 128:b * S + (t + 1) * 128], lw[:, 2, half * 512:(half + 1) * 512], start=True, stop=True)
                elif k == "LF":
                    _, w, b, t, half = st
                    wait_x(SUB_OF[("linear", 0)], b)
                    finished(pe, ("LC", w, half))
                    last = nc.tensor.matmul(bk[:, :], xT[:, b * S + t * 128:b * S + (t + 1) * 128], lw[:, w, half * 512:(half + 1) * 512], start=True, stop=True)
                elif k == "LT":
                    _, w, b, t, half, i = st
                    pe.wait_ge(clipped, count[("LK", w, b, t, half)])
                    buf = (count[("LF", w, b, t, half)] - 1) % 3
                    for h in range(4):
                        last = nc.tensor.transpose(bk[:, h * 128:(h + 1) * 128], le[:, buf, 4 * i + h].rearrange("p a f -> p (a f)"), ident[:, :])
                elif k == "LA":
                    _, b, h = st
                    finished(pe, ("LT", 1, b, TPB - 1, h // 8, 1))
                    nc.tensor.matmul(bk[:, 0:S], featT[:, 1, h, 0:128], featT[:, 0, h, :], start=True, stop=True)
                    last = nc.tensor.matmul(bk[:, S:S + 128], featT[:, 1, h, 128:S], featT[:, 0, h, 128:S], start=True, stop=True)
                elif k == "LO":
                    _, b, g = st
                    finished(pe, ("LA", b, 2 * g + 1))
                    finished(pe, ("LV", b, TPB - 1, g // 4))
                    for t in range(TPB):
                        for j in range(2):
                            h, to = 2 * g + j, (2 * t + j) * 66
                            for i in range(t + 1):
                                last = nc.tensor.matmul(bk[:, to:to + HD + 1], P[:, (count[("LA", b, h)] - 1) % NBUF_P, (t + i) * 128:(t + i + 1) * 128],
                                                        lv[:, i, h, :], start=(i == 0), stop=(i == t))
                elif k == "LX":
                    _, b, t, i = st
                    finished(pe, ("LO", b, 7))
                    for j in range(4):
                        last = nc.tensor.transpose(bk[:, j * 128:(j + 1) * 128], lo[:, t, (4 * i + j) * 128:(4 * i + j + 1) * 128], ident[:, :])
                elif k == "LY":
                    b = st[1]
                    finished(pe, ("LX", b, TPB - 1, 1))
                    for t in range(TPB):
                        for j in range(8):
                            last = nc.tensor.matmul(bk[:, t * 128:(t + 1) * 128], loTv(t, j), lw[:, 3, j * 128:(j + 1) * 128], start=(j == 0), stop=(j == 7))
                if last is not None:
                    last.then_inc(filled[k], 1)

        @block.scalar
        def _(act):
            chain = [0]

            def link(ins):
                chain[0] += 1
                ins.then_inc(act_chain, 1)
                act.wait_ge(act_chain, chain[0])

            act.wait_ge(mamba_in, 16 * N_MAMBA)
            link(nc.scalar.activation(negA[:, :], negA[:, :], ACT.Exp))
            link(nc.scalar.mul(negA[:, :], negA[:, :], -1.0))
            for st in steps:
                k = st[0]
                bk = psum(st) if k in POOL_OF else None
                if k == "DT":
                    full(act, st)
                    nc.scalar.activation(xdt[0:DT_RANK, 512 * st[1]:512 * (st[1] + 1)], bk[0:DT_RANK, :], ACT.Identity,
                                         bias=vecs[0:DT_RANK, 2:3]).then_inc(read[k], 1)
                elif k == "DZ":
                    c = slice(512 * st[1], 512 * (st[1] + 1))
                    full(act, st)
                    nc.scalar.activation(zb[:, c], bk[:, :], ACT.Identity, bias=vecs[:, 0:1]).then_inc(read[k], 1)
                    act.wait_ge(read[k], count[st])
                    if st[1]:
                        act.wait_ge(dz_dve, st[1])
                    link(nc.scalar.activation(absz[:, :], zb[:, c], ACT.Abs))
                    link(nc.scalar.activation(absz[:, :], absz[:, :], ACT.Exp, scale=-1.0))
                    nc.scalar.activation(softp[:, :], absz[:, :], ACT.Ln, bias=one_col[:, 0:1]).then_inc(dz_act, 1)
                elif k == "MB":
                    _, n, c = st
                    i = count[st] - 1
                    if i < 2:
                        act.wait_ge(dz_dve, 2)
                    else:
                        act.wait_ge(scan_done, i - 1)
                    nc.scalar.activation(abar[:, i % 2, :], dt[:, 512 * c:512 * (c + 1)], ACT.Exp, scale=negA[:, n:n + 1]).then_inc(abar_done, 1)
                elif k == "XT":
                    _, s, b = st
                    full(act, st)
                    nc.scalar.copy(xT[:, b * S:(b + 1) * S], bk[:, 0:S]).then_inc(read[k], 1)
                elif k == "GQ":
                    full(act, st)
                    if st[1] == 0:
                        full(act, ("LY", B - 1))
                    nc.scalar.copy(gq, bk[:, 0:S]).then_inc(read[k], 1)
                elif k == "GT":
                    full(act, st)
                    nc.scalar.copy(one_hotT.rearrange("p m s -> p (m s)"), bk[:, :]).then_inc(read[k], 1)
                elif k == "GM":
                    b = st[1]
                    full(act, st)
                    nc.scalar.copy(memT[:, b % 2, :], bk[:, 0:S]).then_inc(read[k], 1)
                elif k == "QK":
                    _, a, b = st
                    n = unit[(a, b)]
                    full(act, st)
                    if n == 0:
                        act.wait_ge(loaded, 16 * N_LOADED0)
                    if n >= 2:
                        act.wait_ge(split_done, n - 1)
                    nc.scalar.activation(qk32[:, n % 2, 0, :], bk[:, 0:S], ACT.Identity, bias=bqk[:, a, 0:1])
                    nc.scalar.activation(qk32[:, n % 2, 1, :], bk[:, S:2 * S], ACT.Identity, bias=bqk[:, a, 1:2]).then_inc(read[k], 1)
                elif k == "Z":
                    _, b, i = st
                    full(act, st)
                    if b >= 2:
                        full(act, ("ZV", b - 2, NH - 1))
                    else:
                        act.wait_ge(z_ones, 1)
                    nc.scalar.copy(Z[:, b % 2, i // 4, 4 * (i % 4):4 * (i % 4) + 4, 0:D], bk[:, :].rearrange("p (h d) -> p h d", d=D)).then_inc(read[k], 1)
                elif k == "MT":
                    _, a, b = st
                    n = unit[(a, b)]
                    full(act, st)
                    if n >= 2:
                        full(act, ("P2", units[n - 2][1], units[n - 2][2], NH - 1))
                    nc.scalar.copy(msT[:, n % 2, :], bk[:, 0:S]).then_inc(read[k], 1)
                elif k == "P2":
                    e = count[st]
                    if e > NBUF_P:
                        full(act, weighs(e - 1 - NBUF_P))
                    if st[2:] == (0, 0) and SUBLAYERS[SUB_OF[("attn", st[1])] - 1][0] == "linear":
                        full(act, ("LO", B - 1, 7))
                    full(act, st)
                    if st[1] == MASKED:
                        act.wait_ge(biased, count[st] - count[("P2", MASKED, 0, 0)] + 1)
                    width = S + 128 if st[1] == CAUSAL else 2 * S
                    nc.scalar.activation(P[:, (e - 1) % NBUF_P, 0:width], bk[:, 0:width], ACT.Exp, scale=SCALE).then_inc(read[k], 1)
                elif k == "OG":
                    _, a, b, g = st
                    n, half = unit[(a, b)], (count[st] - 1) % 2
                    full(act, ("PV", a, b, 4 * g + 3))
                    if n >= 2 and units[n - 2][1] != SELF_WIDE:
                        full(act, ("OT", units[n - 2][1], units[n - 2][2], TPB - 1))
                    elif n >= 2:
                        act.wait_ge(stat_done, stat_no[("STAT", SUB_OF[("attn", SELF_WIDE)], units[n - 2][2])])
                    nc.scalar.copy(og[:, n % 2, g, :], weigh_banks[half][:, 0:S]).then_inc(read["OG"], 1)
                elif k == "OX":
                    _, a, b = st
                    full(act, st)
                    if count[st] > 1:
                        act.wait_ge(filled["Y"], count[st] - 1)
                    nc.scalar.copy(oT[:, :], bk[:, 0:S]).then_inc(read[k], 1)
                elif k == "GATE":
                    _, m, b = st
                    act.wait_ge(top_done, count[st])
                    flat = gw[:, :, :].rearrange("p t e -> p (t e)")
                    nc.scalar.activation(gs[:, :, :].rearrange("p t e -> p (t e)"), flat, ACT.Exp,
                                         scale=(-1.0, 0.2, 1.0, 1.0)[m]).then_inc(gate_exp, 1)
                elif k == "GB":
                    full(act, st)
                    nc.scalar.copy(gT[:, :], bk[0:NE, :]).then_inc(read[k], 1)
                elif k == "MH":
                    _, m, c, e, f = st
                    full(act, st)
                    if m == 2:
                        i = count[("MG", m, c, e, f)]
                        if i > 2:
                            act.wait_ge(read["MG"], i - 2)
                        nc.scalar.activation(gated[:, (i - 1) % 2, :], bk[:, :], ACT.Silu).then_inc(read[k], 1)
                    else:
                        if f == 0 and count[("MO", m, c, e)] > 2:
                            act.wait_ge(filled["MO"], count[("MO", m, c, e)] - 2)
                        if m == 0:
                            nc.scalar.activation(hT[:, e % 2, f, :], bk[:, :], ACT.Gelu).then_inc(read[k], 1)
                        else:
                            nc.scalar.activation(hT[:, e % 2, f, :], bk[:, :], ACT.Gelu if m == 1 else ACT.Relu,
                                                 bias=b1[:, m // 2, e, f:f + 1]).then_inc(read[k], 1)
                elif k == "LC":
                    _, w, i = st
                    full(act, st)
                    nc.scalar.copy(lw[:, w, i * 512:(i + 1) * 512], bk[:, :]).then_inc(read[k], 1)
                elif k == "LV":
                    _, b, t, half = st
                    full(act, st)
                    if b == 0 and t == 0 and half == 0:
                        full(act, ("LC", 1, 1))
                    if b:
                        full(act, ("LO", b - 1, 4 * half + 3))
                    nc.scalar.copy(lv[:, t, 8 * half:8 * half + 8, 0:HD], bk[:, :].rearrange("p (h d) -> p h d", d=HD)).then_inc(read[k], 1)
                elif k == "LF":
                    i = count[st]
                    act.wait_ge(read[k], i)
                    if i > 3:
                        act.wait_ge(filled["LT"], 2 * (i - 3))
                    nc.scalar.activation(le[:, (i - 1) % 3].rearrange("p h a f -> p (h a f)"), lf[:, (i - 1) % 2].rearrange("p h a f -> p (h a f)"), ACT.Exp).then_inc(lexp_done, 1)
                elif k == "LT":
                    _, w, b, t, half, i = st
                    full(act, st)
                    if b:
                        full(act, ("LA", b - 1, 8 * half + 7))
                    h = 8 * half + 4 * i
                    nc.scalar.copy(featT[:, w, h:h + 4, t * 128:(t + 1) * 128], bk[:, :].rearrange("p (h s) -> p h s", h=4)).then_inc(read[k], 1)
                elif k == "LX":
                    _, b, t, i = st
                    full(act, st)
                    if b:
                        full(act, ("LY", b - 1))
                    nc.scalar.copy(loT[:, t, 2 * i:2 * i + 2, :].rearrange("p a b -> p (a b)"), bk[:, :]).then_inc(read[k], 1)

        @block.gpsimd
        def _(pool):
            chain = [0]

            def link(ins):
                chain[0] += 1
                ins.then_inc(pool_chain, 1)
                pool.wait_ge(pool_chain, chain[0])

            for m in (ident, identb):
                link(nc.gpsimd.memset(m[:, :], 0.0))
                link(nc.gpsimd.affine_select(out=m[:, :], in_=m[:, :], compare_op=ALU.not_equal, fill=1.0, base=0, pattern=[[-1, 128]], channel_multiplier=1))
            nc.gpsimd.memset(ones[:, :], 1.0).then_inc(pool_chain, 1)
            nc.gpsimd.memset(one_col[:, :], 1.0).then_inc(pool_chain, 1)
            chain[0] += 2
            link(nc.gpsimd.memset(minus_half[:, :], -0.5))
            link(nc.gpsimd.memset(earlier[:, :], 1.0))
            link(nc.gpsimd.affine_select(out=earlier[:, :], in_=earlier[:, :], compare_op=ALU.is_ge, fill=0.0, base=-1, pattern=[[1, 128]], channel_multiplier=-1))
            link(nc.gpsimd.memset(pick[:, :], 0.0))
            for part in range(2):
                link(nc.gpsimd.affine_select(out=pick[:, :], in_=pick[:, :], compare_op=ALU.not_equal, fill=1.0, base=-NH * part,
                                             pattern=[[-1, NH]], channel_multiplier=1))
            link(nc.gpsimd.memset(causal_q[:, :], 0.0))
            link(nc.gpsimd.affine_select(out=causal_q[:, :], in_=causal_q[:, :], compare_op=ALU.is_ge, fill=NEG, base=0,
                                         pattern=[[-1, 128]], channel_multiplier=1))
            link(nc.gpsimd.memset(causal_k[:, :], 0.0))
            link(nc.gpsimd.affine_select(out=causal_k[:, :], in_=causal_k[:, :], compare_op=ALU.is_ge, fill=NEG, base=0,
                                         pattern=[[1, 128]], channel_multiplier=-1))
            link(nc.gpsimd.memset(keep_past[:, :], 1.0))
            for c in (0, S):
                diagonal = keep_past[:, c:c + 128]
                link(nc.gpsimd.affine_select(out=diagonal, in_=diagonal, compare_op=ALU.is_ge, fill=0.0, base=0,
                                             pattern=[[1, 128]], channel_multiplier=-1))
            link(nc.gpsimd.iota(iota_i[:, :], pattern=[[1, S]], base=0, channel_multiplier=0))
            nc.gpsimd.tensor_copy(iota[:, :], iota_i[:, :]).then_inc(consts_pool, 1)
            for st in steps:
                k = st[0]
                if k == "MC":
                    _, n, c = st
                    i = count[st]
                    part = yacc[:, 512 * c:512 * (c + 1)]
                    finished(pool, st)
                    if n == 0:
                        nc.gpsimd.tensor_copy(part, gc[:, (i - 1) % 2, :]).then_inc(yacc_done, 1)
                    else:
                        pool.wait_ge(yacc_done, i - 1)
                        nc.gpsimd.tensor_tensor(part, part, gc[:, (i - 1) % 2, :], ALU.add).then_inc(yacc_done, 1)
                elif k in ("STAT", "STAT2"):
                    _, s, b = st
                    no = stat_no[st]
                    rms = k == "STAT" and SUBLAYERS[s] in (("attn", 1), ("moe", 0))
                    pool.wait_ge(stat_done, no)
                    link(nc.gpsimd.tensor_scalar(rstd[:, b % 2, :], mv[:, b % 2, :, 1], RMS_EPS if rms else LN_EPS, None, ALU.add))
                    nc.gpsimd.tensor_tensor(rstd[:, b % 2, :], rstd[:, b % 2, :], minus_half[:, :], ALU.pow).then_inc(rstd_done, 1)
                elif k == "SPLIT":
                    _, a, b = st
                    n = unit[(a, b)]
                    finished(pool, ("QK", a, b))
                    if n >= 2:
                        pool.wait_ge(parts_stored, 16 * (n - 1))
                    for q in range(2):
                        x, r = qk32[:, n % 2, q], rem[:, q]
                        hi, mid, low = (parts[:, n % 2, q, i, :] for i in ((0, 1, 2), (2, 1, 0))[q])
                        link(nc.gpsimd.tensor_copy(hi, x))
                        link(nc.gpsimd.tensor_tensor(r, x, hi, ALU.subtract))
                        link(nc.gpsimd.tensor_copy(mid, r))
                        last = nc.gpsimd.tensor_tensor(low, r, mid, ALU.subtract)
                        if q == 0:
                            link(last)
                    last.then_inc(split_done, 1)
                elif st == ("Z", 0, 0):
                    full(pool, ("MO", 0, 1, NE - 1))
                    nc.gpsimd.memset(Z[:, :, :, :, D:D + 1].rearrange("p b t h o -> p (b t h o)"), 1.0).then_inc(z_ones, 1)
                elif k == "LS":
                    i = count[st]
                    pool.wait_ge(lsum_done, i)
                    x = le[:, (i - 1) % 3].rearrange("p h a f -> p (h a) f")
                    nc.gpsimd.tensor_tensor(x, x, lden[:, (i - 1) % 2].unsqueeze(2).to_broadcast([128, 16, FD]), ALU.mult).then_inc(lfeat_done, 1)
                elif st == ("LC", 1, 1):
                    full(pool, st)
                    nc.gpsimd.memset(lv[:, :, :, HD:HD + 1].rearrange("p t h o -> p (t h o)"), 1.0).then_inc(z_ones, 1)

        @block.vector
        def _(dve):
            chain = [0]

            def link(ins):
                chain[0] += 1
                ins.then_inc(dve_chain, 1)
                dve.wait_ge(dve_chain, chain[0])

            V_ = nc.vector
            link(V_.memset(QR[:, :, :, :], 0.0))
            link(V_.memset(V[:, :, :, :, :], 0.0))
            link(V_.memset(V[:, :, :, :, DH:DH + 1], 1.0))
            link(V_.memset(ms[:, :, :, :], 0.0))
            V_.memset(KR[:, :, :, :], 0.0).then_inc(consts, 1)
            dve.wait_ge(consts, 1)
            dve.wait_ge(mamba_in, 16 * N_MAMBA)

            def statistics(src, b, rms):
                for t in range(TPB):
                    V_.bn_stats(stats[:, t, :], src[:, t, :]).then_inc(dve_chain, 1)
                chain[0] += TPB
                dve.wait_ge(dve_chain, chain[0])
                for t in range(TPB):
                    last = V_.bn_aggr(mv[:, b % 2, t, :], stats[:, t, :])
                    if rms or t < TPB - 1:
                        last.then_inc(dve_chain, 1)
                        chain[0] += 1
                if rms:
                    dve.wait_ge(dve_chain, chain[0])
                    for t in range(TPB):
                        last = V_.scalar_tensor_tensor(out=mv[:, b % 2, t, 1:2], in0=mv[:, b % 2, t, 0:1], scalar=mv[:, b % 2, t, 0:1],
                                                       in1=mv[:, b % 2, t, 1:2], op0=ALU.mult, op1=ALU.add)
                        if t < TPB - 1:
                            last.then_inc(dve_chain, 1)
                            chain[0] += 1
                last.then_inc(stat_done, 1)

            for st in steps:
                k = st[0]
                bk = psum(st) if k in POOL_OF else None
                if k == "DZ":
                    c = slice(512 * st[1], 512 * (st[1] + 1))
                    dve.wait_ge(dz_act, st[1] + 1)
                    link(V_.scalar_tensor_tensor(out=dt[:, c], in0=zb[:, c], scalar=0.0, in1=softp, op0=ALU.max, op1=ALU.add))
                    V_.tensor_tensor(dtu[:, c], dt[:, c], xT[:, c], ALU.mult).then_inc(dz_dve, 1)
                    dve.wait_ge(dz_dve, st[1] + 1)
                elif k == "MB":
                    _, n, c = st
                    i = count[st]
                    full(dve, st)
                    V_.scalar_tensor_tensor(out=bu[:, (i - 1) % 2, :], in0=bk[:, :], scalar=bBC[:, 0, n:n + 1], in1=dtu[:, 512 * c:512 * (c + 1)],
                                            op0=ALU.add, op1=ALU.mult).then_inc(read[k], 1)
                    dve.wait_ge(read[k], i)
                    dve.wait_ge(abar_done, i)
                    for b in range(2):
                        part = slice(b * S, (b + 1) * S)
                        last = V_.tensor_tensor_scan(hs[:, (i - 1) % 2, part], abar[:, (i - 1) % 2, part], bu[:, (i - 1) % 2, part], 0.0, ALU.mult, ALU.add)
                        if b == 0:
                            last.then_inc(dve_chain, 1)
                            chain[0] += 1
                    last.then_inc(scan_done, 1)
                elif k == "MC":
                    _, n, c = st
                    i = count[st]
                    full(dve, st)
                    dve.wait_ge(scan_done, i)
                    dve.wait_ge(dve_chain, chain[0])
                    if i > 2:
                        dve.wait_ge(yacc_done, i - 2)
                    V_.scalar_tensor_tensor(out=gc[:, (i - 1) % 2, :], in0=bk[:, :], scalar=bBC[:, 1, n:n + 1], in1=hs[:, (i - 1) % 2, :],
                                            op0=ALU.add, op1=ALU.mult).then_inc(read[k], 1)
                elif k == "MY":
                    b = st[1]
                    c = slice(b * S, (b + 1) * S)
                    dve.wait_ge(yacc_done, NSTATE * (b // 2 + 1))
                    link(V_.scalar_tensor_tensor(out=yacc[:, c], in0=xT[:, c], scalar=vecs[:, 1:2], in1=yacc[:, c], op0=ALU.mult, op1=ALU.add))
                    V_.tensor_tensor(yacc[:, c], yacc[:, c], xT[:, c], ALU.add).then_inc(state_out, 1)
                elif k == "STAT":
                    _, s, b = st
                    kind, a = SUBLAYERS[s]
                    r, x = res[:, b % 2], x_tok[:, TPB * b:TPB * (b + 1), :]
                    if kind == "mamba":
                        src = ("MY", b)
                    elif kind == "linear":
                        src = ("LY", b)
                    elif kind == "attn" and a != SELF_WIDE:
                        src = ("Y", a, b)
                    else:
                        src = None
                    if src:
                        full(dve, src)
                        y = psum(src)[:, 0:S].rearrange("p (t d) -> p t d", t=TPB)
                        if kind == "mamba":
                            V_.tensor_copy(r, y).then_inc(read[src[0]], 1)
                        else:
                            V_.tensor_tensor(r, y, x, ALU.add).then_inc(read[src[0]], 1)
                        finished(dve, src)
                        if kind == "attn" and a not in (3, GATHERED):
                            link(V_.tensor_tensor(r, r, bvo[:, a, 1:2, :].to_broadcast([128, TPB, D]), ALU.add))
                    else:
                        y = acc[:, (b % 2) * TPB:(b % 2 + 1) * TPB, :] if kind == "moe" else wide_sum(b)
                        link(V_.tensor_tensor(r, y, x, ALU.add))
                    statistics(r, b, (kind, a) in (("attn", 1), ("moe", 0)))
                elif k == "STAT2":
                    _, s, b = st
                    dve.wait_ge(rstd_done, stat_no[("STAT", s, b)])
                    for t in range(TPB):
                        link(V_.scalar_tensor_tensor(out=res[:, b % 2, t, :], in0=res[:, b % 2, t, :], scalar=rstd[:, b % 2, t:t + 1], in1=norm_w[:, 1, :],
                                                     op0=ALU.mult, op1=ALU.mult))
                    link(V_.tensor_tensor(res[:, b % 2], res[:, b % 2], x_before[:, TPB * b:TPB * (b + 1), :], ALU.add))
                    statistics(res[:, b % 2], b, False)
                elif k == "NORM":
                    _, s, b = st
                    dve.wait_ge(rstd_done, stat_no[("STAT2" if SUBLAYERS[s] == ("moe", 0) else "STAT", s, b)])
                    if SUBLAYERS[s] == ("attn", 1):
                        link(V_.tensor_copy(x_before[:, TPB * b:TPB * (b + 1), :], x_tok[:, TPB * b:TPB * (b + 1), :]))
                    for t in range(TPB):
                        x, r = x_tok[:, TPB * b + t, :], res[:, b % 2, t, :]
                        if SUBLAYERS[s] == ("attn", 1):
                            last = V_.scalar_tensor_tensor(out=x, in0=r, scalar=rstd[:, b % 2, t:t + 1], in1=norm_w[:, 0, :], op0=ALU.mult, op1=ALU.mult)
                        else:
                            last = V_.tensor_scalar(x, r, mv[:, b % 2, t, 0:1], rstd[:, b % 2, t:t + 1], ALU.subtract, ALU.mult)
                        if t < TPB - 1:
                            last.then_inc(dve_chain, 1)
                            chain[0] += 1
                    last.then_inc(norm_done, 1)
                    dve.wait_ge(norm_done, count[st])
                    dve.wait_ge(dve_chain, chain[0])
                elif k == "V":
                    _, a, b = st
                    n = unit[(a, b)]
                    full(dve, st)
                    if n >= 2 and units[n - 2][1] != SELF_WIDE:
                        full(dve, ("PV", units[n - 2][1], units[n - 2][2], NH - 1))
                    for t in range(TPB):
                        last = V_.tensor_tensor(V[:, n % 2, t, :, 0:DH], bk[:, t * 128:(t + 1) * 128].rearrange("p (h d) -> p h d", d=DH),
                                                bvo[:, a, 0, :].rearrange("p (h d) -> p h d", d=DH), ALU.add)
                    last.then_inc(read[k], 1)
                elif k == "SM":
                    _, a, b, u = st
                    full(dve, st)
                    to = mx[:, unit[(a, b)] % 2, u % 2, 2 * (u // 2):2 * (u // 2) + 2]
                    if a == MASKED:
                        for j in range(2):
                            last = V_.tensor_tensor_reduce(out=unused[:, j, :], in0=bk[:, j * S:(j + 1) * S], in1=biasf[:, b % 2, 0, (u % 2) * S:(u % 2 + 1) * S],
                                                           scale=1.0, scalar=-3e38, op0=ALU.add, op1=ALU.max, accum_out=to[:, j:j + 1])
                            if j == 0:
                                last.then_inc(dve_chain, 1)
                                chain[0] += 1
                        last.then_inc(read[k], 1)
                        finished(dve, st)
                        dve.wait_ge(dve_chain, chain[0])
                    else:
                        nk = (u % 2 + 1) * 128 if a == CAUSAL else S
                        V_.reduce_max(to, bk[:, :].rearrange("p (h s) -> p h s", h=2)[:, :, 0:nk], AX.X).then_inc(read[k], 1)
                elif k == "P2" and st[1] == MASKED:
                    full(dve, st)
                    V_.tensor_tensor(bk[:, :], bk[:, :], biasf[:, st[2] % 2, 1, :], ALU.add).then_inc(biased, 1)
                elif k == "MS":
                    _, a, b = st
                    n = unit[(a, b)]
                    finished(dve, ("SM", a, b, 15))
                    if n >= 2:
                        full(dve, ("MT", units[n - 2][1], units[n - 2][2]))
                    hi, low = ms[:, n % 2, :, 0:NH], ms[:, n % 2, :, NH:2 * NH]
                    link(V_.tensor_scalar(hi, mx[:, n % 2], -1.0, None, ALU.mult))
                    V_.scalar_tensor_tensor(out=low, in0=mx[:, n % 2], scalar=-1.0, in1=hi, op0=ALU.mult, op1=ALU.subtract).then_inc(shift_done, 1)
                elif k == "ZV":
                    _, b, h = st
                    full(dve, st)
                    y = bk[:, :].rearrange("p (t s) -> p t s", t=TPB)
                    link(V_.reciprocal(rden[:, :, 0:1], y[:, :, D:D + 1]))
                    for t in range(TPB):
                        to = wide_sum(b)[:, t, :]
                        if h == 0:
                            last = V_.tensor_scalar(to, y[:, t, 0:D], rden[:, t, 0:1], None, ALU.mult)
                        else:
                            last = V_.scalar_tensor_tensor(out=to, in0=y[:, t, 0:D], scalar=rden[:, t, 0:1], in1=to, op0=ALU.mult, op1=ALU.add)
                        if t < TPB - 1:
                            last.then_inc(dve_chain, 1)
                            chain[0] += 1
                    last.then_inc(read[k], 1)
                    dve.wait_ge(dve_chain, chain[0])
                    dve.wait_ge(read[k], count[st])
                elif k == "OT":
                    _, a, b, t = st
                    full(dve, st)
                    y = bk[:, :].rearrange("p (h c) -> p h c", c=32)
                    link(V_.reciprocal(rden[:, t, :].unsqueeze(2), y[:, :, DH:DH + 1]))
                    i = count[("OX", a, b)]
                    if i > 1:
                        dve.wait_ge(filled["OX"], i - 1)
                    V_.tensor_tensor(o[:, t, :].rearrange("p (h d) -> p h d", d=DH), y[:, :, 0:DH],
                                     rden[:, t, :].unsqueeze(2).to_broadcast([128, NH, DH]), ALU.mult).then_inc(read[k], 1)
                elif k == "GS":
                    _, b, t = st
                    full(dve, st)
                    if t == 0 and b:
                        full(dve, ("GT", b - 1))
                    link(V_.max(top[:, 0, :], bk[:, 0:S]))
                    link(V_.max_index(top_at[:, 0, :], top[:, 0, :], bk[:, 0:S]))
                    link(V_.tensor_copy(top_atf[:, 0, :], top_at[:, 0, :]))
                    V_.tensor_scalar(one_hot[:, t, :], iota[:, :], top_atf[:, 0, 0:1], None, ALU.is_equal).then_inc(read[k], 1)
                elif k == "BIAS":
                    b = st[1]
                    if b == 0:
                        dve.wait_ge(mask_in, 48)
                    if b >= 2:
                        dve.wait_ge(mask_more[b - 2], 16)
                    if b >= 2:
                        dve.wait_ge(biased, NH * (b - 1))
                    to = biasf[:, b % 2]
                    link(V_.tensor_scalar(to, mask[:, b % 2], 0.0, NEG, ALU.is_equal, ALU.mult))
                    V_.scalar_tensor_tensor(out=to, in0=adj, scalar=1.0 / SCALE, in1=to, op0=ALU.mult, op1=ALU.add).then_inc(bias_sum, 1)
                    dve.wait_ge(bias_sum, b + 1)
                elif k == "GATE":
                    _, m, b = st
                    full(dve, st)
                    lg = bk[:, 0:TPB * NE].rearrange("p (t e) -> p t e", e=NE)
                    V_.tensor_tensor(logits[:, :, :], lg, gate_b[:, m:m + 1, :].to_broadcast([128, TPB, NE]), ALU.add).then_inc(read[k], 1)
                    finished(dve, st)
                    for t in range(TPB):
                        link(V_.max(top[:, t, :], logits[:, t, :]))
                    for t in range(TPB):
                        link(V_.max_index(top_at[:, t, :], top[:, t, :], logits[:, t, :]))
                    link(V_.tensor_copy(top_atf[:, :, :], top_at[:, :, :]))
                    if m == 0:
                        V_.tensor_copy(gw[:, :, :], top[:, :, :]).then_inc(top_done, 1)
                    else:
                        V_.tensor_tensor(gw[:, :, :], top[:, :, :], top[:, :, 0:1].to_broadcast([128, TPB, 8]), ALU.subtract).then_inc(top_done, 1)
                    dve.wait_ge(gate_exp, count[st])
                    if m == 0:
                        link(V_.tensor_scalar(gs[:, :, :], gs[:, :, :], 1.0, None, ALU.add))
                        link(V_.reciprocal(gs[:, :, :], gs[:, :, :]))
                    link(V_.tensor_tensor(gden[:, :, :], gs[:, :, 0:1], gs[:, :, 1:2], ALU.add))
                    if m == 0:
                        link(V_.tensor_scalar(gden[:, :, :], gden[:, :, :], 1e-6, None, ALU.add))
                    if m == 1:
                        link(V_.reduce_sum(gz[:, :, :], gs[:, :, :], AX.X))
                        link(V_.scalar_tensor_tensor(out=gden[:, :, :], in0=gz[:, :, :], scalar=1e-9, in1=gden[:, :, :], op0=ALU.mult, op1=ALU.add))
                    link(V_.reciprocal(gden[:, :, :], gden[:, :, :]))
                    link(V_.tensor_tensor(gs[:, :, :], gs[:, :, :], gden[:, :, :].to_broadcast([128, TPB, 8]), ALU.mult))
                    for t in range(TPB):
                        g = gates[:, TPB * b + t, :]
                        link(V_.tensor_scalar(g, iota[:, 0:NE], top_atf[:, t, 0:1], gs[:, t, 0:1], ALU.is_equal, ALU.mult))
                        link(V_.tensor_scalar(gtmp[:, :], iota[:, 0:NE], top_atf[:, t, 1:2], gs[:, t, 1:2], ALU.is_equal, ALU.mult))
                        link(V_.tensor_tensor(g, g, gtmp[:, :], ALU.add))
                        if m == 0:
                            ch = chosen[:, TPB * b + t, :]
                            link(V_.tensor_scalar(ch, iota[:, 0:NE], top_atf[:, t, 0:1], None, ALU.is_equal))
                            link(V_.scalar_tensor_tensor(out=ch, in0=iota[:, 0:NE], scalar=top_atf[:, t, 1:2], in1=ch, op0=ALU.is_equal, op1=ALU.add))
                    V_.tensor_copy(gtmp[:, :], gtmp[:, :]).then_inc(gates_done, 1)
                    dve.wait_ge(gates_done, count[st])
                elif k == "RANK":
                    full(dve, st)
                    sums = bk[:, NTT * NE:2 * NTT * NE].rearrange("p (t e) -> p t e", e=NE)
                    link(V_.memset(prefix[:, 0, :], 0.0))
                    for t in range(1, NTT):
                        link(V_.tensor_tensor(prefix[:, t, :], sums[:, t - 1, :], prefix[:, t - 1, :], ALU.add))
                    V_.tensor_tensor(prefix[:, :, :], bk[:, 0:NTT * NE].rearrange("p (t e) -> p t e", e=NE), prefix[:, :, :], ALU.add).then_inc(read[k], 1)
                    finished(dve, st)
                    link(V_.scalar_tensor_tensor(out=gates[:, :, :], in0=prefix[:, :, :], scalar=float(CAPACITY), in1=gates[:, :, :], op0=ALU.is_lt, op1=ALU.mult))
                elif k == "BI":
                    full(dve, st)
                    V_.tensor_copy(acc[:, :, :], bk[:, :].rearrange("p (t d) -> p t d", d=D)).then_inc(read[k], 1)
                    finished(dve, st)
                elif k == "MG":
                    _, m, c, e, f = st
                    full(dve, st)
                    finished(dve, ("MH", m, c, e, f))
                    if f == 0 and count[("MO", m, c, e)] > 2:
                        dve.wait_ge(filled["MO"], count[("MO", m, c, e)] - 2)
                    V_.tensor_tensor(hT[:, e % 2, f, :], bk[:, :], gated[:, (count[st] - 1) % 2, :], ALU.mult).then_inc(read[k], 1)
                elif k == "MO":
                    _, m, c, e = st
                    full(dve, st)
                    for t in range(4):
                        g = gates[:, 4 * c + t, e:e + 1]
                        y = bk[:, t * 128:(t + 1) * 128]
                        if e == 0 and m in (0, 2):
                            last = V_.tensor_scalar(acc[:, t, :], y, g, None, ALU.mult)
                        else:
                            last = V_.scalar_tensor_tensor(out=acc[:, t, :], in0=y, scalar=g, in1=acc[:, t, :], op0=ALU.mult, op1=ALU.add)
                        if t < 3:
                            last.then_inc(dve_chain, 1)
                            chain[0] += 1
                    last.then_inc(read[k], 1)
                    finished(dve, st)
                    dve.wait_ge(dve_chain, chain[0])
                elif k == "LF":
                    i = count[st]
                    full(dve, st)
                    f = bk[:, :].rearrange("p (h f) -> p h f", f=FD)
                    link(V_.reduce_max(lmax_v[:, 0, :], f, AX.X))
                    link(V_.tensor_reduce(lmax_v[:, 1, :], f, AX.X, ALU.min))
                    if i > 2:
                        dve.wait_ge(lexp_done, i - 2)
                    link(V_.tensor_tensor(lf[:, (i - 1) % 2, :, 0, :], f, lmax_v[:, 0, :].unsqueeze(2).to_broadcast([128, 8, FD]), ALU.subtract))
                    V_.scalar_tensor_tensor(out=lf[:, (i - 1) % 2, :, 1, :], in0=f, scalar=-1.0, in1=lmax_v[:, 1, :].unsqueeze(2).to_broadcast([128, 8, FD]),
                                            op0=ALU.mult, op1=ALU.add).then_inc(read[k], 1)
                elif k == "LS":
                    i = count[st]
                    dve.wait_ge(lexp_done, i)
                    if i > 2:
                        dve.wait_ge(lfeat_done, i - 2)
                    link(V_.reduce_sum(lden[:, (i - 1) % 2], le[:, (i - 1) % 3].rearrange("p h a f -> p (h a) f"), AX.X))
                    V_.reciprocal(lden[:, (i - 1) % 2], lden[:, (i - 1) % 2]).then_inc(lsum_done, 1)
                elif k == "LK":
                    i = count[st]
                    dve.wait_ge(lfeat_done, i)
                    x = le[:, (i - 1) % 3].rearrange("p h a f -> p (h a f)")
                    V_.tensor_scalar(x, x, 1e-12, None, ALU.max).then_inc(clipped, 1)
                elif k == "LA":
                    _, b, h = st
                    i = count[st]
                    full(dve, st)
                    if i > 4:
                        dve.wait_ge(filled["LO"], (i - 5) // 2 + 1)
                    V_.tensor_tensor(P[:, (i - 1) % NBUF_P, 0:S + 128], bk[:, 0:S + 128], keep_past[:, :], ALU.mult).then_inc(read[k], 1)
                elif k == "LO":
                    _, b, g = st
                    full(dve, st)
                    if g == 0 and b:
                        full(dve, ("LX", b - 1, TPB - 1, 1))
                    y = bk[:, 0:4 * 66].rearrange("p (h c) -> p h c", c=66)
                    link(V_.tensor_scalar(rden[:, 0, 0:4].unsqueeze(2), y[:, :, HD:HD + 1], 1e-12, None, ALU.add))
                    link(V_.reciprocal(rden[:, 0, 0:4], rden[:, 0, 0:4]))
                    for t in range(TPB):
                        last = V_.tensor_tensor(lo[:, t, 2 * g * HD:2 * (g + 1) * HD].rearrange("p (h d) -> p h d", d=HD), y[:, 2 * t:2 * t + 2, 0:HD],
                                                rden[:, 0, 2 * t:2 * t + 2].unsqueeze(2).to_broadcast([128, 2, HD]), ALU.mult)
                        if t == 0:
                            last.then_inc(dve_chain, 1)
                            chain[0] += 1
                    last.then_inc(read[k], 1)
                    dve.wait_ge(dve_chain, chain[0])
                    finished(dve, st)


def kernel(**inputs):
    import numpy as np
    import concourse.bacc as bacc
    from concourse.bass_utils import run_bass_kernel_spmd as run

    w = {k: np.asarray(v) for k, v in inputs.items()}
    f32 = np.float32
    zero = np.zeros((D,), f32)
    eye = np.eye(D, dtype=f32)

    def tokens(a):
        return a.reshape(NTT, 128, D).transpose(1, 0, 2)

    def all_heads(a, n):
        return np.repeat(a.reshape(a.shape[:-1] + (n, DH)), NH // n, axis=-2).reshape(a.shape[:-1] + (D,))

    g = "L0_ffn_"
    wkv = w["L3_xattn_Wkv"]
    qkv = w["L2_attn_w_qkv"]
    attn = [
        [w["L0_xattn_W" + c].T for c in "qkvo"],
        [w[g + "qw"], all_heads(w[g + "kw"], 4), all_heads(w[g + "vw"], 4), w[g + "ow"]],
        [eye, eye, w["L3_xattn_Wq"].T, eye],
        [w["L1_xattn_w_" + c].T for c in "qkvo"],
        [qkv[:, 0:D], qkv[:, D:2 * D], qkv[:, 2 * D:3 * D], w["L2_attn_w_out"]],
        [w["L2_xattn_W" + c].T for c in "qkvo"],
        [w["L3_xattn_Wq"].T, all_heads(wkv[0:DH].T, 1), all_heads(wkv[DH:2 * DH].T, 1), w["L3_xattn_Wc"].T],
    ]
    bq = w["L2_attn_b_qkv"]
    bias = [
        [w["L0_xattn_b" + c] for c in "qkvo"],
        [w[g + "qb"], all_heads(w[g + "kb"], 4), all_heads(w[g + "vb"], 4), w[g + "ob"]],
        [zero] * 4,
        [zero] * 4,
        [bq[0:D], bq[D:2 * D], bq[2 * D:3 * D], w["L2_attn_b_out"]],
        [w["L2_xattn_b" + c] for c in "qkvo"],
        [zero] * 4,
    ]
    bias = np.stack([np.stack(x) for x in bias])

    def by_dim(a):
        return np.swapaxes(a.reshape(a.shape[:-1] + (NH, DH)), -1, -2).reshape(a.shape)

    attn = [[by_dim(x[0]), by_dim(x[1]), x[2], x[3]] for x in attn]
    mask = w["mask_Bx1xSxS2_ik1"][:, 0]
    adj = w["L2_xattn_adj"]

    def both_ways(a):
        pair = np.stack([a, np.swapaxes(a, -1, -2)], axis=-3)
        pair = pair.reshape(pair.shape[:-2] + (TPB, 128, S))
        return np.moveaxis(pair, -2, 0).reshape((128,) + pair.shape[:-3] + (TPB * S,))

    lin = "L3_attn_"
    lin_w = np.stack([w[lin + c].T.reshape(NH, HD, D).transpose(1, 0, 2) for c in ("Wq", "Wk")], axis=1)
    lin_k = np.stack([w[lin + c].transpose(1, 0, 2) for c in ("Kq", "Kk")], axis=1)
    wide = w["L1_attn_weight"].reshape(NH, D, D).transpose(1, 0, 2).reshape(D, NH * D)

    def up(a):
        return a.transpose(1, 0, 2)

    def down(a):
        return a.reshape(NE, -1, 128, D).transpose(2, 0, 1, 3)

    def rows(a):
        return np.broadcast_to(a[None], (128,) + a.shape)

    zero8 = np.zeros((NE,), f32)
    arrays = {
        "xT": w["x"].reshape(NT, D).T, "x": tokens(w["x"]),
        "ctxT": w["ctx_1024"].reshape(NT, D).T, "ctx": tokens(w["ctx_1024"]),
        "w_xdt": w["L0_attn_W_xdt"].T, "w_dt": w["L0_attn_W_dt"].T,
        "w_BC": np.stack([w["L0_attn_W_B"].T, w["L0_attn_W_C"].T], axis=1),
        "A_log": w["L0_attn_A_log"], "b_BC": rows(np.stack([w["L0_attn_b_B"], w["L0_attn_b_C"]])),
        "dt_D": np.stack([w["L0_attn_b_dt"], w["L0_attn_D"]], axis=1), "b_xdt": w["L0_attn_b_xdt"][:, None],
        "w_attn": np.stack([np.stack(x) for x in attn]).transpose(2, 0, 1, 3),
        "b_qk": by_dim(bias[:, 0:2]).transpose(2, 0, 1), "b_vo": rows(bias[:, 2:4]),
        "gate_w": np.stack([w[g + "gate_w"], w["L1_ffn_Wg"], w["L2_ffn_gate_w"].T, w["L3_ffn_Wr"]], axis=1),
        "gate_b": rows(np.stack([zero8, w["L1_ffn_bg"], zero8, w["L3_ffn_br"]])),
        "b1": np.stack([w["L1_ffn_b1"], w["L3_ffn_b1"]]).reshape(2, NE, 2, 128).transpose(3, 0, 1, 2),
        "b2": np.stack([w["L1_ffn_b2"], w["L3_ffn_b2"]], axis=1),
        "norm_w": rows(np.stack([w[g + "norm1_w"], w[g + "norm2_w"]])),
        "wide_w": wide,
        "w1_0": up(w[g + "w1"]), "w2_0": down(w[g + "w2"]),
        "w1_1": up(w["L1_ffn_W1"]), "w2_1": down(w["L1_ffn_W2"]),
        "w1_2": w["L2_ffn_w1"].transpose(2, 0, 1), "w3_2": w["L2_ffn_w3"].transpose(2, 0, 1),
        "w2_2": down(w["L2_ffn_w2"].transpose(0, 2, 1)),
        "w1_3": up(w["L3_ffn_W1"]), "w2_3": down(w["L3_ffn_W2"]),
        **{f"mask{b}": both_ways(mask[b]) for b in range(B)}, "adj": both_ways(adj),
        "lin_v": w[lin + "Wv"], "lin_o": w[lin + "Wo"].reshape(8, 128, D).transpose(1, 0, 2).reshape(128, 8 * D),
        "lin_w0": lin_w[:, :, 0:8], "lin_w1": lin_w[:, :, 8:16], "lin_k0": lin_k[:, :, 0:8], "lin_k1": lin_k[:, :, 8:16],
    }
    arrays = {k: np.ascontiguousarray(v) for k, v in arrays.items()}
    nc = bacc.Bacc("TRN2", target_bir_lowering=False, num_devices=1)
    ins = {k: nc.dram_tensor(f"in_{k}", a.shape, mybir.dt.from_np(a.dtype), kind="ExternalInput").ap() for k, a in arrays.items()}
    scratch = nc.dram_tensor("split_parts", (2, 2, 3, 128, S), mybir.dt.bfloat16, kind="Internal").ap()
    out = nc.dram_tensor("out", (B, S, D), mybir.dt.float32, kind="ExternalOutput").ap()
    decoder(nc, ins, scratch, out)
    r = run(nc, [{f"in_{k}": a for k, a in arrays.items()}], core_ids=[0])
    return r.results[0]["out"]
```
